# Optimizing a Trainium2 kernel written in Bass

```python
import numpy as np
import jax
import jax.numpy as jnp

def _softmax(x, axis=-1):
    return jax.nn.softmax(x, axis=axis)

def _gelu(x):
    return jax.nn.gelu(x, approximate=True)

def _silu(x):
    return jax.nn.silu(x)

def _sigmoid(x):
    return jax.nn.sigmoid(x)

def _layernorm(x, axis=-1, eps=1e-05):
    m = jnp.mean(x, axis=axis, keepdims=True)
    v = jnp.var(x, axis=axis, keepdims=True)
    return (x - m) / jnp.sqrt(v + eps)

def _scatter_add(tgt, idx, src, axis=0):
    return tgt.at[idx].add(src)

def _segment_sum(src, seg, n):
    return jax.ops.segment_sum(src, seg, n)
kernel_name = 'mk_gnn_resnorm_d4_gnn_r8_1d0580'

def setup_inputs(seed: int=0):
    np.random.seed(seed)
    _w = jnp.asarray

    def _rec_inputs():
        import jax
        import jax.numpy as jnp
        _gk = jax.random.key(seed)
        x = -0.0005121 + 1.001 * jax.random.normal(jax.random.fold_in(_gk, 1), (6250, 64), jnp.float32)
        _s = jax.random.randint(jax.random.fold_in(_gk, 2), (100000,), 0, 6250, jnp.int32)
        _d = jax.random.randint(jax.random.fold_in(_gk, 3), (100000,), 0, 6250, jnp.int32)
        _loop = jnp.arange(6250, dtype=jnp.int32)
        src = jnp.concatenate([_s, _d, _loop])
        dst = jnp.concatenate([_d, _s, _loop])
        _o = jnp.argsort(dst, stable=True)
        src = src[_o]
        dst = dst[_o]
        edge_attr_16 = 0.000254156 + 0.999948 * jax.random.normal(jax.random.fold_in(_gk, 12), (206250, 16), jnp.float32)
        edge_attr_32 = -5.3897e-05 + 0.999841 * jax.random.normal(jax.random.fold_in(_gk, 13), (206250, 32), jnp.float32)
        return (x, src, dst, edge_attr_16, edge_attr_32)
    x, src, dst, edge_attr_16, edge_attr_32 = _rec_inputs()

    def _L0_gnn_setup():
        import jax, jax.numpy as jnp
        import numpy as np
        N_NODES = 6250
        N_EDGES = 100000
        D_NODE = 64
        D_EDGE = 32
        D_OUT = 64
        key = jax.random.key(seed)
        k1, k2, k3, k4, k5, k6, k7, k8 = jax.random.split(key, 8)
        d_in = 2 * D_NODE + D_EDGE
        return {'node_feats': jax.random.normal(k1, (N_NODES, D_NODE), dtype=jnp.float32), 'edge_feats': jax.random.normal(k2, (N_EDGES, D_EDGE), dtype=jnp.float32), 'src': jax.random.randint(k3, (N_EDGES,), 0, N_NODES, dtype=jnp.int64), 'dst': jax.random.randint(k4, (N_EDGES,), 0, N_NODES, dtype=jnp.int64), 'W1': jax.random.normal(k5, (d_in, D_OUT), dtype=jnp.float32) / np.sqrt(d_in), 'b1': jnp.zeros((D_OUT,), dtype=jnp.float32), 'W2': jax.random.normal(k6, (D_OUT, D_OUT), dtype=jnp.float32) / np.sqrt(D_OUT), 'b2': jnp.zeros((D_OUT,), dtype=jnp.float32)}
    _L0_gnn_all = _L0_gnn_setup()
    _L0_gnn_in = {k: v for k, v in _L0_gnn_all.items() if k in ('W1', 'b1', 'W2', 'b2')}
    del _L0_gnn_all

    def _L1_gnn_setup():
        import jax, jax.numpy as jnp
        import numpy as np
        N, E = (6250, 100000)
        NODE_DIM, EDGE_DIM, HEADS = (64, 16, 4)
        C = NODE_DIM // HEADS
        NEG_SLOPE = 0.2
        BN_EPS = 1e-05
        key = jax.random.key(seed)
        ks = jax.random.split(key, 12)
        glorot = lambda k, shape: jax.random.normal(k, shape, jnp.float32) * np.sqrt(2.0 / (shape[0] + shape[-1]))
        return {'x': jax.random.normal(ks[0], (N, NODE_DIM), jnp.float32), 'edge_index': jax.random.randint(ks[1], (2, E), 0, N, jnp.int32), 'edge_attr': jax.random.normal(ks[2], (E, EDGE_DIM), jnp.float32), 'W_l': glorot(ks[3], (NODE_DIM, HEADS * C)), 'b_l': jnp.zeros((HEADS * C,), jnp.float32), 'W_r': glorot(ks[4], (NODE_DIM, HEADS * C)), 'b_r': jnp.zeros((HEADS * C,), jnp.float32), 'W_e': glorot(ks[5], (EDGE_DIM, HEADS * C)), 'att': glorot(ks[6], (HEADS, C)), 'bias': jnp.zeros((HEADS * C,), jnp.float32), 'gamma': jnp.ones((NODE_DIM,), jnp.float32), 'beta': jnp.zeros((NODE_DIM,), jnp.float32)}
    _L1_gnn_all = _L1_gnn_setup()
    _L1_gnn_in = {k: v for k, v in _L1_gnn_all.items() if k in ('W_l', 'b_l', 'W_r', 'b_r', 'W_e', 'att', 'bias', 'gamma', 'beta')}
    del _L1_gnn_all

    def _L2_gnn_setup():
        import jax, jax.numpy as jnp
        import numpy as np
        ALPHA = 0.2
        key = jax.random.key(seed)
        k1, k2, k3, k4 = jax.random.split(key, 4)
        N, E, d_in, d_out = (12500, 200000, 64, 64)
        node_features = jax.random.normal(k1, (N, d_in), dtype=jnp.float32)
        edge_index = jax.random.randint(k2, (2, E), 0, N, dtype=jnp.int64)
        W = jax.random.normal(k3, (d_in, d_out), dtype=jnp.float32) * (1.414 * np.sqrt(2.0 / (d_in + d_out)))
        a = jax.random.normal(k4, (2 * d_out,), dtype=jnp.float32) * (1.414 * np.sqrt(2.0 / (2 * d_out + 1)))
        return {'node_features': node_features, 'edge_index': edge_index, 'W': W, 'a': a}
    _L2_gnn_all = _L2_gnn_setup()
    _L2_gnn_in = {k: v for k, v in _L2_gnn_all.items() if k in ('W', 'a')}
    del _L2_gnn_all

    def _L3_gnn_setup():
        import jax, jax.numpy as jnp
        import numpy as np
        N_NODES = 6250
        N_EDGES = 100000
        D_FEAT = 64
        key = jax.random.key(seed)
        k1, k2, k3 = jax.random.split(key, 3)
        xs = jax.random.normal(k1, (N_NODES, D_FEAT), dtype=jnp.float32)
        src = jax.random.randint(k2, (N_EDGES,), 0, N_NODES, dtype=jnp.int32)
        dst = jax.random.randint(k3, (N_EDGES,), 0, N_NODES, dtype=jnp.int32)
        return {'xs': xs, 'src': src, 'dst': dst}
    _L3_gnn_all = _L3_gnn_setup()
    _L3_gnn_in = {k: v for k, v in _L3_gnn_all.items() if k in ()}
    del _L3_gnn_all
    return {'x': x, 'src': src, 'dst': dst, 'edge_attr_16': edge_attr_16, 'edge_attr_32': edge_attr_32, 'L0_gnn_W1': _L0_gnn_in['W1'], 'L0_gnn_b1': _L0_gnn_in['b1'], 'L0_gnn_W2': _L0_gnn_in['W2'], 'L0_gnn_b2': _L0_gnn_in['b2'], 'L1_gnn_W_l': _L1_gnn_in['W_l'], 'L1_gnn_b_l': _L1_gnn_in['b_l'], 'L1_gnn_W_r': _L1_gnn_in['W_r'], 'L1_gnn_b_r': _L1_gnn_in['b_r'], 'L1_gnn_W_e': _L1_gnn_in['W_e'], 'L1_gnn_att': _L1_gnn_in['att'], 'L1_gnn_bias': _L1_gnn_in['bias'], 'L1_gnn_gamma': _L1_gnn_in['gamma'], 'L1_gnn_beta': _L1_gnn_in['beta'], 'L2_gnn_W': _L2_gnn_in['W'], 'L2_gnn_a': _L2_gnn_in['a']}

def reference(x, src, dst, edge_attr_16, edge_attr_32, L0_gnn_W1, L0_gnn_b1, L0_gnn_W2, L0_gnn_b2, L1_gnn_W_l, L1_gnn_b_l, L1_gnn_W_r, L1_gnn_b_r, L1_gnn_W_e, L1_gnn_att, L1_gnn_bias, L1_gnn_gamma, L1_gnn_beta, L2_gnn_W, L2_gnn_a):
    import jax
    import jax.numpy as jnp

    def _L0_gnn_ref(node_feats, edge_feats, src, dst, W1, b1, W2, b2):
        import jax, jax.numpy as jnp
        import numpy as np
        N_NODES = 6250
        N_EDGES = 100000
        D_NODE = 64
        D_EDGE = 32
        D_OUT = 64
        x = jnp.concatenate([node_feats[src], node_feats[dst], edge_feats], axis=1)
        m = jnp.maximum(x @ W1 + b1, 0.0) @ W2 + b2
        return jax.ops.segment_sum(m, dst, num_segments=N_NODES)

    def _L1_gnn_ref(x, edge_index, edge_attr, W_l, b_l, W_r, b_r, W_e, att, bias, gamma, beta):
        import jax, jax.numpy as jnp
        import numpy as np
        N, E = (6250, 100000)
        NODE_DIM, EDGE_DIM, HEADS = (64, 16, 4)
        C = NODE_DIM // HEADS
        NEG_SLOPE = 0.2
        BN_EPS = 1e-05
        src, dst = (edge_index[0], edge_index[1])
        n = x.shape[0]
        xl = (x @ W_l + b_l).reshape(n, HEADS, C)
        xr = (x @ W_r + b_r).reshape(n, HEADS, C)
        e = (edge_attr @ W_e).reshape(-1, HEADS, C)
        g = jax.nn.leaky_relu(xl[src] + xr[dst] + e, NEG_SLOPE)
        logits = jnp.einsum('ehc,hc->eh', g, att)
        amax = jax.ops.segment_max(logits, dst, num_segments=n)
        ex = jnp.exp(logits - amax[dst])
        denom = jax.ops.segment_sum(ex, dst, num_segments=n)
        alpha = ex / (denom[dst] + 1e-16)
        msg = xl[src] * alpha[..., None]
        out = jax.ops.segment_sum(msg, dst, num_segments=n).reshape(n, HEADS * C) + bias
        mean = out.mean(axis=0)
        var = out.var(axis=0)
        out = (out - mean) * jax.lax.rsqrt(var + BN_EPS) * gamma + beta
        return jax.nn.gelu(out + x, approximate=False)

    def _L2_gnn_ref(node_features, edge_index, W, a):
        import jax, jax.numpy as jnp
        import numpy as np
        ALPHA = 0.2
        N = node_features.shape[0]
        d_out = W.shape[1]
        src, tgt = (edge_index[0], edge_index[1])
        h = node_features @ W
        s_src = h @ a[:d_out]
        s_tgt = h @ a[d_out:]
        e = jax.nn.leaky_relu(s_src[src] + s_tgt[tgt], negative_slope=ALPHA)
        m = jax.ops.segment_max(e, tgt, num_segments=N)
        e_exp = jnp.exp(e - m[tgt])
        denom = jax.ops.segment_sum(e_exp, tgt, num_segments=N)
        attention = e_exp / denom[tgt]
        h_prime = jax.ops.segment_sum(h[src] * attention[:, None], tgt, num_segments=N)
        return jax.nn.elu(h_prime)

    def _L3_gnn_ref(xs, src, dst):
        import jax, jax.numpy as jnp
        import numpy as np
        N_NODES = 6250
        N_EDGES = 100000
        D_FEAT = 64
        gathered = xs[src]
        sums = jax.ops.segment_sum(gathered, dst, num_segments=N_NODES)
        counts = jax.ops.segment_sum(jnp.ones((src.shape[0],), dtype=xs.dtype), dst, num_segments=N_NODES)
        return sums / jnp.maximum(counts, 1.0)[:, None]
    edge_index = jnp.stack([src, dst])
    x = _layernorm(x + _L0_gnn_ref(x, edge_attr_32, src, dst, L0_gnn_W1, L0_gnn_b1, L0_gnn_W2, L0_gnn_b2), axis=-1)
    x = _layernorm(x + _L1_gnn_ref(x, edge_index, edge_attr_16, L1_gnn_W_l, L1_gnn_b_l, L1_gnn_W_r, L1_gnn_b_r, L1_gnn_W_e, L1_gnn_att, L1_gnn_bias, L1_gnn_gamma, L1_gnn_beta), axis=-1)
    x = _layernorm(x + _L2_gnn_ref(x, edge_index, L2_gnn_W, L2_gnn_a), axis=-1)
    x = _layernorm(x + _L3_gnn_ref(x, src, dst), axis=-1)
    return x

_drawn_inputs = setup_inputs


def setup_inputs(seed=0):
    import zlib

    import numpy as np

    out = dict(_drawn_inputs(seed))
    spreads = {'L0_gnn_b1': (0.0, 0.1),
     'L0_gnn_b2': (0.0, 0.1),
     'L1_gnn_b_l': (0.0, 0.8),
     'L1_gnn_b_r': (0.0, 0.8),
     'L1_gnn_bias': (0.0, 0.8),
     'L1_gnn_gamma': (1.0, 0.2),
     'L1_gnn_beta': (0.0, 0.1)}
    factors = {}
    for name, (base, spread) in spreads.items():
        noise = np.random.default_rng([zlib.crc32(name.encode()), seed]).standard_normal(out[name].shape)
        drawn = base * np.exp(spread * noise) if base else spread * noise
        out[name] = jnp.asarray(drawn.astype(out[name].dtype))
    for name, factor in factors.items():
        out[name] = (out[name] * factor).astype(out[name].dtype)
    return out
```

```python
import numpy as np
import concourse.bass as bass
from concourse import mybir
from contextlib import ExitStack

F32 = mybir.dt.float32
BF16 = mybir.dt.bfloat16
I32 = mybir.dt.int32
ALU = mybir.AluOpType
ACT = mybir.ActivationFunctionType
AX = mybir.AxisListType.X

P = 128
N = 6250
E = 206250
D = 64
HEADS = 4
B = 7
Q = 3
NB = -(-E // (P * B * Q)) * Q
NT = NB * B
RB = -(-NT // P)
NTP = RB * P
EFULL, EREST = E // P, E % P
KN = -(-N // P)
KP = KN + 1
NP = KP * P
NREST = N - (KN - 1) * P
HI = -(-(N + 1) // P)
BIG = 3.0e38
LN_EPS = 1e-5
BN_EPS = 1e-5
SLOPE = 0.2
LAST_C = -(-NB // P)
SP_TILES = 4
SPLIT = 10
SG = 4


class Layer:

    def __init__(self, name, gathered, window, attr, heads, gather_table, window_table):
        self.name, self.gathered, self.window, self.attr, self.heads = name, gathered, window, attr, heads
        self.gather_table, self.window_table = gather_table, window_table
        self.msg = D + heads
        self.row = D + 2 * heads
        self.parts = 3 if window == D else 1
        self.win_dt = BF16 if self.parts == 3 else F32


class Batch:

    def __init__(self, loop, c):
        self.loop, self.c = loop, c
        self.q = c % Q
        self.n = loop * Q + c
        self.turn = loop + c // Q

    def __add__(self, d):
        return Batch(self.loop, self.c + d)

    def exists(self):
        return not isinstance(self.n, int) or 0 <= self.n < NB

    def used(self, back=0):
        return self.n + 1 - back

    def landed(self, dmas=1):
        return (self.turn + 1) * (16 * dmas)

    def landed_before(self, dmas=1):
        return self.turn * (16 * dmas)


def wait(eng, sem, count):
    if not isinstance(count, int) or count > 0:
        eng.wait_ge(sem, count)


def over_batches(eng, first, step):
    start = 2 * Q
    loops = (NB - start) // Q - 1
    for n in range(first, start):
        step(Batch(0, n))
    with eng.Fori(0, loops) as it:
        for c in range(Q):
            step(Batch(it, start + c))
    for n in range(start + loops * Q, NB + 2):
        step(Batch(0, n))


def bc(ap, axis, shape):
    return ap.unsqueeze(axis).to_broadcast(shape)


def load_windows(nc, eng, L, S, win, win_in, b, tiles):
    _, bases = nc.values_load_multi_w_load_instructions(
        S["base_row"][0:1, bass.ds(b.n * B + tiles[0], len(tiles))], engines=[eng.engine], min_val=0, max_val=N,
        skip_runtime_bounds_check_because="they are destinations, which lie in 0..N")
    for j, base in zip(tiles, bases):
        eng.dma_start(win[:, b.q, j, :], L.window_table[bass.ds(base, P), :]).then_inc(win_in[b.q], 16)


def edge_pass(nc, L, S, hist):
    soft = L.heads > 0
    H = L.heads
    ax = L.attr
    groups = {0: [], 32: [(0, 4), (4, 3)], 16: [(0, 7)]}[ax]
    ctx = ExitStack()
    with ctx:
        def sb(name, shape, dt=F32):
            return ctx.enter_context(nc.sbuf_tensor(f"{L.name}_{name}", shape, dt))

        def pb(name, shape):
            return ctx.enter_context(nc.psum_tensor(f"{L.name}_{name}", shape, F32))

        def sem(name):
            return ctx.enter_context(nc.semaphore(f"{L.name}_{name}"))

        idx = sb("idx", [P, Q, B], I32)
        G = sb("G", [P, Q, B * L.gathered])
        rel = sb("rel", [P, Q, B * P], BF16)
        same = sb("same", [P, Q, B, P])
        out_rows = sb("out_rows", [P, Q, B * L.row])
        Gv = G[:].rearrange("p q (b w) -> p q b w", b=B)
        outv = out_rows[:].rearrange("p q (b w) -> p q b w", b=B)
        relv = rel[:].rearrange("p q (b e) -> p q b e", b=B)
        sums = [pb(f"sums{q}", [P, 512]) for q in range(Q)]
        if L.window:
            hot = sb("hot", [P, Q, B, P], L.win_dt)
            win = sb("win", [P, Q, B, L.parts * L.window], L.win_dt)
            z_banks = 1 if soft else Q
            z = [pb(f"z{q}", [P, 512]) for q in range(z_banks)]
            zs = sb("zs", [P, Q, B * L.window])
            act_out = sb("act_out", [P, Q, B * L.window])
        if ax:
            attr = sb("attr", [P, Q, B, ax])
            attrT = sb("attrT", [P, Q, 2, P])
            attrT_ps = pb("attrT_ps", [P, 512])
        if soft:
            logits = sb("logits", [P, Q, B * H]) if H > 1 else act_out
            edges = sb("edges", [B * H, Q, 2, P])
            runmax = sb("runmax", [B * H, P])
            segmax = sb("segmax", [B * H, Q, P])
            diff = sb("diff", [P, Q, B * H])
            msg = sb("msg", [P, Q, B, L.msg])
            lt_ps = pb("lt_ps", [P, 512])[0:B * H, 0:P]
            mb_all = pb("mb_ps", [P, 512])
            mb_ps = mb_all[:, 0:B * H]
            mb_cols = B * H + B * H % 2
        if hist:
            hot_hi = sb("hot_hi", [P, Q, B, HI], BF16)
            hot_lo = sb("hot_lo", [P, Q, B, P], BF16)
            count_ps = pb("count_ps", [P, 512])

        idx_ready = sem("idx_ready")
        gather_turn = sem("gather_turn")
        gathered = [S[f"{L.name}_gathered{q}"] for q in range(Q)]
        rel_in = [sem(f"rel_in{q}") for q in range(Q)]
        stored = [sem(f"stored{q}") for q in range(Q)]
        masks_made = sem("masks_made")
        sums_made = sem("sums_made")
        sums_copied = sem("sums_copied")
        z_added = sem("z_added")
        act_done = sem("act_done")
        if L.window:
            win_in = [sem(f"win_in{q}") for q in range(Q)]
            hot_made = sem("hot_made")
            z_made = sem("z_made")
        if ax:
            attr_in = [sem(f"attr_in{q}") for q in range(Q)]
            attr_turned = sem("attr_turned")
            attr_copied = sem("attr_copied")
        if soft:
            edges_in = [sem(f"edges_in{q}") for q in range(Q)]
            att_done = sem("att_done")
            logits_ready = sem("logits_ready")
            logits_turned = sem("logits_turned")
            prefix_done = sem("prefix_done")
            max_ready = sem("max_ready")
            max_turned = sem("max_turned")
            diff_ready = sem("diff_ready")
            weights_ready = sem("weights_ready")
            msg_ready = sem("msg_ready")
        if hist:
            hist_ready = sem("hist_ready")
            hist_used = sem("hist_used")
        lg_ready = (logits_ready if H > 1 else act_done) if soft else None
        block = ctx.enter_context(nc.Block())

        relD = S["rel_rows"]
        Tv = S["T_" + L.name].rearrange("(n p b) w -> n p (b w)", p=P, b=B)

        @block.sync
        def _(sp):
            def step(i):
                b = i + 2
                if b.exists():
                    wait(sp, masks_made, b.used(Q))
                    sp.dma_start(rel[:, b.q, :],
                                 relD[bass.ds(b.n * (B * P), B * P)].unsqueeze(0).to_broadcast([P, B * P])
                                 ).then_inc(rel_in[b.q], 16)
                    if ax:
                        wait(sp, attr_turned, b.used(Q))
                        attr_load(b)
                    if L.window:
                        wait(sp, z_made, b.used(Q))
                        load_windows(nc, sp, L, S, win, win_in, b, range(0, SP_TILES))
                o = i + (-2)
                if o.exists():
                    wait(sp, sums_copied, o.used())
                    sp.dma_start(Tv[bass.ds(o.n, 1), :, :].rearrange("a p w -> p (a w)"),
                                 out_rows[:, o.q, :]).then_inc(stored[o.q], 16)
                if soft and b.exists():
                    wait(sp, max_ready, b.used(Q))
                    src = S["edge_rows"][bass.ds(b.n * B, B), 0:H, :].rearrange("b h x -> (b h) x")
                    sp.dma_start(edges[:, b.q, :, :].rearrange("r a e -> r (a e)"), src
                                 ).then_inc(edges_in[b.q], 16)

            def attr_load(b):
                A = S["attr"][ax]
                n0 = b.n * B
                if isinstance(n0, int) and n0 + B > EFULL:
                    whole = max(0, EFULL - n0)
                    if whole:
                        sp.dma_start(attr[:, b.q, 0:whole, :],
                                     A[n0 * P:(n0 + whole) * P, :].rearrange("(b p) f -> p b f", p=P)
                                     ).then_inc(attr_in[b.q], 16)
                    if n0 <= EFULL:
                        sp.dma_start(attr[0:EREST, b.q, whole, :], A[EFULL * P:E, :]).then_inc(attr_in[b.q], 16)
                else:
                    sp.dma_start(attr[:, b.q, :, :],
                                 A[bass.ds(b.n * (B * P), B * P), :].rearrange("(b p) f -> p b f", p=P)
                                 ).then_inc(attr_in[b.q], 16)

            over_batches(sp, -2, step)
            for n in range(NB - Q, NB):
                sp.wait_ge(stored[n % Q], Batch(0, n).landed())

        @block.gpsimd
        def _(pool):
            freed = {"mlp": z_added, "gatv2": None, "gat": None, "mean": sums_made}[L.name]
            freed = freed or msg_ready

            def step(b):
                if not b.exists():
                    return
                wait(pool, idx_ready, b.used())
                wait(pool, freed, b.used(Q))
                pool.sem_inc(gather_turn, 1)
                for j in range(B):
                    pool.indirect_dma_start(
                        out=G[:, b.q, j * L.gathered:(j + 1) * L.gathered], out_offset=None,
                        in_=L.gather_table, in_offset=bass.IndirectOffsetOnAxis(ap=idx[:, b.q, j:j + 1], axis=0)
                    ).then_inc(gathered[b.q], 16)

            over_batches(pool, 0, step)

        @block.vector
        def _(dve):
            def one_hots(b):
                wait(dve, rel_in[b.q], b.landed())
                wait(dve, z_made, b.used(Q))
                nc.vector.tensor_scalar(hot[:, b.q, :, :], relv[:, b.q, :, :], S["lane"][:, 0:1], None,
                                        ALU.is_equal).then_inc(hot_made, 1)

            def same_destination(b):
                wait(dve, rel_in[b.q], b.landed())
                wait(dve, sums_made, b.used(Q))
                nc.vector.tensor_tensor(same[:, b.q, :, :], relv[:, b.q, :, :],
                                        bc(S["rel_cols"][:, bass.ds(b.n * B, B)], 2, [P, B, P]),
                                        ALU.is_equal).then_inc(masks_made, 1)

            def indices(b):
                nc.vector.tensor_copy(idx[:, b.q, :], S["src_cols"][:, bass.ds(b.n * B, B)]).then_inc(idx_ready, 1)

            def add_gathered(b):
                wait(dve, gathered[b.q], b.landed(B))
                wait(dve, z_made, b.used())
                if not soft:
                    wait(dve, act_done, b.used(Q))
                w = L.window
                nc.vector.tensor_tensor(zs[:, b.q, :].rearrange("p (b w) -> p b w", w=w),
                                        z[b.q % z_banks][:, 0:B * w].rearrange("p (b w) -> p b w", w=w),
                                        Gv[:, b.q, :, L.gathered - w:L.gathered], ALU.add).then_inc(z_added, 1)
                if soft:
                    wait(dve, z_added, b.used())
                    nc.vector.scalar_tensor_tensor(out=act_out[:, b.q, :], in0=zs[:, b.q, :], scalar=SLOPE,
                                                   in1=zs[:, b.q, :], op0=ALU.mult, op1=ALU.max
                                                   ).then_inc(act_done, 1)

            def prefix(b):
                wait(dve, logits_turned, b.used())
                wait(dve, edges_in[b.q], b.landed())
                nc.vector.tensor_tensor_scan(runmax[:, :], edges[:, b.q, 0, :], lt_ps, 0.0, ALU.add, ALU.max
                                             ).then_inc(prefix_done, 1)
                wait(dve, prefix_done, b.used())
                wait(dve, max_turned, b.used(Q))
                nc.vector.tensor_tensor_scan(segmax[:, b.q, ::-1], edges[:, b.q, 1, ::-1], runmax[:, ::-1],
                                             0.0, ALU.add, ALU.max).then_inc(max_ready, 1)

            def heads_dot(b):
                wait(dve, act_done, b.used())
                g4 = act_out[:, b.q, :].rearrange("p (b w) -> p b w", b=B)
                nc.vector.tensor_tensor(zs[:, b.q, :].rearrange("p (b w) -> p b w", b=B), g4,
                                        bc(S["att_bc"][:, :], 1, [P, B, D]), ALU.mult).then_inc(att_done, 1)
                wait(dve, att_done, b.used())
                nc.vector.tensor_reduce(logits[:, b.q, :],
                                        zs[:, b.q, :].rearrange("p (r c) -> p r c", c=D // H), AX, ALU.add
                                        ).then_inc(logits_ready, 1)

            def subtract_max(b):
                wait(dve, max_turned, b.used())
                wait(dve, weights_ready, b.used(Q))
                nc.vector.tensor_tensor(diff[:, b.q, :], logits[:, b.q, :], mb_ps, ALU.subtract
                                        ).then_inc(diff_ready, 1)

            def weigh(b):
                wait(dve, weights_ready, b.used())
                c = D // H
                nc.vector.tensor_tensor(
                    msg[:, b.q, :, 0:D].rearrange("p b (h c) -> p b h c", c=c),
                    Gv[:, b.q, :, 0:D].rearrange("p b (h c) -> p b h c", c=c),
                    bc(msg[:, b.q, :, D:D + H], 3, [P, B, H, c]), ALU.mult).then_inc(msg_ready, 1)

            def count(b):
                wait(dve, hist_used, b.used(Q))
                nc.vector.tensor_tensor(hot_hi[:, b.q, :, :], bc(S["iota"][:, 0:HI], 1, [P, B, HI]),
                                        bc(S["hi_cols"][:, bass.ds(b.n * B, B)], 2, [P, B, HI]), ALU.is_equal)
                nc.vector.tensor_tensor(hot_lo[:, b.q, :, :], bc(S["iota"][:, :], 1, [P, B, P]),
                                        bc(S["lo_cols"][:, bass.ds(b.n * B, B)], 2, [P, B, P]), ALU.is_equal
                                        ).then_inc(hist_ready, 1)

            def step(i):
                if L.window and (i + 1).exists():
                    one_hots(i + 1)
                if i.exists():
                    if L.window:
                        add_gathered(i)
                    else:
                        wait(dve, gathered[i.q], i.landed(B))
                if (i + 3).exists():
                    indices(i + 3)
                if soft:
                    p = i + (-1)
                    if p.exists():
                        prefix(p)
                    if i.exists() and H > 1:
                        heads_dot(i)
                    if p.exists():
                        subtract_max(p)
                    if i.exists():
                        same_destination(i)
                    if p.exists():
                        weigh(p)
                elif i.exists():
                    same_destination(i)
                if hist and i.exists():
                    count(i)

            for n in range(2):
                indices(Batch(0, n))
            over_batches(dve, -1, step)
            if hist:
                dve.wait_ge(hist_used, NB)
                nc.vector.tensor_copy(S["counts"][:, :], count_ps[0:HI, 0:P])

        @block.scalar
        def _(act):
            def copy_sums(b):
                wait(act, sums_made, b.used())
                wait(act, stored[b.q], b.landed_before())
                act.activation(outv[:, b.q, :, 0:L.msg],
                               sums[b.q][:, 0:B * L.msg].rearrange("p (b w) -> p b w", b=B), ACT.Copy
                               ).then_inc(sums_copied, 1)

            def copy_attr(b):
                wait(act, attr_turned, b.used())
                wait(act, z_made, b.used(Q))
                for g, (t0, nt) in enumerate(groups):
                    last = act.activation(attrT[0:nt * ax, b.q, g, :], attrT_ps[0:nt * ax, g * P:(g + 1) * P],
                                          ACT.Copy)
                last.then_inc(attr_copied, 1)

            def nonlinear(b):
                wait(act, z_added, b.used())
                wait(act, sums_made, b.used(Q))
                act.activation(act_out[:, b.q, :], zs[:, b.q, :], ACT.Relu).then_inc(act_done, 1)

            def exponentiate(b):
                wait(act, diff_ready, b.used())
                wait(act, sums_made, b.used(Q))
                wait(act, stored[b.q], b.landed_before())
                act.activation(outv[:, b.q, :, L.msg:L.row],
                               mb_ps.rearrange("p (b h) -> p b h", h=H), ACT.Copy)
                act.activation(msg[:, b.q, :, D:D + H],
                               diff[:, b.q, :].rearrange("p (b h) -> p b h", h=H), ACT.Exp
                               ).then_inc(weights_ready, 1)

            def step(i):
                if (i + (-2)).exists():
                    copy_sums(i + (-2))
                if ax and (i + 1).exists():
                    copy_attr(i + 1)
                if L.window and not soft and i.exists():
                    nonlinear(i)
                w = i + 2
                if L.window and w.exists():
                    wait(act, z_made, w.used(Q))
                    load_windows(nc, act, L, S, win, win_in, w, range(SP_TILES, B))
                if soft and (i + (-1)).exists():
                    exponentiate(i + (-1))

            over_batches(act, -2, step)

        @block.tensor
        def _(pe):
            ident = S["ident"]

            def turn_attr(b):
                n0 = b.n * B
                partial = isinstance(n0, int) and n0 + B > EFULL
                dmas = (1 if EFULL > n0 else 0) + (1 if n0 <= EFULL else 0) if partial else 1
                wait(pe, attr_in[b.q], b.landed_before() + 16 * dmas if partial else b.landed())
                wait(pe, attr_copied, b.used(1))
                for g, (t0, nt) in enumerate(groups):
                    last = pe.transpose(attrT_ps[0:nt * ax, g * P:(g + 1) * P],
                                        attr[:, b.q, t0:t0 + nt, :].rearrange("p b f -> p (b f)"), ident[:, :])
                last.then_inc(attr_turned, 1)

            def make_z(b):
                wait(pe, hot_made, b.used())
                wait(pe, win_in[b.q], b.landed(B))
                wait(pe, z_added, b.used(z_banks))
                w = L.window
                if ax:
                    wait(pe, attr_copied, b.used())
                for t0, nt in groups or [(0, B)]:
                    if ax:
                        g = groups.index((t0, nt))
                        pe.matmul(z[b.q % z_banks][:, t0 * w:(t0 + nt) * w], attrT[0:nt * ax, b.q, g, :],
                                  S["attr_w"][ax][0:nt * ax, 0:nt * w], start=True, stop=True)
                    for j in range(t0, t0 + nt):
                        for part in range(L.parts):
                            last = pe.matmul(z[b.q % z_banks][:, j * w:(j + 1) * w], hot[:, b.q, j, :],
                                             win[:, b.q, j, part * w:(part + 1) * w],
                                             start=not ax and part == 0, stop=True, skip_group_check=True)
                last.then_inc(z_made, 1)

            def turn_max(b):
                wait(pe, max_ready, b.used())
                wait(pe, diff_ready, b.used(1))
                wait(pe, weights_ready, b.used(1))
                pe.matmul(mb_all[:, 0:mb_cols], segmax[:, b.q, :], ident[0:B * H, 0:mb_cols], start=True, stop=True
                          ).then_inc(max_turned, 1)

            def turn_logits(b):
                wait(pe, lg_ready, b.used())
                wait(pe, max_ready, b.used(1))
                pe.transpose(lt_ps, logits[:, b.q, :], ident[:, :]).then_inc(logits_turned, 1)

            def make_sums(b):
                wait(pe, masks_made, b.used())
                if soft:
                    wait(pe, msg_ready, b.used())
                elif L.window:
                    wait(pe, act_done, b.used())
                else:
                    wait(pe, gathered[b.q], b.landed(B))
                wait(pe, sums_copied, b.used(Q))
                for j in range(B):
                    if soft:
                        rhs = msg[:, b.q, j, :]
                    elif L.window:
                        rhs = act_out[:, b.q, j * D:(j + 1) * D]
                    else:
                        rhs = Gv[:, b.q, j, :]
                    last = pe.matmul(sums[b.q][:, j * L.msg:(j + 1) * L.msg], same[:, b.q, j, :], rhs,
                                     start=True, stop=True)
                last.then_inc(sums_made, 1)

            def add_counts(b):
                wait(pe, hist_ready, b.used())
                for j in range(B):
                    first = isinstance(b.n, int) and b.n == 0 and j == 0
                    final = isinstance(b.n, int) and b.n == NB - 1 and j == B - 1
                    last = pe.matmul(count_ps[0:HI, 0:P], hot_hi[:, b.q, j, :], hot_lo[:, b.q, j, :],
                                     start=first, stop=final, skip_group_check=True)
                last.then_inc(hist_used, 1)

            def step(i):
                p = i + (-1)
                if ax and (i + 1).exists():
                    turn_attr(i + 1)
                if soft and p.exists():
                    turn_max(p)
                if L.window and (i + 1).exists():
                    make_z(i + 1)
                if soft and i.exists():
                    turn_logits(i)
                if p.exists():
                    make_sums(p)
                if hist and p.exists():
                    add_counts(p)

            over_batches(pe, -1, step)


class Chain:

    def __init__(self, eng, sem):
        self.eng, self.sem, self.count = eng, sem, 0

    def __call__(self, instruction):
        instruction.then_inc(self.sem, 1)
        self.count += 1
        self.eng.wait_ge(self.sem, self.count)


def prepare(nc, S, A, zero_fill):
    W = RB * P
    ctx = ExitStack()
    with ctx:
        def sb(name, shape, dt=F32):
            return ctx.enter_context(nc.sbuf_tensor("prep_" + name, shape, dt))

        def sem(name):
            return ctx.enter_context(nc.semaphore("prep_" + name))

        rows = {k: sb(k + "_rows", [P, RB, P], I32) for k in ("src", "dst")}
        f = {k: sb(k + "_f", [P, RB, P]) for k in ("src", "dst", "rel", "hi", "lo")}
        hi_int = sb("hi_int", [P, RB, P], I32)
        rel_bf = sb("rel_bf", [P, RB, P], BF16)
        masks = sb("masks", [P, RB, 2, P])
        next_first = sb("next_first", [P, RB], I32)
        ends = sb("ends", [P, RB])
        one_int = sb("one_int", [1, 2], I32)
        zeros = sb("zeros", [P, KP * (D + 2 * HEADS)])
        last_a = sb("last_a", [D + HEADS, NT], I32)
        last_b = sb("last_b", [D + HEADS, NT], I32)
        iota_i = sb("iota_i", [P, P], I32)
        lane_i = sb("lane_i", [P, 1], I32)
        turned = [ctx.enter_context(nc.psum_tensor(f"prep_turned{n}", [P, SG * P], F32)) for n in range(2)]
        cleared = sem("cleared")
        chain_v = sem("chain_v")
        chain_g = sem("chain_g")
        edges_in = sem("edges_in")
        params_in = sem("params_in")
        ident_made = sem("ident_made")
        weights_cleared = sem("weights_cleared")
        rows_made = sem("rows_made")
        rows_out = sem("rows_out")
        back_in = sem("back_in")
        turned_made = sem("turned_made")
        turned_used = sem("turned_used")
        zeros_made = sem("zeros_made")
        zeros_out = sem("zeros_out")
        block = ctx.enter_context(nc.Block())
        full_r, full_q = EFULL // P, EFULL % P
        jobs = [(k, r) for k in ("src", "rel", "hi", "lo") for r in range(0, RB, SG)]
        cols = {"src": S["src_cols"], "rel": S["rel_cols"], "hi": S["hi_cols"], "lo": S["lo_cols"]}

        @block.sync
        def _(sp):
            sp.wait_ge(cleared, 1)
            loads = 0
            for k in ("dst", "src"):
                e = A[k]
                sp.dma_start(rows[k][:, 0:full_r, :], e[0:full_r * P * P].rearrange("(r q e) -> q r e", q=P, e=P)
                             ).then_inc(edges_in, 16)
                sp.dma_start(rows[k][0:full_q, full_r, :],
                             e[full_r * P * P:EFULL * P].rearrange("(q e) -> q e", e=P)).then_inc(edges_in, 16)
                sp.dma_start(rows[k][full_q:full_q + 1, full_r, 0:EREST], e[EFULL * P:E].unsqueeze(0)
                             ).then_inc(edges_in, 16)
            X = S["X"]
            params = [
                (X[:, 0:KN - 1, :], A["x"][0:(KN - 1) * P, :].rearrange("(k p) f -> p k f", p=P)),
                (X[0:NREST, KN - 1, :], A["x"][(KN - 1) * P:N, :]),
                (S["w1"][:, 0:D], A["L0_gnn_W1"][0:D, :]),
                (S["w1"][:, D:2 * D], A["L0_gnn_W1"][D:2 * D, :]),
                (S["w2"][:, :], A["L0_gnn_W2"]),
                (S["bias0"][:, D:2 * D], A["L0_gnn_b1"].unsqueeze(0).to_broadcast([P, D])),
                (S["b2"][:, :], A["L0_gnn_b2"].unsqueeze(0).to_broadcast([P, D])),
                (S["wlr"][:, 0:D], A["L1_gnn_W_l"]),
                (S["wlr"][:, D:2 * D], A["L1_gnn_W_r"]),
                (S["bias1"][:, 0:D], A["L1_gnn_b_l"].unsqueeze(0).to_broadcast([P, D])),
                (S["bias1"][:, D:2 * D], A["L1_gnn_b_r"].unsqueeze(0).to_broadcast([P, D])),
                (S["att_bc"][:, :], A["L1_gnn_att"].rearrange("h c -> (h c)").unsqueeze(0).to_broadcast([P, D])),
                (S["bias"][:, :], A["L1_gnn_bias"].unsqueeze(0).to_broadcast([P, D])),
                (S["gamma"][:, :], A["L1_gnn_gamma"].unsqueeze(0).to_broadcast([P, D])),
                (S["beta"][:, :], A["L1_gnn_beta"].unsqueeze(0).to_broadcast([P, D])),
                (S["w3"][:, 0:D], A["L2_gnn_W"]),
            ]
            sp.wait_ge(weights_cleared, 1)
            for dst, src in params:
                sp.dma_start(dst, src).then_inc(params_in, 16)
            with nc.allow_non_contiguous_dma(reason="the two halves of a, once"):
                sp.dma_start(S["a2"][:, :], A["L2_gnn_a"].rearrange("(s f) -> f s", s=2)).then_inc(params_in, 16)
            n = len(params) + 1
            for width, tiles, w in ((32, 4, A["L0_gnn_W1"][2 * D:2 * D + 32, :]), (16, B, A["L1_gnn_W_e"])):
                for j in range(tiles):
                    sp.dma_start(S["attr_w"][width][j * width:(j + 1) * width, j * D:(j + 1) * D], w
                                 ).then_inc(params_in, 16)
                n += tiles
            sp.wait_ge(zeros_made, 1)
            for t in zero_fill:
                w = t.shape[1]
                sp.dma_start(t.rearrange("(p k) w -> p (k w)", p=P), zeros[:, 0:KP * w]).then_inc(zeros_out, 16)
            sp.wait_ge(rows_made, 1)
            view = S["rel_rows"].rearrange("(r q e) -> q r e", q=P, e=P)
            sp.dma_start(view, rel_bf[:, :, :]).then_inc(rows_out, 16)
            for h in range(HEADS):
                sp.dma_start(S["edge_rows"][:, h, :].rearrange("(r q) x -> q r x", q=P),
                             masks[:, :, :, :].rearrange("p r a e -> p r (a e)")).then_inc(rows_out, 16)
            with nc.allow_non_contiguous_dma(reason="one number per tile, once"):
                sp.dma_start(S["first_dram"][0:NTP].rearrange("(r q) -> q r", q=P), rows["dst"][:, :, 0]
                             ).then_inc(rows_out, 16)
                sp.dma_start(S["last_dram"][1:NTP + 1].rearrange("(r q) -> q r", q=P), rows["dst"][:, :, P - 1]
                             ).then_inc(rows_out, 16)
            sp.dma_start(S["first_dram"][NTP:NTP + 1].unsqueeze(0), one_int[0:1, 0:1]).then_inc(rows_out, 16)
            sp.dma_start(S["last_dram"][0:1].unsqueeze(0), one_int[0:1, 1:2]).then_inc(rows_out, 16)
            sp.wait_ge(rows_out, 16 * (5 + HEADS))
            sp.dma_start(S["base_row"][0:1, :], S["first_dram"][0:NTP].unsqueeze(0)).then_inc(back_in, 16)
            with nc.allow_non_contiguous_dma(reason="one number per tile, once"):
                sp.dma_start(next_first[:, :], S["first_dram"][1:NTP + 1].rearrange("(r q) -> q r", q=P)
                             ).then_inc(back_in, 16)
            for dst, o in ((last_a, 0), (last_b, 1)):
                sp.dma_start(dst[:, :], S["last_dram"][o:o + NT].unsqueeze(0).to_broadcast([D + HEADS, NT])
                             ).then_inc(back_in, 16)
            sp.wait_ge(params_in, 16 * n)
            sp.wait_ge(zeros_out, 16 * len(zero_fill))
            sp.wait_ge(back_in, 64)

        @block.gpsimd
        def _(pool):
            pool.memset(rows["dst"][:, RB - 1, :], N)
            pool.memset(rows["src"][:, RB - 1, :], 0).then_inc(cleared, 1)
            pool.memset(S["X"][:, KN - 1:KP, :], 0.0)
            pool.memset(S["bias0"][:, 0:D], 0.0)
            pool.memset(S["attr_w"][32][:, :], 0.0)
            pool.memset(S["attr_w"][16][:, :], 0.0).then_inc(weights_cleared, 1)
            pool.memset(zeros[:, :], 0.0)
            pool.memset(one_int[0:1, 0:1], N)
            pool.memset(one_int[0:1, 1:2], -1).then_inc(zeros_made, 1)
            chain = Chain(pool, chain_g)
            chain(pool.memset(S["ident"][:, :], 0.0))
            chain(pool.affine_select(out=S["ident"][:, :], in_=S["ident"][:, :], compare_op=ALU.not_equal, fill=1.0,
                                     base=0, pattern=[[-1, P]], channel_multiplier=1))
            chain(pool.memset(S["tri"][:, :], 1.0))
            chain(pool.affine_select(out=S["tri"][:, :], in_=S["tri"][:, :], compare_op=ALU.is_gt, fill=0.0,
                                     base=0, pattern=[[1, HI]], channel_multiplier=-1))
            pool.memset(S["ones"][:, :], 1.0)
            pool.iota(iota_i[:, :], pattern=[[1, P]], base=0, channel_multiplier=0)
            pool.iota(lane_i[:, :], pattern=[[1, 1]], base=0, channel_multiplier=1).then_inc(ident_made, 1)

        @block.vector
        def _(dve):
            v = nc.vector
            chain = Chain(dve, chain_v)
            dve.wait_ge(edges_in, 16 * 6)
            v.tensor_copy(f["src"][:, :, :], rows["src"][:, :, :])
            chain(v.tensor_copy(f["dst"][:, :, :], rows["dst"][:, :, :]))
            v.tensor_tensor(f["rel"][:, :, :], f["dst"][:, :, :], f["dst"][:, :, 0:1].to_broadcast([P, RB, P]),
                            ALU.subtract)
            chain(v.tensor_scalar(hi_int[:, :, :], f["dst"][:, :, :], 1.0 / P, 127.0 / 256.0, ALU.mult,
                                  ALU.subtract))
            v.tensor_copy(rel_bf[:, :, :], f["rel"][:, :, :])
            v.memset(masks[:, :, :, :], 0.0)
            chain(v.tensor_copy(f["hi"][:, :, :], hi_int[:, :, :]))
            v.scalar_tensor_tensor(out=f["lo"][:, :, :], in0=f["hi"][:, :, :], scalar=-float(P),
                                   in1=f["dst"][:, :, :], op0=ALU.mult, op1=ALU.add)
            v.tensor_tensor(masks[:, :, 0, 1:P], f["rel"][:, :, 1:P], f["rel"][:, :, 0:P - 1], ALU.is_equal)
            chain(v.tensor_tensor(masks[:, :, 1, 0:P - 1], f["rel"][:, :, 1:P], f["rel"][:, :, 0:P - 1],
                                  ALU.is_equal))
            v.tensor_scalar(masks[:, :, :, :].rearrange("p r a e -> p (r a e)"),
                            masks[:, :, :, :].rearrange("p r a e -> p (r a e)"), 1.0, BIG, ALU.subtract,
                            ALU.mult).then_inc(rows_made, 1)
            dve.wait_ge(ident_made, 1)
            v.tensor_copy(S["iota"][:, :], iota_i[:, :])
            v.tensor_copy(S["lane"][:, :], lane_i[:, :])
            for n, (k, r) in enumerate(jobs):
                m = min(SG, RB - r)
                dve.wait_ge(turned_made, n + 1)
                v.tensor_copy(cols[k][:, r * P:(r + m) * P], turned[n % 2][:, 0:m * P]).then_inc(turned_used, 1)
            dve.wait_ge(back_in, 64)
            chain(v.tensor_tensor(ends[:, :], next_first[:, :], rows["dst"][:, :, 0], ALU.is_equal))
            v.scalar_tensor_tensor(out=S["carry_row"][:, :], in0=ends[:, :], scalar=float(1 << 20),
                                   in1=rows["dst"][:, :, 0], op0=ALU.mult, op1=ALU.add)
            v.tensor_tensor(S["through"][:, :], last_a[:, :], last_b[:, :], ALU.is_equal)

        @block.tensor
        def _(pe):
            pe.wait_ge(ident_made, 1)
            pe.wait_ge(rows_made, 1)
            for n, (k, r) in enumerate(jobs):
                m = min(SG, RB - r)
                wait(pe, turned_used, n - 1)
                for j in range(m):
                    last = pe.transpose(turned[n % 2][:, j * P:(j + 1) * P], f[k][:, r + j, :], S["ident"][:, :])
                last.then_inc(turned_made, 1)


def rank(nc, S):
    ctx = ExitStack()
    with ctx:
        def sb(name, shape, dt=F32):
            return ctx.enter_context(nc.sbuf_tensor("rank_" + name, shape, dt))

        ones = sb("ones", [HI, P])
        upto = sb("upto", [HI, P])
        before = sb("before", [HI, 1])
        last = sb("last", [P, HI])
        first = sb("first", [P, HI])
        whole = sb("whole", [P, HI], I32)
        tile_l = sb("tile_l", [P, HI])
        tile_f = sb("tile_f", [P, HI])
        batch = sb("batch", [P, HI])
        ps = ctx.enter_context(nc.psum_tensor("rank_ps", [P, 512], F32))
        chain_v = ctx.enter_context(nc.semaphore("rank_chain_v"))
        scanned = ctx.enter_context(nc.semaphore("rank_scanned"))
        summed = ctx.enter_context(nc.semaphore("rank_summed"))
        added = ctx.enter_context(nc.semaphore("rank_added"))
        turned = ctx.enter_context(nc.semaphore("rank_turned"))
        block = ctx.enter_context(nc.Block())

        @block.vector
        def _(dve):
            v = nc.vector
            chain = Chain(dve, chain_v)
            chain(v.memset(ones[:, :], 1.0))
            v.tensor_tensor_scan(upto[:, :], ones[:, :], S["counts"][:, :], 0.0, ALU.mult, ALU.add
                                 ).then_inc(scanned, 1)
            dve.wait_ge(summed, 1)
            chain(v.tensor_copy(before[:, :], ps[0:HI, 0:1]))
            v.tensor_scalar(upto[:, :], upto[:, :], before[:, 0:1], None, ALU.add).then_inc(added, 1)
            dve.wait_ge(turned, 1)
            v.tensor_copy(S["degree"][:, :], ps[:, P:P + HI])
            chain(v.tensor_scalar(last[:, :], ps[:, 2 * P:2 * P + HI], 1.0, None, ALU.subtract))
            chain(v.tensor_tensor(first[:, :], last[:, :], S["degree"][:, :], ALU.subtract))
            chain(v.tensor_scalar(first[:, :], first[:, :], 1.0, None, ALU.add))
            for e, t in ((first, tile_f), (last, tile_l)):
                chain(v.tensor_scalar(whole[:, :], e[:, :], 1.0 / P, 127.0 / 256.0, ALU.mult, ALU.subtract))
                chain(v.tensor_copy(t[:, :], whole[:, :]))
            v.tensor_tensor(S["spans"][:, :], tile_l[:, :], tile_f[:, :], ALU.is_gt)
            chain(v.tensor_scalar(whole[:, :], tile_l[:, :], 1.0 / B, 3.0 / B, ALU.mult, ALU.subtract))
            chain(v.tensor_copy(batch[:, :], whole[:, :]))
            chain(v.scalar_tensor_tensor(out=last[:, :], in0=tile_l[:, :], scalar=-float(P), in1=last[:, :],
                                         op0=ALU.mult, op1=ALU.add))
            chain(v.scalar_tensor_tensor(out=last[:, :], in0=last[:, :], scalar=float(B), in1=tile_l[:, :],
                                         op0=ALU.mult, op1=ALU.add))
            v.scalar_tensor_tensor(out=S["last_row"][:, :], in0=batch[:, :], scalar=float(P * B - B),
                                   in1=last[:, :], op0=ALU.mult, op1=ALU.add)

        @block.tensor
        def _(pe):
            pe.wait_ge(scanned, 1)
            pe.matmul(ps[0:HI, 0:1], S["tri"][:, :], upto[:, P - 1:P], start=True, stop=True).then_inc(summed, 1)
            pe.wait_ge(added, 1)
            pe.transpose(ps[:, P:P + HI], S["counts"][:, :], S["ident"][0:HI, 0:HI])
            pe.transpose(ps[:, 2 * P:2 * P + HI], upto[:, :], S["ident"][0:HI, 0:HI]).then_inc(turned, 1)


def project(nc, name, source, blocks, weights, cols, S, evacuate, store=None):
    ctx = ExitStack()
    with ctx:
        turned = [ctx.enter_context(nc.psum_tensor(f"{name}_turned{n}", [D, SG * P], F32)) for n in range(2)]
        out = [ctx.enter_context(nc.psum_tensor(f"{name}_out{n}", [P, 512], F32)) for n in range(2)]
        lhsT = ctx.enter_context(nc.sbuf_tensor(name + "_lhsT", [D, 2, SG * P], F32))
        turned_made = ctx.enter_context(nc.semaphore(name + "_turned_made"))
        turned_copied = ctx.enter_context(nc.semaphore(name + "_turned_copied"))
        product_made = ctx.enter_context(nc.semaphore(name + "_product_made"))
        product_used = ctx.enter_context(nc.semaphore(name + "_product_used"))
        tables_out = ctx.enter_context(nc.semaphore(name + "_tables_out"))
        block = ctx.enter_context(nc.Block())
        groups = [(k, min(SG, blocks - k)) for k in range(0, blocks, SG)]

        @block.tensor
        def _(pe):
            def turn(n):
                k, m = groups[n]
                wait(pe, turned_copied, n - 1)
                for j in range(m):
                    last = pe.transpose(turned[n % 2][:, j * P:(j + 1) * P], source[:, k + j, :], S["ident"][:, :])
                last.then_inc(turned_made, 1)

            turn(0)
            for n, (k, m) in enumerate(groups):
                if n + 1 < len(groups):
                    turn(n + 1)
                pe.wait_ge(turned_copied, n + 1)
                wait(pe, product_used, n - 1)
                for j in range(m):
                    last = pe.matmul(out[n % 2][:, j * cols:(j + 1) * cols], lhsT[:, n % 2, j * P:(j + 1) * P],
                                     weights, start=True, stop=True)
                last.then_inc(product_made, 1)

        @block.scalar
        def _(act):
            for n, (k, m) in enumerate(groups):
                act.wait_ge(turned_made, n + 1)
                wait(act, product_made, n - 1)
                act.activation(lhsT[:, n % 2, 0:m * P], turned[n % 2][:, 0:m * P], ACT.Copy
                               ).then_inc(turned_copied, 1)

        @block.vector
        def _(dve):
            for n, (k, m) in enumerate(groups):
                dve.wait_ge(product_made, n + 1)
                evacuate(k, m, out[n % 2][:, 0:m * cols].rearrange("p (k w) -> p k w", k=m)
                         ).then_inc(product_used, 1)

        if store:
            @block.sync
            def _(sp):
                sp.wait_ge(product_used, len(groups))
                for dst, src in store:
                    sp.dma_start(dst, src).then_inc(tables_out, 16)
                sp.wait_ge(tables_out, 16 * len(store))


def node_view(table):
    return table.rearrange("(k p) w -> p k w", p=P)


def tables(nc, L, S, weights, cols, bias):
    g, w = L.gathered, L.window
    with nc.sbuf_tensor(L.name + "_table", [P, KP, cols], F32) as table:
        def evacuate(k, m, product):
            if bias is None:
                return nc.vector.tensor_copy(table[:, k:k + m, :], product)
            return nc.vector.tensor_tensor(table[:, k:k + m, :], product, bc(bias, 1, [P, m, cols]), ALU.add)

        store = [(node_view(L.gather_table), table[:, :, 0:g])]
        if L.parts == 1:
            store.append((node_view(L.window_table), table[:, :, g:g + w]))
        with nc.allow_non_contiguous_dma(reason="a column of the window table"):
            project(nc, L.name + "_tables", S["X"], KP, weights, cols, S, evacuate, store=store)
        if L.parts == 3:
            split_table(nc, L, table)


def split_table(nc, L, table):
    g, w = L.gathered, L.window
    with (
        nc.sbuf_tensor(L.name + "_parts", [P, KP, 3 * w], BF16) as parts,
        nc.semaphore(L.name + "_rounded") as rounded,
        nc.semaphore(L.name + "_left") as left,
        nc.semaphore(L.name + "_parts_out") as parts_out,
        nc.Block() as block,
    ):
        chunks = [(k, min(SPLIT, KP - k)) for k in range(0, KP, SPLIT)]
        jobs = [(part, k, m) for part in range(3) for k, m in chunks]

        @block.scalar
        def _(act):
            for n, (part, k, m) in enumerate(jobs):
                wait(act, left, n + 1 - len(chunks))
                act.activation(parts[:, k:k + m, part * w:(part + 1) * w], table[:, k:k + m, g:g + w], ACT.Copy
                               ).then_inc(rounded, 1)

        @block.vector
        def _(dve):
            for n, (part, k, m) in enumerate(jobs[:2 * len(chunks)]):
                dve.wait_ge(rounded, n + 1)
                nc.vector.tensor_tensor(table[:, k:k + m, g:g + w], table[:, k:k + m, g:g + w],
                                        parts[:, k:k + m, part * w:(part + 1) * w], ALU.subtract).then_inc(left, 1)

        @block.sync
        def _(sp):
            sp.wait_ge(rounded, len(jobs))
            sp.dma_start(node_view(L.window_table), parts[:, :, :]).then_inc(parts_out, 16)
            sp.wait_ge(parts_out, 16)


def carry(nc, L, S):
    soft = L.heads > 0
    H, M = L.heads, L.msg
    T, C = S["T_" + L.name], S["C_" + L.name]
    ctx = ExitStack()
    with ctx:
        def sb(name, shape, dt=F32):
            return ctx.enter_context(nc.sbuf_tensor(f"{L.name}_c_{name}", shape, dt))

        def sem(name):
            return ctx.enter_context(nc.semaphore(f"{L.name}_c_{name}"))

        tails = sb("tails", [P, LAST_C, B, L.row])
        tail_sums = sb("tail_sums", [M, NT])
        state = sb("state", [M, NTP])
        rows = sb("rows", [P, RB, L.row])
        if soft:
            wide = sb("wide", [P, LAST_C, B, M])
            tail_max = sb("tail_max", [M, NT])
            top = sb("top", [M, NTP])
            gate = sb("gate", [M, NT])
            fade = sb("fade", [M, NT])
        ps = [ctx.enter_context(nc.psum_tensor(f"{L.name}_c_ps{n}", [P, SG * P], F32)) for n in range(2)]
        tails_in, wide_made, turned, copied = sem("tails_in"), sem("wide_made"), sem("turned"), sem("copied")
        chain_v, shifted, faded, scanned = sem("chain_v"), sem("shifted"), sem("faded"), sem("scanned")
        back, back_copied, loaded = sem("back"), sem("back_copied"), sem("loaded")
        fetched, scattered = S[L.name + "_fetched"], S[L.name + "_scattered"]
        block = ctx.enter_context(nc.Block())
        counts = [min(P, NB - c * P) for c in range(LAST_C)]
        Tv = T.rearrange("(n p b) w -> n p (b w)", p=P, b=B)
        jobs = []
        for c in range(LAST_C):
            for j0 in range(0, B, SG):
                jobs.append((tail_sums, tails, c, j0, min(SG, B - j0)))
                if soft:
                    jobs.append((tail_max, wide, c, j0, min(SG, B - j0)))
        backs = [(s, r, min(SG, RB - r)) for r in range(0, RB, SG) for s in (("state", "top") if soft else ("state",))]

        @block.sync
        def _(sp):
            for c in range(LAST_C):
                sp.dma_start(tails[0:counts[c], c, :, :].rearrange("n b w -> n (b w)"),
                             Tv[c * P:c * P + counts[c], P - 1, :]).then_inc(tails_in, 16)
            sp.wait_ge(scattered, 16 * RB)
            sp.dma_start(S["node_carry"][:, :, 0:L.row], node_view(C)[:, 0:KN, :]).then_inc(loaded, 16)
            sp.wait_ge(loaded, 16)

        @block.gpsimd
        def _(pool):
            for k in range(KN):
                pool.indirect_dma_start(
                    out=S["node_sums"][:, k * L.row:(k + 1) * L.row], out_offset=None, in_=T,
                    in_offset=bass.IndirectOffsetOnAxis(ap=S["last_row"][:, k:k + 1], axis=0)).then_inc(fetched, 16)
            for r in range(RB):
                wait(pool, back_copied, sum(1 for s, r0, m in backs if r0 <= r))
                pool.indirect_dma_start(
                    out=C, out_offset=bass.IndirectOffsetOnAxis(ap=S["carry_row"][:, r:r + 1], axis=0),
                    in_=rows[:, r, :], in_offset=None, bounds_check=NP - 1, oob_is_err=False
                ).then_inc(scattered, 16)
            pool.wait_ge(fetched, 16 * KN)

        @block.tensor
        def _(pe):
            pe.wait_ge(tails_in, 16 * LAST_C)
            if soft:
                pe.wait_ge(wide_made, 1)
            for n, (dst, src, c, j0, m) in enumerate(jobs):
                wait(pe, copied, n - 1)
                k = counts[c]
                for j in range(m):
                    last = pe.transpose(ps[n % 2][0:M, j * P:j * P + k], src[0:k, c, j0 + j, 0:M],
                                        S["ident"][0:k, 0:k])
                last.then_inc(turned, 1)
            pe.wait_ge(scanned, 1)
            pe.wait_ge(copied, len(jobs))
            for n, (s, r, m) in enumerate(backs):
                wait(pe, back_copied, n - 1)
                src = state if s == "state" else top
                for j in range(m):
                    last = pe.transpose(ps[n % 2][:, j * P:j * P + M], src[:, (r + j) * P:(r + j + 1) * P],
                                        S["ident"][0:M, 0:M])
                last.then_inc(back, 1)

        @block.scalar
        def _(act):
            for n, (dst, src, c, j0, m) in enumerate(jobs):
                act.wait_ge(turned, n + 1)
                k = counts[c]
                t0 = c * P * B
                act.activation(
                    dst[:, t0:t0 + k * B].rearrange("f (n b) -> f b n", b=B)[:, j0:j0 + m, :],
                    ps[n % 2][0:M, 0:m * P].rearrange("f (b n) -> f b n", b=m)[:, :, 0:k], ACT.Copy
                ).then_inc(copied, 1)
            if soft:
                act.wait_ge(shifted, 1)
                act.activation(tail_max[:, :], tail_max[:, :], ACT.Exp)
                act.activation(fade[:, 1:NT], fade[:, 1:NT], ACT.Exp).then_inc(faded, 1)
            for n, (s, r, m) in enumerate(backs):
                act.wait_ge(back, n + 1)
                part = slice(0, M) if s == "state" else slice(D, M)
                to = slice(0, M) if s == "state" else slice(M, L.row)
                act.activation(rows[:, r:r + m, to],
                               ps[n % 2][:, 0:m * P].rearrange("p (r f) -> p r f", r=m)[:, :, part], ACT.Copy
                               ).then_inc(back_copied, 1)

        @block.vector
        def _(dve):
            v = nc.vector
            chain = Chain(dve, chain_v)
            if soft:
                dve.wait_ge(tails_in, 16 * LAST_C)
                c64 = D // H
                for c in range(LAST_C):
                    k = counts[c]
                    top_h = tails[0:k, c, :, M:L.row]
                    v.tensor_copy(wide[0:k, c, :, 0:D].rearrange("n b (h c) -> n b h c", c=c64),
                                  bc(top_h, 3, [k, B, H, c64]))
                    last = v.tensor_copy(wide[0:k, c, :, D:M], top_h)
                last.then_inc(wide_made, 1)
                v.memset(top[:, :], 0.0)
            chain(v.memset(state[:, :], 0.0))
            if soft:
                chain(v.tensor_scalar(gate[:, :], S["through"][0:M, :], 1.0, BIG, ALU.subtract, ALU.mult))
                dve.wait_ge(copied, len(jobs))
                chain(v.tensor_tensor_scan(fade[:, :], gate[:, :], tail_max[:, :], 0.0, ALU.add, ALU.max))
                v.tensor_copy(top[:, 1:NT], fade[:, 0:NT - 1])
                chain(v.tensor_tensor(tail_max[:, :], tail_max[:, :], fade[:, :], ALU.subtract))
                chain(v.tensor_tensor(gate[:, 1:NT], fade[:, 0:NT - 1], fade[:, 1:NT], ALU.subtract))
                v.tensor_scalar(fade[:, 1:NT], gate[:, 1:NT], 0.0, None, ALU.min).then_inc(shifted, 1)
                dve.wait_ge(faded, 1)
                chain(v.memset(gate[:, 0:1], 0.0))
                v.tensor_tensor(gate[:, 1:NT], fade[:, 1:NT], S["through"][0:M, 1:NT], ALU.mult)
                chain(v.tensor_tensor(tail_sums[:, :], tail_sums[:, :], tail_max[:, :], ALU.mult))
                v.tensor_tensor_scan(state[:, 1:NT], gate[:, 0:NT - 1], tail_sums[:, 0:NT - 1], 0.0,
                                     ALU.mult, ALU.add).then_inc(scanned, 1)
            else:
                dve.wait_ge(copied, len(jobs))
                v.tensor_tensor_scan(state[:, 1:NT], S["through"][0:M, 0:NT - 1], tail_sums[:, 0:NT - 1], 0.0,
                                     ALU.mult, ALU.add).then_inc(scanned, 1)


def spread(ap, w):
    return bc(ap, 2, [ap.shape[0], ap.shape[1], w])


def edge_scores(nc, S):
    with (
        nc.psum_tensor("scores_ps", [P, 512], F32) as ps,
        nc.sbuf_tensor("scores_wT", [D, D], F32) as wT,
        nc.semaphore("scores_turned") as turned,
        nc.semaphore("scores_copied") as copied,
        nc.semaphore("scores_made") as made,
        nc.Block() as block,
    ):
        @block.tensor
        def _(pe):
            pe.transpose(ps[0:D, 0:D], S["w3"][:, 0:D], S["ident"][0:D, 0:D]).then_inc(turned, 1)
            pe.wait_ge(copied, 1)
            pe.matmul(ps[0:D, P:P + 2], wT[:, :], S["a2"][:, :], start=True, stop=True).then_inc(made, 1)

        @block.vector
        def _(dve):
            dve.wait_ge(turned, 1)
            nc.vector.tensor_copy(wT[:, :], ps[0:D, 0:D]).then_inc(copied, 1)
            dve.wait_ge(made, 1)
            nc.vector.tensor_copy(S["w3"][:, D:D + 2], ps[0:D, P:P + 2])


def layernorm(v, dve, chain, X, work, stat, squares_summed, root_done, turn):
    mean, var = stat[:, 0, :], stat[:, 1, :]
    chain(v.tensor_reduce(mean, work, AX, ALU.add))
    chain(v.tensor_scalar(mean, mean, 1.0 / D, None, ALU.mult))
    chain(v.tensor_tensor(work, work, spread(mean, D), ALU.subtract))
    chain(v.tensor_tensor(X, work, work, ALU.mult))
    chain(v.tensor_reduce(var, X, AX, ALU.add))
    v.tensor_scalar(var, var, 1.0 / D, LN_EPS, ALU.mult, ALU.add).then_inc(squares_summed, 1)
    dve.wait_ge(root_done, turn)
    chain(v.reciprocal(var, var))
    chain(v.tensor_tensor(X, work, spread(var, D), ALU.mult))


def finish(nc, L, S, out=None):
    H, M, K = L.heads, L.msg, KN
    sums = S["node_sums"][:, 0:K * L.row].rearrange("p (k w) -> p k w", k=K)
    into = S["node_carry"][:, :, 0:L.row]
    X = S["X"][:, 0:K, :]
    nodes = S["work"]
    spans, degree = S["spans"][:, 0:K], S["degree"][:, 0:K]

    if L.name == "mlp":
        with (
            nc.semaphore("mlp_f_chain") as chain_v,
            nc.Block() as block,
        ):
            @block.vector
            def _(dve):
                chain = Chain(dve, chain_v)
                chain(nc.vector.tensor_tensor(into, into, spread(spans, D), ALU.mult))
                chain(nc.vector.tensor_tensor(nodes[:, :, :], sums, into, ALU.add))
                chain(nc.vector.tensor_tensor(into, spread(degree, D), bc(S["b2"][:, :], 1, [P, K, D]), ALU.mult))
                nc.vector.tensor_tensor(X, X, into, ALU.add)

        def evacuate(k, m, product):
            return nc.vector.tensor_tensor(nodes[:, k:k + m, :], product, S["X"][:, k:k + m, :], ALU.add)

        project(nc, "mlp_w2", S["work"], K, S["w2"][:, :], D, S, evacuate)

    ctx = ExitStack()
    with ctx:
        def sb(name, shape):
            return ctx.enter_context(nc.sbuf_tensor(f"{L.name}_f_{name}", shape, F32))

        def sem(name):
            return ctx.enter_context(nc.semaphore(f"{L.name}_f2_{name}"))

        stat = sb("stat", [P, 2, K])
        chain_v, squares_summed, root_done, stored = sem("chain"), sem("squares_summed"), sem("root_done"), sem("stored")
        if H:
            top = sb("top", [P, K, H])
            carried_top = sb("carried_top", [P, K, H])
            weight = sb("weight", [P, 2, K, H])
            shifted, weighed = sem("shifted"), sem("weighed")
        if L.name == "gatv2":
            part = sb("part", [P, D])
            mean = sb("mean", [P, D])
            scale = sb("scale", [P, D])
            ps = ctx.enter_context(nc.psum_tensor("gatv2_f_ps", [P, 512], F32))
            part_made, node_sum_made, var_made, scale_made = (sem("part_made"), sem("node_sum_made"),
                                                              sem("var_made"), sem("scale_made"))
            act_in, act_out = sem("act_in"), sem("act_out")
        if L.name == "gat":
            act_in, act_out = sem("act_in"), sem("act_out")
            neg = sb("neg", [P, K, D])
        if out is not None:
            normed = sem("normed")
        block = ctx.enter_context(nc.Block())

        @block.vector
        def _(dve):
            v = nc.vector
            chain = Chain(dve, chain_v)

            def softmax_sums():
                c = D // H
                wide = [P, K, H, c]
                v.tensor_scalar(weight[:, 0, :, 0], spans, 1.0, BIG, ALU.subtract, ALU.mult)
                chain(v.tensor_tensor(carried_top[:, :, :], into[:, :, M:L.row], spread(spans, H), ALU.mult))
                chain(v.tensor_tensor(carried_top[:, :, :], carried_top[:, :, :],
                                      weight[:, 0, :, 0:1].to_broadcast([P, K, H]), ALU.add))
                chain(v.tensor_tensor(top[:, :, :], carried_top[:, :, :], sums[:, :, M:L.row], ALU.max))
                v.tensor_tensor(weight[:, 0, :, :], sums[:, :, M:L.row], top[:, :, :], ALU.subtract)
                v.tensor_tensor(weight[:, 1, :, :], carried_top[:, :, :], top[:, :, :], ALU.subtract
                                ).then_inc(shifted, 1)
                dve.wait_ge(weighed, 1)
                for n, t in enumerate((sums, into)):
                    v.tensor_tensor(t[:, :, D:M], t[:, :, D:M], weight[:, n, :, :], ALU.mult)
                    for h in range(H):
                        last = v.tensor_tensor(t[:, :, h * c:(h + 1) * c], t[:, :, h * c:(h + 1) * c],
                                               weight[:, n, :, h:h + 1].to_broadcast([P, K, c]), ALU.mult)
                chain(last)
                v.tensor_tensor(nodes[:, :, :], sums[:, :, 0:D], into[:, :, 0:D], ALU.add)
                chain(v.tensor_tensor(top[:, :, :], sums[:, :, D:M], into[:, :, D:M], ALU.add))
                if L.name == "gatv2":
                    chain(v.tensor_scalar(top[:, :, :], top[:, :, :], 1e-16, None, ALU.add))
                chain(v.reciprocal(top[:, :, :], top[:, :, :]))
                for h in range(H):
                    last = v.tensor_tensor(nodes[:, :, h * c:(h + 1) * c], nodes[:, :, h * c:(h + 1) * c],
                                           top[:, :, h:h + 1].to_broadcast([P, K, c]), ALU.mult)
                chain(last)

            def sum_over_nodes(turn):
                src = part_of[turn - 1]
                chain(v.tensor_reduce(part[:, :], src[:, 0:K - 1, 0:D].rearrange("p k f -> p f k"), AX, ALU.add))
                v.tensor_tensor(part[0:NREST, :], part[0:NREST, :], src[0:NREST, K - 1, 0:D], ALU.add
                                ).then_inc(part_made, 1)
                dve.wait_ge(node_sum_made, turn)

            if L.name == "gatv2":
                part_of = [nodes, into]
                softmax_sums()
                chain(v.tensor_tensor(nodes[:, :, :], nodes[:, :, :], bc(S["bias"][:, :], 1, [P, K, D]), ALU.add))
                sum_over_nodes(1)
                chain(v.tensor_scalar(mean[:, :], ps[:, 0:D], 1.0 / N, None, ALU.mult))
                chain(v.tensor_tensor(nodes[:, :, :], nodes[:, :, :], bc(mean[:, :], 1, [P, K, D]), ALU.subtract))
                chain(v.tensor_tensor(into[:, :, 0:D], nodes[:, :, :], nodes[:, :, :], ALU.mult))
                sum_over_nodes(2)
                v.tensor_scalar(scale[:, :], ps[:, D:2 * D], 1.0 / N, BN_EPS, ALU.mult, ALU.add
                                ).then_inc(var_made, 1)
                dve.wait_ge(scale_made, 1)
                chain(v.reciprocal(scale[:, :], scale[:, :]))
                chain(v.tensor_tensor(scale[:, :], scale[:, :], S["gamma"][:, :], ALU.mult))
                chain(v.tensor_tensor(nodes[:, :, :], nodes[:, :, :], bc(scale[:, :], 1, [P, K, D]), ALU.mult))
                chain(v.tensor_tensor(nodes[:, :, :], nodes[:, :, :], bc(S["beta"][:, :], 1, [P, K, D]), ALU.add))
                v.tensor_tensor(nodes[:, :, :], nodes[:, :, :], X, ALU.add).then_inc(act_in, 1)
                dve.wait_ge(act_out, 1)
                chain(v.tensor_tensor(nodes[:, :, :], nodes[:, :, :], X, ALU.add))
            elif L.name == "gat":
                softmax_sums()
                v.tensor_scalar(neg[:, :, :], nodes[:, :, :], 0.0, None, ALU.min).then_inc(act_in, 1)
                chain(v.scalar_tensor_tensor(out=nodes[:, :, :], in0=nodes[:, :, :], scalar=0.0, in1=X,
                                             op0=ALU.max, op1=ALU.add))
                dve.wait_ge(act_out, 1)
                chain(v.scalar_tensor_tensor(out=nodes[:, :, :], in0=neg[:, :, :], scalar=-1.0,
                                             in1=nodes[:, :, :], op0=ALU.add, op1=ALU.add))
            elif L.name == "mean":
                chain(v.tensor_tensor(into, into, spread(spans, D), ALU.mult))
                chain(v.tensor_tensor(nodes[:, :, :], sums, into, ALU.add))
                chain(v.tensor_scalar(stat[:, 0, :], degree, 1.0, None, ALU.max))
                chain(v.reciprocal(stat[:, 0, :], stat[:, 0, :]))
                chain(v.tensor_tensor(nodes[:, :, :], nodes[:, :, :], spread(stat[:, 0, :], D), ALU.mult))
                chain(v.tensor_tensor(nodes[:, :, :], nodes[:, :, :], X, ALU.add))
            layernorm(v, dve, chain, X, nodes[:, :, :], stat, squares_summed, root_done, 1)
            if out is not None:
                dve.sem_inc(normed, 1)

        @block.scalar
        def _(act):
            if H:
                act.wait_ge(shifted, 1)
                act.activation(weight[:, :, :, :], weight[:, :, :, :], ACT.Exp).then_inc(weighed, 1)
            if L.name == "gatv2":
                act.wait_ge(var_made, 1)
                act.activation(scale[:, :], scale[:, :], ACT.Sqrt).then_inc(scale_made, 1)
                act.wait_ge(act_in, 1)
                act.activation(nodes[:, :, :], nodes[:, :, :], ACT.Gelu).then_inc(act_out, 1)
            if L.name == "gat":
                act.wait_ge(act_in, 1)
                act.activation(neg[:, :, :], neg[:, :, :], ACT.Exp).then_inc(act_out, 1)
            act.wait_ge(squares_summed, 1)
            act.activation(stat[:, 1, :], stat[:, 1, :], ACT.Sqrt).then_inc(root_done, 1)

        if L.name == "gatv2":
            @block.tensor
            def _(pe):
                for turn in range(2):
                    pe.wait_ge(part_made, turn + 1)
                    pe.matmul(ps[:, turn * D:(turn + 1) * D], S["ones"][:, :], part[:, :], start=True, stop=True
                              ).then_inc(node_sum_made, 1)

        if out is not None:
            @block.sync
            def _(sp):
                sp.wait_ge(normed, 1)
                sp.dma_start(out[0:(K - 1) * P, :].rearrange("(k p) f -> p k f", p=P), X[:, 0:K - 1, :]
                             ).then_inc(stored, 16)
                sp.dma_start(out[(K - 1) * P:N, :], X[0:NREST, K - 1, :]).then_inc(stored, 16)
                sp.wait_ge(stored, 32)


def store_nodes(nc, L, S):
    with nc.semaphore(L.name + "_table_out") as table_out, nc.Block() as block:
        @block.sync
        def _(sp):
            sp.dma_start(node_view(L.gather_table), S["X"][:, :, :]).then_inc(table_out, 16)
            sp.wait_ge(table_out, 16)


def clear_semaphores(nc, numbers):
    with nc.Block() as block:
        @block.gpsimd
        def _(pool):
            pool.sem_clear(numbers)


def build(nc, A, out, last=4):
    def dram(name, shape, dt=F32):
        return nc.dram_tensor(name, shape, dt, kind="Internal").ap()

    layers = [
        Layer("mlp", D, D, 32, 0, dram("mlp_src", [NP, D]), dram("mlp_dst", [NP, 3 * D], BF16)),
        Layer("gatv2", D, D, 16, HEADS, dram("gatv2_src", [NP, D]), dram("gatv2_dst", [NP, 3 * D], BF16)),
        Layer("gat", D + 1, 1, 0, 1, dram("gat_src", [NP, D + 1]), dram("gat_dst", [NP, 1])),
        Layer("mean", D, 0, 0, 0, dram("mean_src", [NP, D]), None),
    ]
    ctx = ExitStack()
    with ctx:
        def sb(name, shape, dt=F32):
            return ctx.enter_context(nc.sbuf_tensor(name, shape, dt))

        row = D + 2 * HEADS
        S = {
            "X": sb("X", [P, KP, D]), "work": sb("work", [P, KN, D]),
            "src_cols": sb("src_cols", [P, NTP], I32), "rel_cols": sb("rel_cols", [P, NTP]),
            "hi_cols": sb("hi_cols", [P, NTP], BF16), "lo_cols": sb("lo_cols", [P, NTP], BF16),
            "base_row": sb("base_row", [1, NTP], I32),
            "lane": sb("lane", [P, 1]), "iota": sb("iota", [P, P], BF16), "ident": sb("ident", [P, P]),
            "tri": sb("tri", [HI, HI]), "ones": sb("ones", [P, P]), "counts": sb("counts", [HI, P]),
            "through": sb("through", [D + HEADS, NT]), "carry_row": sb("carry_row", [P, RB], I32),
            "degree": sb("degree", [P, HI]), "spans": sb("spans", [P, HI]), "last_row": sb("last_row", [P, HI], I32),
            "w1": sb("w1", [D, 2 * D]), "w2": sb("w2", [D, D]), "b2": sb("b2", [P, D]), "bias0": sb("bias0", [P, 2 * D]),
            "wlr": sb("wlr", [D, 2 * D]), "bias1": sb("bias1", [P, 2 * D]), "att_bc": sb("att_bc", [P, D]),
            "bias": sb("bias", [P, D]), "gamma": sb("gamma", [P, D]), "beta": sb("beta", [P, D]),
            "w3": sb("w3", [D, D + 2]), "a2": sb("a2", [D, 2]),
            "attr_w": {32: sb("attr_w32", [P, 4 * D]), 16: sb("attr_w16", [16 * B, B * D])},
            "attr": {32: A["edge_attr_32"], 16: A["edge_attr_16"]},
            "rel_rows": dram("rel_rows", [NTP * P], BF16), "edge_rows": dram("edge_rows", [NTP, HEADS, 2 * P]),
            "first_dram": dram("first_dram", [NTP + 1], I32), "last_dram": dram("last_dram", [NTP + 1], I32),
        }
        for L in layers:
            S["T_" + L.name] = dram("sums_" + L.name, [NT * P, L.row])
            S["C_" + L.name] = dram("carry_" + L.name, [NP, L.row])
        for L in layers:
            for name in [f"gathered{q}" for q in range(Q)] + ["fetched", "scattered"]:
                S[f"{L.name}_{name}"] = ctx.enter_context(nc.semaphore(f"{L.name}_{name}"))
        numbers = range(min(nc.free_semaphores), max(nc.free_semaphores) + 1)
        prepare(nc, S, A, [S["C_" + L.name] for L in layers])
        edge_scores(nc, S)
        for n, L in enumerate(layers[:last]):
            if n:
                clear_semaphores(nc, numbers)
            if L.name == "mlp":
                tables(nc, L, S, S["w1"][:, :], 2 * D, S["bias0"][:, :])
            elif L.name == "gatv2":
                tables(nc, L, S, S["wlr"][:, :], 2 * D, S["bias1"][:, :])
            elif L.name == "gat":
                tables(nc, L, S, S["w3"][:, :], D + 2, None)
            else:
                store_nodes(nc, L, S)
            edge_pass(nc, L, S, hist=(n == 0))
            if n == 0:
                rank(nc, S)
            with (
                nc.sbuf_tensor(L.name + "_node_sums", [P, KN * L.row], F32) as node_sums,
                nc.sbuf_tensor(L.name + "_node_carry", [P, KN, L.row], F32) as node_carry,
            ):
                S["node_sums"], S["node_carry"] = node_sums, node_carry
                carry(nc, L, S)
                finish(nc, L, S, out if n == last - 1 else None)


INPUTS = ["x", "src", "dst", "edge_attr_16", "edge_attr_32", "L0_gnn_W1", "L0_gnn_b1", "L0_gnn_W2", "L0_gnn_b2",
          "L1_gnn_W_l", "L1_gnn_b_l", "L1_gnn_W_r", "L1_gnn_b_r", "L1_gnn_W_e", "L1_gnn_att", "L1_gnn_bias",
          "L1_gnn_gamma", "L1_gnn_beta", "L2_gnn_W", "L2_gnn_a"]


def kernel(**inputs):
    import concourse.bacc as bacc
    from concourse.bass_utils import run_bass_kernel_spmd

    nc = bacc.Bacc("TRN2", target_bir_lowering=False, num_devices=1)
    arrays, A = {}, {}
    for name in INPUTS:
        a = np.ascontiguousarray(inputs[name])
        arrays["in_" + name] = a
        A[name] = nc.dram_tensor("in_" + name, a.shape, mybir.dt.from_np(a.dtype), kind="ExternalInput").ap()
    out = nc.dram_tensor("out_nodes", (N, D), F32, kind="ExternalOutput").ap()
    build(nc, A, out)
    r = run_bass_kernel_spmd(nc, [arrays], core_ids=[0])
    return r.results[0]["out_nodes"]
```

```python
import numpy as np
import concourse.bass as bass
from concourse import mybir
from contextlib import ExitStack

F32 = mybir.dt.float32
BF16 = mybir.dt.bfloat16
I32 = mybir.dt.int32
ALU = mybir.AluOpType
ACT = mybir.ActivationFunctionType
AX = mybir.AxisListType.X

P = 128
N = 6250
E = 206250
D = 64
HEADS = 4
B = 7
Q = 4
NB = -(-E // (P * B))
NT = NB * B
ETILES = -(-E // P)
RB = -(-NT // P)
NTP = RB * P
EFULL, EREST = E // P, E % P
KN = -(-N // P)
KP = KN + 1
NP = KP * P
NREST = N - (KN - 1) * P
HI = -(-(N + 1) // P)
BIG = 3.0e38
LN_EPS = 1e-5
BN_EPS = 1e-5
SLOPE = 0.2
LAST_C = -(-NB // P)
SP_TILES = 4
EARLY, EARLY_SOFT = 10, 28
SG = 4


class Layer:

    def __init__(self, name, gathered, window, attr, heads, gather_table, window_table):
        self.name, self.gathered, self.window, self.attr, self.heads = name, gathered, window, attr, heads
        self.gather_table, self.window_table = gather_table, window_table
        self.msg = D + heads
        self.row = D + 2 * heads
        self.parts = 3 if window == D else 1
        self.win_dt = BF16 if self.parts == 3 else F32


class Batch:

    def __init__(self, loop, c):
        self.loop, self.c = loop, c
        self.q = c % Q
        self.n = loop * Q + c
        self.turn = loop + c // Q

    def __add__(self, d):
        return Batch(self.loop, self.c + d)

    def exists(self):
        return not isinstance(self.n, int) or 0 <= self.n < NB

    def used(self, back=0):
        return self.n + 1 - back

    def landed(self, dmas=1):
        return (self.turn + 1) * (16 * dmas)

    def tiles(self):
        return min(B, ETILES - self.n * B) if isinstance(self.n, int) else B

    def rows_landed(self):
        return self.landed_before(B) + 16 * self.tiles()

    def landed_before(self, dmas=1):
        return self.turn * (16 * dmas)


def wait(eng, sem, count):
    if not isinstance(count, int) or count > 0:
        eng.wait_ge(sem, count)


def over_batches(eng, first, step):
    start = 2 * Q
    loops = (NB - start) // Q - 1
    for n in range(first, start):
        step(Batch(0, n))
    with eng.Fori(0, loops) as it:
        for c in range(Q):
            step(Batch(it, start + c))
    for n in range(start + loops * Q, NB + 2):
        step(Batch(0, n))


def bc(ap, axis, shape):
    return ap.unsqueeze(axis).to_broadcast(shape)


def load_windows(nc, eng, L, S, win, win_in, b, tiles):
    _, bases = nc.values_load_multi_w_load_instructions(
        S["base_row"][0:1, bass.ds(b.n * B + tiles[0], len(tiles))], engines=[eng.engine], min_val=0, max_val=N,
        skip_runtime_bounds_check_because="they are destinations, which lie in 0..N")
    for j, base in zip(tiles, bases):
        eng.dma_start(win[:, b.q, j, :], L.window_table[bass.ds(base, P), :]).then_inc(win_in[b.q], 16)


def edge_pass(nc, L, S, hist):
    soft = L.heads > 0
    H = L.heads
    ax = L.attr
    groups = {0: [], 32: [(0, 4), (4, 3)], 16: [(0, 7)]}[ax]
    ctx = ExitStack()
    with ctx:
        def sb(name, shape, dt=F32):
            return ctx.enter_context(nc.sbuf_tensor(f"{L.name}_{name}", shape, dt))

        def pb(name, shape):
            return ctx.enter_context(nc.psum_tensor(f"{L.name}_{name}", shape, F32))

        def sem(name):
            return ctx.enter_context(nc.semaphore(f"{L.name}_{name}"))

        idx = sb("idx", [P, Q, B], I32)
        G = sb("G", [P, Q, B * L.gathered])
        rel = sb("rel", [P, Q, B * P], BF16)
        same = sb("same", [P, Q, B, P])
        out_rows = sb("out_rows", [P, Q, B * L.row])
        Gv = G[:].rearrange("p q (b w) -> p q b w", b=B)
        outv = out_rows[:].rearrange("p q (b w) -> p q b w", b=B)
        relv = rel[:].rearrange("p q (b e) -> p q b e", b=B)
        sums = [pb(f"sums{n}", [P, 512]) for n in range(2)]
        if L.window:
            hot = sb("hot", [P, Q, B, P], L.win_dt)
            win = sb("win", [P, Q, B, L.parts * L.window], L.win_dt)
            z = [pb(f"z{n}", [P, 512]) for n in range(2)]
            zs = sb("zs", [P, Q, B * L.window])
            act_out = sb("act_out", [P, Q, B * L.window])
        if ax:
            attr = sb("attr", [P, Q, B, ax])
            attrT = sb("attrT", [P, Q, 2, P])
            attrT_ps = pb("attrT_ps", [P, 512])
        if soft:
            logits = sb("logits", [P, Q, B * H]) if H > 1 else act_out
            edges = sb("edges", [B * H, Q, 2, P])
            runmax = sb("runmax", [B * H, P])
            segmax = sb("segmax", [B * H, Q, P])
            diff = sb("diff", [P, Q, B * H])
            msg = sb("msg", [P, Q, B, L.msg])
            lt_ps = pb("lt_ps", [P, 512])[0:B * H, 0:P]
            mb_all = pb("mb_ps", [P, 512])
            mb_ps = mb_all[:, 0:B * H]
            mb_cols = B * H + B * H % 2
        if hist:
            hot_hi = sb("hot_hi", [P, Q, B, HI], BF16)
            hot_lo = sb("hot_lo", [P, Q, B, P], BF16)
            count_ps = pb("count_ps", [P, 512])

        idx_ready = sem("idx_ready")
        gather_turn = sem("gather_turn")
        gathered = [S[f"{L.name}_gathered{q}"] for q in range(Q)]
        rel_in = [sem(f"rel_in{q}") for q in range(Q)]
        stored = [sem(f"stored{q}") for q in range(Q)]
        masks_made = sem("masks_made")
        sums_made = sem("sums_made")
        sums_copied = sem("sums_copied")
        z_added = sem("z_added")
        act_done = sem("act_done")
        if L.window:
            win_in = [sem(f"win_in{q}") for q in range(Q)]
            hot_made = sem("hot_made")
            z_made = sem("z_made")
        if ax:
            attr_in = [sem(f"attr_in{q}") for q in range(Q)]
            attr_turned = sem("attr_turned")
            attr_copied = sem("attr_copied")
        if soft:
            edges_in = [sem(f"edges_in{q}") for q in range(Q)]
            att_done = sem("att_done")
            logits_ready = sem("logits_ready")
            logits_turned = sem("logits_turned")
            prefix_done = sem("prefix_done")
            max_ready = sem("max_ready")
            max_turned = sem("max_turned")
            diff_ready = sem("diff_ready")
            weights_ready = sem("weights_ready")
            msg_ready = sem("msg_ready")
        if hist:
            hist_ready = sem("hist_ready")
            hist_used = sem("hist_used")
        lg_ready = (logits_ready if H > 1 else act_done) if soft else None
        block = ctx.enter_context(nc.Block())

        relD = S["rel_rows"]
        Tv = S["T_" + L.name].rearrange("(n p b) w -> n p (b w)", p=P, b=B)

        @block.sync
        def _(sp):
            def step(i):
                b = i + 2
                if b.exists():
                    wait(sp, masks_made, b.used(Q))
                    sp.dma_start(rel[:, b.q, :],
                                 relD[bass.ds(b.n * (B * P), B * P)].unsqueeze(0).to_broadcast([P, B * P])
                                 ).then_inc(rel_in[b.q], 16)
                    if ax:
                        wait(sp, attr_turned, b.used(Q))
                        attr_load(b)
                    if L.window:
                        wait(sp, z_made, b.used(Q))
                        load_windows(nc, sp, L, S, win, win_in, b, range(0, SP_TILES))
                o = i + (-2)
                if o.exists():
                    wait(sp, sums_copied, o.used())
                    sp.dma_start(Tv[bass.ds(o.n, 1), :, :].rearrange("a p w -> p (a w)"),
                                 out_rows[:, o.q, :]).then_inc(stored[o.q], 16)
                if soft and b.exists():
                    wait(sp, max_ready, b.used(Q))
                    src = S["edge_rows"][bass.ds(b.n * B, B), 0:H, :].rearrange("b h x -> (b h) x")
                    sp.dma_start(edges[:, b.q, :, :].rearrange("r a e -> r (a e)"), src
                                 ).then_inc(edges_in[b.q], 16)

            def attr_load(b):
                A = S["attr"][ax]
                n0 = b.n * B
                if isinstance(n0, int) and n0 + B > EFULL:
                    whole = max(0, EFULL - n0)
                    if whole:
                        sp.dma_start(attr[:, b.q, 0:whole, :],
                                     A[n0 * P:(n0 + whole) * P, :].rearrange("(b p) f -> p b f", p=P)
                                     ).then_inc(attr_in[b.q], 16)
                    if n0 <= EFULL:
                        sp.dma_start(attr[0:EREST, b.q, whole, :], A[EFULL * P:E, :]).then_inc(attr_in[b.q], 16)
                else:
                    sp.dma_start(attr[:, b.q, :, :],
                                 A[bass.ds(b.n * (B * P), B * P), :].rearrange("(b p) f -> p b f", p=P)
                                 ).then_inc(attr_in[b.q], 16)

            over_batches(sp, -2, step)
            for n in range(NB - Q, NB):
                sp.wait_ge(stored[n % Q], Batch(0, n).landed())

        @block.gpsimd
        def _(pool):
            freed = {"mlp": z_added, "gatv2": None, "gat": None, "mean": sums_made}[L.name]
            freed = freed or msg_ready

            def step(b):
                if not b.exists():
                    return
                wait(pool, idx_ready, b.used())
                wait(pool, freed, b.used(Q))
                pool.sem_inc(gather_turn, 1)
                for j in range(b.tiles()):
                    pool.indirect_dma_start(
                        out=G[:, b.q, j * L.gathered:(j + 1) * L.gathered], out_offset=None,
                        in_=L.gather_table, in_offset=bass.IndirectOffsetOnAxis(ap=idx[:, b.q, j:j + 1], axis=0)
                    ).then_inc(gathered[b.q], 16)

            over_batches(pool, 0, step)

        @block.vector
        def _(dve):
            def one_hots(b):
                wait(dve, rel_in[b.q], b.landed())
                wait(dve, z_made, b.used(Q))
                nc.vector.tensor_scalar(hot[:, b.q, :, :], relv[:, b.q, :, :], S["lane"][:, 0:1], None,
                                        ALU.is_equal).then_inc(hot_made, 1)

            def same_destination(b):
                wait(dve, rel_in[b.q], b.landed())
                wait(dve, sums_made, b.used(Q))
                nc.vector.tensor_tensor(same[:, b.q, :, :], relv[:, b.q, :, :],
                                        bc(S["rel_cols"][:, bass.ds(b.n * B, B)], 2, [P, B, P]),
                                        ALU.is_equal).then_inc(masks_made, 1)

            def indices(b):
                nc.vector.tensor_copy(idx[:, b.q, :], S["src_cols"][:, bass.ds(b.n * B, B)]).then_inc(idx_ready, 1)

            def add_gathered(b):
                wait(dve, gathered[b.q], b.rows_landed())
                wait(dve, z_made, b.used())
                if not soft:
                    wait(dve, act_done, b.used(Q))
                w = L.window
                nc.vector.tensor_tensor(zs[:, b.q, :].rearrange("p (b w) -> p b w", w=w),
                                        z[b.q % 2][:, 0:B * w].rearrange("p (b w) -> p b w", w=w),
                                        Gv[:, b.q, :, L.gathered - w:L.gathered], ALU.add).then_inc(z_added, 1)
                if soft:
                    wait(dve, z_added, b.used())
                    nc.vector.scalar_tensor_tensor(out=act_out[:, b.q, :], in0=zs[:, b.q, :], scalar=SLOPE,
                                                   in1=zs[:, b.q, :], op0=ALU.mult, op1=ALU.max
                                                   ).then_inc(act_done, 1)

            def prefix(b):
                wait(dve, logits_turned, b.used())
                wait(dve, edges_in[b.q], b.landed())
                nc.vector.tensor_tensor_scan(runmax[:, :], edges[:, b.q, 0, :], lt_ps, 0.0, ALU.add, ALU.max
                                             ).then_inc(prefix_done, 1)
                wait(dve, prefix_done, b.used())
                wait(dve, max_turned, b.used(Q))
                nc.vector.tensor_tensor_scan(segmax[:, b.q, ::-1], edges[:, b.q, 1, ::-1], runmax[:, ::-1],
                                             0.0, ALU.add, ALU.max).then_inc(max_ready, 1)

            def heads_dot(b):
                wait(dve, act_done, b.used())
                g4 = act_out[:, b.q, :].rearrange("p (b w) -> p b w", b=B)
                nc.vector.tensor_tensor(zs[:, b.q, :].rearrange("p (b w) -> p b w", b=B), g4,
                                        bc(S["att_bc"][:, :], 1, [P, B, D]), ALU.mult).then_inc(att_done, 1)
                wait(dve, att_done, b.used())
                nc.vector.tensor_reduce(logits[:, b.q, :],
                                        zs[:, b.q, :].rearrange("p (r c) -> p r c", c=D // H), AX, ALU.add
                                        ).then_inc(logits_ready, 1)

            def subtract_max(b):
                wait(dve, max_turned, b.used())
                wait(dve, weights_ready, b.used(Q))
                nc.vector.tensor_tensor(diff[:, b.q, :], logits[:, b.q, :], mb_ps, ALU.subtract
                                        ).then_inc(diff_ready, 1)

            def weigh(b):
                wait(dve, weights_ready, b.used())
                c = D // H
                nc.vector.tensor_tensor(
                    msg[:, b.q, :, 0:D].rearrange("p b (h c) -> p b h c", c=c),
                    Gv[:, b.q, :, 0:D].rearrange("p b (h c) -> p b h c", c=c),
                    bc(msg[:, b.q, :, D:D + H], 3, [P, B, H, c]), ALU.mult).then_inc(msg_ready, 1)

            def count(b):
                wait(dve, hist_used, b.used(Q))
                nc.vector.tensor_tensor(hot_hi[:, b.q, :, :], bc(S["iota"][:, 0:HI], 1, [P, B, HI]),
                                        bc(S["hi_cols"][:, bass.ds(b.n * B, B)], 2, [P, B, HI]), ALU.is_equal)
                nc.vector.tensor_tensor(hot_lo[:, b.q, :, :], bc(S["iota"][:, :], 1, [P, B, P]),
                                        bc(S["lo_cols"][:, bass.ds(b.n * B, B)], 2, [P, B, P]), ALU.is_equal
                                        ).then_inc(hist_ready, 1)

            def step(i):
                if L.window and (i + 1).exists():
                    one_hots(i + 1)
                if i.exists():
                    if L.window:
                        add_gathered(i)
                    else:
                        wait(dve, gathered[i.q], i.rows_landed())
                if (i + 3).exists():
                    indices(i + 3)
                if soft:
                    p = i + (-1)
                    if p.exists():
                        prefix(p)
                    if i.exists() and H > 1:
                        heads_dot(i)
                    if p.exists():
                        subtract_max(p)
                    if i.exists():
                        same_destination(i)
                    if p.exists():
                        weigh(p)
                elif i.exists():
                    same_destination(i)
                if hist and i.exists():
                    count(i)

            for n in range(2):
                indices(Batch(0, n))
            over_batches(dve, -1, step)
            if hist:
                dve.wait_ge(hist_used, NB)
                nc.vector.tensor_copy(S["counts"][:, :], count_ps[0:HI, 0:P])

        @block.scalar
        def _(act):
            def copy_sums(b):
                wait(act, sums_made, b.used())
                wait(act, stored[b.q], b.landed_before())
                act.activation(outv[:, b.q, :, 0:L.msg],
                               sums[b.q % 2][:, 0:B * L.msg].rearrange("p (b w) -> p b w", b=B), ACT.Copy
                               ).then_inc(sums_copied, 1)

            def copy_attr(b):
                wait(act, attr_turned, b.used())
                wait(act, z_made, b.used(Q))
                for g, (t0, nt) in enumerate(groups):
                    last = act.activation(attrT[0:nt * ax, b.q, g, :], attrT_ps[0:nt * ax, g * P:(g + 1) * P],
                                          ACT.Copy)
                last.then_inc(attr_copied, 1)

            def nonlinear(b):
                wait(act, z_added, b.used())
                wait(act, sums_made, b.used(Q))
                act.activation(act_out[:, b.q, :], zs[:, b.q, :], ACT.Relu).then_inc(act_done, 1)

            def exponentiate(b):
                wait(act, diff_ready, b.used())
                wait(act, sums_made, b.used(Q))
                wait(act, stored[b.q], b.landed_before())
                act.activation(outv[:, b.q, :, L.msg:L.row],
                               mb_ps.rearrange("p (b h) -> p b h", h=H), ACT.Copy)
                act.activation(msg[:, b.q, :, D:D + H],
                               diff[:, b.q, :].rearrange("p (b h) -> p b h", h=H), ACT.Exp
                               ).then_inc(weights_ready, 1)

            def step(i):
                if (i + (-2)).exists():
                    copy_sums(i + (-2))
                if ax and (i + 1).exists():
                    copy_attr(i + 1)
                if L.window and not soft and i.exists():
                    nonlinear(i)
                w = i + 2
                if L.window and w.exists():
                    wait(act, z_made, w.used(Q))
                    load_windows(nc, act, L, S, win, win_in, w, range(SP_TILES, B))
                if soft and (i + (-1)).exists():
                    exponentiate(i + (-1))

            over_batches(act, -2, step)

        @block.tensor
        def _(pe):
            ident = S["ident"]

            def turn_attr(b):
                n0 = b.n * B
                partial = isinstance(n0, int) and n0 + B > EFULL
                dmas = (1 if EFULL > n0 else 0) + (1 if n0 <= EFULL else 0) if partial else 1
                wait(pe, attr_in[b.q], b.landed_before() + 16 * dmas if partial else b.landed())
                wait(pe, attr_copied, b.used(1))
                for g, (t0, nt) in enumerate(groups):
                    last = pe.transpose(attrT_ps[0:nt * ax, g * P:(g + 1) * P],
                                        attr[:, b.q, t0:t0 + nt, :].rearrange("p b f -> p (b f)"), ident[:, :])
                last.then_inc(attr_turned, 1)

            def make_z(b):
                wait(pe, hot_made, b.used())
                wait(pe, win_in[b.q], b.landed(B))
                wait(pe, z_added, b.used(2))
                w = L.window
                if ax:
                    wait(pe, attr_copied, b.used())
                for t0, nt in groups or [(0, B)]:
                    if ax:
                        g = groups.index((t0, nt))
                        pe.matmul(z[b.q % 2][:, t0 * w:(t0 + nt) * w], attrT[0:nt * ax, b.q, g, :],
                                  S["attr_w"][ax][0:nt * ax, 0:nt * w], start=True, stop=True)
                    for j in range(t0, t0 + nt):
                        for part in range(L.parts):
                            last = pe.matmul(z[b.q % 2][:, j * w:(j + 1) * w], hot[:, b.q, j, :],
                                             win[:, b.q, j, part * w:(part + 1) * w],
                                             start=not ax and part == 0, stop=True, skip_group_check=True)
                last.then_inc(z_made, 1)

            def turn_max(b):
                wait(pe, max_ready, b.used())
                wait(pe, diff_ready, b.used(1))
                wait(pe, weights_ready, b.used(1))
                pe.matmul(mb_all[:, 0:mb_cols], segmax[:, b.q, :], ident[0:B * H, 0:mb_cols], start=True, stop=True
                          ).then_inc(max_turned, 1)

            def turn_logits(b):
                wait(pe, lg_ready, b.used())
                wait(pe, max_ready, b.used(1))
                pe.transpose(lt_ps, logits[:, b.q, :], ident[:, :]).then_inc(logits_turned, 1)

            def make_sums(b):
                wait(pe, masks_made, b.used())
                if soft:
                    wait(pe, msg_ready, b.used())
                elif L.window:
                    wait(pe, act_done, b.used())
                else:
                    wait(pe, gathered[b.q], b.rows_landed())
                wait(pe, sums_copied, b.used(2))
                for j in range(B):
                    if soft:
                        rhs = msg[:, b.q, j, :]
                    elif L.window:
                        rhs = act_out[:, b.q, j * D:(j + 1) * D]
                    else:
                        rhs = Gv[:, b.q, j, :]
                    last = pe.matmul(sums[b.q % 2][:, j * L.msg:(j + 1) * L.msg], same[:, b.q, j, :], rhs,
                                     start=True, stop=True)
                last.then_inc(sums_made, 1)

            def add_counts(b):
                wait(pe, hist_ready, b.used())
                for j in range(B):
                    first = isinstance(b.n, int) and b.n == 0 and j == 0
                    final = isinstance(b.n, int) and b.n == NB - 1 and j == B - 1
                    last = pe.matmul(count_ps[0:HI, 0:P], hot_hi[:, b.q, j, :], hot_lo[:, b.q, j, :],
                                     start=first, stop=final, skip_group_check=True)
                last.then_inc(hist_used, 1)

            def step(i):
                p = i + (-1)
                if ax and (i + 1).exists():
                    turn_attr(i + 1)
                if soft and p.exists():
                    turn_max(p)
                if L.window and (i + 1).exists():
                    make_z(i + 1)
                if soft and i.exists():
                    turn_logits(i)
                if p.exists():
                    make_sums(p)
                if hist and p.exists():
                    add_counts(p)

            over_batches(pe, -1, step)


class Chain:

    def __init__(self, eng, sem):
        self.eng, self.sem, self.count = eng, sem, 0

    def __call__(self, instruction):
        instruction.then_inc(self.sem, 1)
        self.count += 1
        self.eng.wait_ge(self.sem, self.count)


def prepare(nc, S, A, zero_fill):
    W = RB * P
    ctx = ExitStack()
    with ctx:
        def sb(name, shape, dt=F32):
            return ctx.enter_context(nc.sbuf_tensor("prep_" + name, shape, dt))

        def sem(name):
            return ctx.enter_context(nc.semaphore("prep_" + name))

        rows = {k: sb(k + "_rows", [P, RB, P], I32) for k in ("src", "dst")}
        f = {k: sb(k + "_f", [P, RB, P]) for k in ("src", "dst", "rel", "hi", "lo")}
        hi_int = sb("hi_int", [P, RB, P], I32)
        rel_bf = sb("rel_bf", [P, RB, P], BF16)
        masks = sb("masks", [P, RB, 2, P])
        next_first = sb("next_first", [P, RB], I32)
        last_before = sb("last_before", [P, RB], I32)
        ends = sb("ends", [P, RB])
        starts = sb("starts", [P, RB])
        one_int = sb("one_int", [1, 2], I32)
        zeros = sb("zeros", [P, KP * (D + 2 * HEADS)])
        last_a = sb("last_a", [D + HEADS, NT], I32)
        last_b = sb("last_b", [D + HEADS, NT], I32)
        iota_i = sb("iota_i", [P, P], I32)
        lane_i = sb("lane_i", [P, 1], I32)
        turned = [ctx.enter_context(nc.psum_tensor(f"prep_turned{n}", [P, SG * P], F32)) for n in range(2)]
        cleared = sem("cleared")
        chain_v = sem("chain_v")
        chain_g = sem("chain_g")
        edges_in = sem("edges_in")
        params_in = sem("params_in")
        ident_made = sem("ident_made")
        weights_cleared = sem("weights_cleared")
        rows_made = sem("rows_made")
        rows_out = sem("rows_out")
        back_in = sem("back_in")
        turned_made = sem("turned_made")
        turned_used = sem("turned_used")
        zeros_made = sem("zeros_made")
        zeros_out = sem("zeros_out")
        block = ctx.enter_context(nc.Block())
        full_r, full_q = EFULL // P, EFULL % P
        jobs = [(k, r) for k in ("src", "rel", "hi", "lo") for r in range(0, RB, SG)]
        cols = {"src": S["src_cols"], "rel": S["rel_cols"], "hi": S["hi_cols"], "lo": S["lo_cols"]}

        @block.sync
        def _(sp):
            sp.wait_ge(cleared, 1)
            loads = 0
            for k in ("dst", "src"):
                e = A[k]
                sp.dma_start(rows[k][:, 0:full_r, :], e[0:full_r * P * P].rearrange("(r q e) -> q r e", q=P, e=P)
                             ).then_inc(edges_in, 16)
                sp.dma_start(rows[k][0:full_q, full_r, :],
                             e[full_r * P * P:EFULL * P].rearrange("(q e) -> q e", e=P)).then_inc(edges_in, 16)
                sp.dma_start(rows[k][full_q:full_q + 1, full_r, 0:EREST], e[EFULL * P:E].unsqueeze(0)
                             ).then_inc(edges_in, 16)
            X = S["X"]
            params = [
                (X[:, 0:KN - 1, :], A["x"][0:(KN - 1) * P, :].rearrange("(k p) f -> p k f", p=P)),
                (X[0:NREST, KN - 1, :], A["x"][(KN - 1) * P:N, :]),
                (S["w1"][:, 0:D], A["L0_gnn_W1"][0:D, :]),
                (S["w1"][:, D:2 * D], A["L0_gnn_W1"][D:2 * D, :]),
                (S["w2"][:, :], A["L0_gnn_W2"]),
                (S["bias0"][:, D:2 * D], A["L0_gnn_b1"].unsqueeze(0).to_broadcast([P, D])),
                (S["b2"][:, :], A["L0_gnn_b2"].unsqueeze(0).to_broadcast([P, D])),
                (S["wlr"][:, 0:D], A["L1_gnn_W_l"]),
                (S["wlr"][:, D:2 * D], A["L1_gnn_W_r"]),
                (S["bias1"][:, 0:D], A["L1_gnn_b_l"].unsqueeze(0).to_broadcast([P, D])),
                (S["bias1"][:, D:2 * D], A["L1_gnn_b_r"].unsqueeze(0).to_broadcast([P, D])),
                (S["att_bc"][:, :], A["L1_gnn_att"].rearrange("h c -> (h c)").unsqueeze(0).to_broadcast([P, D])),
                (S["bias"][:, :], A["L1_gnn_bias"].unsqueeze(0).to_broadcast([P, D])),
                (S["gamma"][:, :], A["L1_gnn_gamma"].unsqueeze(0).to_broadcast([P, D])),
                (S["beta"][:, :], A["L1_gnn_beta"].unsqueeze(0).to_broadcast([P, D])),
                (S["w3"][:, 0:D], A["L2_gnn_W"]),
            ]
            sp.wait_ge(weights_cleared, 1)
            for dst, src in params:
                sp.dma_start(dst, src).then_inc(params_in, 16)
            with nc.allow_non_contiguous_dma(reason="the two halves of a, once"):
                sp.dma_start(S["a2"][:, :], A["L2_gnn_a"].rearrange("(s f) -> f s", s=2)).then_inc(params_in, 16)
            n = len(params) + 1
            for width, tiles, w in ((32, 4, A["L0_gnn_W1"][2 * D:2 * D + 32, :]), (16, B, A["L1_gnn_W_e"])):
                for j in range(tiles):
                    sp.dma_start(S["attr_w"][width][j * width:(j + 1) * width, j * D:(j + 1) * D], w
                                 ).then_inc(params_in, 16)
                n += tiles
            sp.wait_ge(zeros_made, 1)
            for t in zero_fill:
                w = t.shape[1]
                sp.dma_start(t.rearrange("(p k) w -> p (k w)", p=P), zeros[:, 0:KP * w]).then_inc(zeros_out, 16)
            sp.wait_ge(rows_made, 1)
            view = S["rel_rows"].rearrange("(r q e) -> q r e", q=P, e=P)
            sp.dma_start(view, rel_bf[:, :, :]).then_inc(rows_out, 16)
            for h in range(HEADS):
                sp.dma_start(S["edge_rows"][:, h, :].rearrange("(r q) x -> q r x", q=P),
                             masks[:, :, :, :].rearrange("p r a e -> p r (a e)")).then_inc(rows_out, 16)
            with nc.allow_non_contiguous_dma(reason="one number per tile, once"):
                sp.dma_start(S["first_dram"][0:NTP].rearrange("(r q) -> q r", q=P), rows["dst"][:, :, 0]
                             ).then_inc(rows_out, 16)
                sp.dma_start(S["last_dram"][1:NTP + 1].rearrange("(r q) -> q r", q=P), rows["dst"][:, :, P - 1]
                             ).then_inc(rows_out, 16)
            sp.dma_start(S["first_dram"][NTP:NTP + 1].unsqueeze(0), one_int[0:1, 0:1]).then_inc(rows_out, 16)
            sp.dma_start(S["last_dram"][0:1].unsqueeze(0), one_int[0:1, 1:2]).then_inc(rows_out, 16)
            sp.wait_ge(rows_out, 16 * (5 + HEADS))
            sp.dma_start(S["base_row"][0:1, :], S["first_dram"][0:NTP].unsqueeze(0)).then_inc(back_in, 16)
            with nc.allow_non_contiguous_dma(reason="one number per tile, once"):
                sp.dma_start(next_first[:, :], S["first_dram"][1:NTP + 1].rearrange("(r q) -> q r", q=P)
                             ).then_inc(back_in, 16)
                sp.dma_start(last_before[:, :], S["last_dram"][0:NTP].rearrange("(r q) -> q r", q=P)
                             ).then_inc(back_in, 16)
            for dst, o in ((last_a, 0), (last_b, 1)):
                sp.dma_start(dst[:, :], S["last_dram"][o:o + NT].unsqueeze(0).to_broadcast([D + HEADS, NT])
                             ).then_inc(back_in, 16)
            sp.wait_ge(params_in, 16 * n)
            sp.wait_ge(zeros_out, 16 * len(zero_fill))
            sp.wait_ge(back_in, 80)

        @block.gpsimd
        def _(pool):
            pool.memset(rows["dst"][:, RB - 1, :], N)
            pool.memset(rows["src"][:, RB - 1, :], 0).then_inc(cleared, 1)
            pool.memset(S["X"][:, KN - 1:KP, :], 0.0)
            pool.memset(S["bias0"][:, 0:D], 0.0)
            pool.memset(S["attr_w"][32][:, :], 0.0)
            pool.memset(S["attr_w"][16][:, :], 0.0).then_inc(weights_cleared, 1)
            pool.memset(zeros[:, :], 0.0)
            pool.memset(one_int[0:1, 0:1], N)
            pool.memset(one_int[0:1, 1:2], -1).then_inc(zeros_made, 1)
            chain = Chain(pool, chain_g)
            chain(pool.memset(S["ident"][:, :], 0.0))
            chain(pool.affine_select(out=S["ident"][:, :], in_=S["ident"][:, :], compare_op=ALU.not_equal, fill=1.0,
                                     base=0, pattern=[[-1, P]], channel_multiplier=1))
            chain(pool.memset(S["tri"][:, :], 1.0))
            chain(pool.affine_select(out=S["tri"][:, :], in_=S["tri"][:, :], compare_op=ALU.is_gt, fill=0.0,
                                     base=0, pattern=[[1, HI]], channel_multiplier=-1))
            pool.memset(S["ones"][:, :], 1.0)
            pool.iota(iota_i[:, :], pattern=[[1, P]], base=0, channel_multiplier=0)
            pool.iota(lane_i[:, :], pattern=[[1, 1]], base=0, channel_multiplier=1).then_inc(ident_made, 1)

        @block.vector
        def _(dve):
            v = nc.vector
            chain = Chain(dve, chain_v)
            dve.wait_ge(edges_in, 16 * 6)
            v.tensor_copy(f["src"][:, :, :], rows["src"][:, :, :])
            chain(v.tensor_copy(f["dst"][:, :, :], rows["dst"][:, :, :]))
            v.tensor_tensor(f["rel"][:, :, :], f["dst"][:, :, :], f["dst"][:, :, 0:1].to_broadcast([P, RB, P]),
                            ALU.subtract)
            chain(v.tensor_scalar(hi_int[:, :, :], f["dst"][:, :, :], 1.0 / P, 127.0 / 256.0, ALU.mult,
                                  ALU.subtract))
            v.tensor_copy(rel_bf[:, :, :], f["rel"][:, :, :])
            v.memset(masks[:, :, :, :], 0.0)
            chain(v.tensor_copy(f["hi"][:, :, :], hi_int[:, :, :]))
            v.scalar_tensor_tensor(out=f["lo"][:, :, :], in0=f["hi"][:, :, :], scalar=-float(P),
                                   in1=f["dst"][:, :, :], op0=ALU.mult, op1=ALU.add)
            v.tensor_tensor(masks[:, :, 0, 1:P], f["rel"][:, :, 1:P], f["rel"][:, :, 0:P - 1], ALU.is_equal)
            chain(v.tensor_tensor(masks[:, :, 1, 0:P - 1], f["rel"][:, :, 1:P], f["rel"][:, :, 0:P - 1],
                                  ALU.is_equal))
            v.tensor_scalar(masks[:, :, :, :].rearrange("p r a e -> p (r a e)"),
                            masks[:, :, :, :].rearrange("p r a e -> p (r a e)"), 1.0, BIG, ALU.subtract,
                            ALU.mult).then_inc(rows_made, 1)
            dve.wait_ge(ident_made, 1)
            v.tensor_copy(S["iota"][:, :], iota_i[:, :])
            v.tensor_copy(S["lane"][:, :], lane_i[:, :])
            for n, (k, r) in enumerate(jobs):
                m = min(SG, RB - r)
                dve.wait_ge(turned_made, n + 1)
                v.tensor_copy(cols[k][:, r * P:(r + m) * P], turned[n % 2][:, 0:m * P]).then_inc(turned_used, 1)
            dve.wait_ge(back_in, 80)
            v.tensor_tensor(starts[:, :], last_before[:, :], rows["dst"][:, :, 0], ALU.not_equal)
            chain(v.tensor_tensor(ends[:, :], next_first[:, :], rows["dst"][:, :, 0], ALU.is_equal))
            chain(v.tensor_tensor(ends[:, :], ends[:, :], starts[:, :], ALU.max))
            v.scalar_tensor_tensor(out=S["carry_row"][:, :], in0=ends[:, :], scalar=float(1 << 20),
                                   in1=rows["dst"][:, :, 0], op0=ALU.mult, op1=ALU.add)
            v.tensor_tensor(S["through"][:, :], last_a[:, :], last_b[:, :], ALU.is_equal)

        @block.tensor
        def _(pe):
            pe.wait_ge(ident_made, 1)
            pe.wait_ge(rows_made, 1)
            for n, (k, r) in enumerate(jobs):
                m = min(SG, RB - r)
                wait(pe, turned_used, n - 1)
                for j in range(m):
                    last = pe.transpose(turned[n % 2][:, j * P:(j + 1) * P], f[k][:, r + j, :], S["ident"][:, :])
                last.then_inc(turned_made, 1)


class Rank:

    def __init__(self, nc, ctx, S):
        def sb(name, shape, dt=F32):
            return ctx.enter_context(nc.sbuf_tensor("rank_" + name, shape, dt))

        def sem(name):
            return ctx.enter_context(nc.semaphore("rank_" + name))

        self.nc, self.S = nc, S
        self.ones, self.upto, self.before = sb("ones", [HI, P]), sb("upto", [HI, P]), sb("before", [HI, 1])
        self.last, self.first, self.whole = sb("last", [P, HI]), sb("first", [P, HI]), sb("whole", [P, HI], I32)
        self.tile_l, self.tile_f, self.batch = sb("tile_l", [P, HI]), sb("tile_f", [P, HI]), sb("batch", [P, HI])
        self.ps = ctx.enter_context(nc.psum_tensor("rank_ps", [P, 512], F32))
        self.scanned, self.summed, self.added, self.turned = sem("scanned"), sem("summed"), sem("added"), sem("turned")

    def on_vector(self, dve, chain, ranked):
        v, S = self.nc.vector, self.S
        chain(v.memset(self.ones[:, :], 1.0))
        v.tensor_tensor_scan(self.upto[:, :], self.ones[:, :], S["counts"][:, :], 0.0, ALU.mult, ALU.add
                             ).then_inc(self.scanned, 1)
        dve.wait_ge(self.summed, 1)
        chain(v.tensor_copy(self.before[:, :], self.ps[0:HI, 0:1]))
        v.tensor_scalar(self.upto[:, :], self.upto[:, :], self.before[:, 0:1], None, ALU.add).then_inc(self.added, 1)
        dve.wait_ge(self.turned, 1)
        v.tensor_copy(S["degree"][:, :], self.ps[:, P:P + HI])
        chain(v.tensor_scalar(self.last[:, :], self.ps[:, 2 * P:2 * P + HI], 1.0, None, ALU.subtract))
        chain(v.tensor_tensor(self.first[:, :], self.last[:, :], S["degree"][:, :], ALU.subtract))
        chain(v.tensor_scalar(self.first[:, :], self.first[:, :], 1.0, None, ALU.add))
        for e, t in ((self.first, self.tile_f), (self.last, self.tile_l)):
            chain(v.tensor_scalar(self.whole[:, :], e[:, :], 1.0 / P, 127.0 / 256.0, ALU.mult, ALU.subtract))
            chain(v.tensor_copy(t[:, :], self.whole[:, :]))
        v.tensor_tensor(S["spans"][:, :], self.tile_l[:, :], self.tile_f[:, :], ALU.is_gt)
        chain(v.tensor_scalar(self.whole[:, :], self.tile_l[:, :], 1.0 / B, 3.0 / B, ALU.mult, ALU.subtract))
        chain(v.tensor_copy(self.batch[:, :], self.whole[:, :]))
        chain(v.scalar_tensor_tensor(out=self.last[:, :], in0=self.tile_l[:, :], scalar=-float(P), in1=self.last[:, :],
                                     op0=ALU.mult, op1=ALU.add))
        chain(v.scalar_tensor_tensor(out=self.last[:, :], in0=self.last[:, :], scalar=float(B), in1=self.tile_l[:, :],
                                     op0=ALU.mult, op1=ALU.add))
        v.scalar_tensor_tensor(out=S["last_row"][:, :], in0=self.batch[:, :], scalar=float(P * B - B),
                               in1=self.last[:, :], op0=ALU.mult, op1=ALU.add).then_inc(ranked, 1)

    def on_tensor(self, pe):
        ps, S, upto = self.ps, self.S, self.upto
        pe.wait_ge(self.scanned, 1)
        pe.matmul(ps[0:HI, 0:1], S["tri"][:, :], upto[:, P - 1:P], start=True, stop=True).then_inc(self.summed, 1)
        pe.wait_ge(self.added, 1)
        pe.transpose(ps[:, P:P + HI], S["counts"][:, :], S["ident"][0:HI, 0:HI])
        pe.transpose(ps[:, 2 * P:2 * P + HI], upto[:, :], S["ident"][0:HI, 0:HI]).then_inc(self.turned, 1)


def edge_scores(nc, S):
    with (
        nc.psum_tensor("scores_ps", [P, 512], F32) as ps,
        nc.sbuf_tensor("scores_wT", [D, D], F32) as wT,
        nc.semaphore("scores_turned") as turned,
        nc.semaphore("scores_copied") as copied,
        nc.semaphore("scores_made") as made,
        nc.Block() as block,
    ):
        @block.tensor
        def _(pe):
            pe.transpose(ps[0:D, 0:D], S["w3"][:, 0:D], S["ident"][0:D, 0:D]).then_inc(turned, 1)
            pe.wait_ge(copied, 1)
            pe.matmul(ps[0:D, P:P + 2], wT[:, :], S["a2"][:, :], start=True, stop=True).then_inc(made, 1)

        @block.vector
        def _(dve):
            dve.wait_ge(turned, 1)
            nc.vector.tensor_copy(wT[:, :], ps[0:D, 0:D]).then_inc(copied, 1)
            dve.wait_ge(made, 1)
            nc.vector.tensor_copy(S["w3"][:, D:D + 2], ps[0:D, P:P + 2])


class Projection:

    def __init__(self, nc, ctx, name, S, jobs):
        self.nc, self.S, self.jobs = nc, S, jobs
        self.turned = [ctx.enter_context(nc.psum_tensor(f"{name}_turned{n}", [D, SG * P], F32)) for n in range(2)]
        self.out = [ctx.enter_context(nc.psum_tensor(f"{name}_out{n}", [P, 512], F32)) for n in range(2)]
        self.lhsT = ctx.enter_context(nc.sbuf_tensor(name + "_lhsT", [D, 2, SG * P], F32))
        self.turned_made = ctx.enter_context(nc.semaphore(name + "_turned_made"))
        self.turned_copied = ctx.enter_context(nc.semaphore(name + "_turned_copied"))
        self.product_made = ctx.enter_context(nc.semaphore(name + "_product_made"))
        self.product_used = ctx.enter_context(nc.semaphore(name + "_product_used"))

    def on_tensor(self, pe, numbers):
        for n in numbers:
            _, k, m, source, _, _ = self.jobs[n]
            wait(pe, self.turned_copied, n - 1)
            for j in range(m):
                last = pe.transpose(self.turned[n % 2][:, j * P:(j + 1) * P], source[:, k + j, :],
                                    self.S["ident"][:, :])
            last.then_inc(self.turned_made, 1)
        for n in numbers:
            _, k, m, _, weights, cols = self.jobs[n]
            pe.wait_ge(self.turned_copied, n + 1)
            wait(pe, self.product_used, n - 1)
            for j in range(m):
                last = pe.matmul(self.out[n % 2][:, j * cols:(j + 1) * cols], self.lhsT[:, n % 2, j * P:(j + 1) * P],
                                 weights, start=True, stop=True)
            last.then_inc(self.product_made, 1)

    def on_scalar(self, act, numbers):
        for n in numbers:
            m = self.jobs[n][2]
            act.wait_ge(self.turned_made, n + 1)
            wait(act, self.product_made, n - 1)
            act.activation(self.lhsT[:, n % 2, 0:m * P], self.turned[n % 2][:, 0:m * P], ACT.Copy
                           ).then_inc(self.turned_copied, 1)

    def on_vector(self, dve, numbers, evacuate):
        for n in numbers:
            _, k, m, _, _, cols = self.jobs[n]
            dve.wait_ge(self.product_made, n + 1)
            evacuate(k, m, self.out[n % 2][:, 0:m * cols].rearrange("p (k w) -> p k w", k=m)
                     ).then_inc(self.product_used, 1)

    def numbers(self, kind, chunk):
        return [n for n, j in enumerate(self.jobs) if j[0] == (kind, chunk)]


CHUNK = 2 * SG
CHUNKS = [(k, min(CHUNK, KP - k)) for k in range(0, KP, CHUNK)]
NCH = len(CHUNKS)


def table_jobs(L, S, c):
    k0, m0 = CHUNKS[c]
    return [(("table", c), k, min(SG, k0 + m0 - k), S["X"], L.weights, L.cols) for k in range(k0, k0 + m0, SG)]


class Tables:

    def __init__(self, nc, ctx, L, S, projection):
        self.nc, self.L, self.S, self.projection = nc, L, S, projection
        n = L.name
        self.table = ctx.enter_context(nc.sbuf_tensor(n + "_table", [P, 2, CHUNK, L.cols], F32))
        self.filled = ctx.enter_context(nc.semaphore(n + "_filled"))
        self.stored = [ctx.enter_context(nc.semaphore(f"{n}_table_out{q}")) for q in range(2)]
        self.stores = 2
        if L.parts == 3:
            self.parts = ctx.enter_context(nc.sbuf_tensor(n + "_parts", [P, 2, CHUNK, 3 * L.window], BF16))
            self.rounded = ctx.enter_context(nc.semaphore(n + "_rounded"))
            self.left = ctx.enter_context(nc.semaphore(n + "_left"))

    def on_vector(self, dve, c):
        v, L, q = self.nc.vector, self.L, c % 2
        k0, m0 = CHUNKS[c]

        def evacuate(k, m, product):
            out = self.table[:, q, k - k0:k - k0 + m, :]
            if L.bias is None:
                return v.tensor_copy(out, product)
            return v.tensor_tensor(out, product, bc(L.bias, 1, [P, m, L.cols]), ALU.add)

        wait(dve, self.stored[q], 16 * self.stores * (c // 2))
        self.projection.on_vector(dve, self.projection.numbers("table", c), evacuate)
        dve.wait_ge(self.projection.product_used, self.projection.numbers("table", c)[-1] + 1)
        dve.sem_inc(self.filled, 1)
        if L.parts == 3:
            g, w = L.gathered, L.window
            left = self.table[:, q, 0:m0, g:g + w]
            for part in range(2):
                out = left if part == 0 else self.parts[:, q, 0:m0, 2 * w:3 * w]
                dve.wait_ge(self.rounded, 2 * c + part + 1)
                v.tensor_tensor(out, left, self.parts[:, q, 0:m0, part * w:(part + 1) * w], ALU.subtract
                                ).then_inc(self.left, 1)

    def on_scalar(self, act, c):
        L, q = self.L, c % 2
        if L.parts != 3:
            return
        m0, g, w = CHUNKS[c][1], L.gathered, L.window
        act.wait_ge(self.filled, c + 1)
        wait(act, self.stored[q], 16 * self.stores * (c // 2))
        for part in range(2):
            if part:
                act.wait_ge(self.left, 2 * c + 1)
            act.activation(self.parts[:, q, 0:m0, part * w:(part + 1) * w], self.table[:, q, 0:m0, g:g + w],
                           ACT.Copy).then_inc(self.rounded, 1)

    def on_sync(self, sp, c):
        L, q = self.L, c % 2
        k0, m0 = CHUNKS[c]
        g, w = L.gathered, L.window
        sp.wait_ge(self.filled, c + 1)
        sp.dma_start(node_view(L.gather_table)[:, k0:k0 + m0, :], self.table[:, q, 0:m0, 0:g]
                     ).then_inc(self.stored[q], 16)
        if L.parts == 3:
            sp.wait_ge(self.left, 2 * (c + 1))
            sp.dma_start(node_view(L.window_table)[:, k0:k0 + m0, :], self.parts[:, q, 0:m0, :]
                         ).then_inc(self.stored[q], 16)
        else:
            with self.nc.allow_non_contiguous_dma(reason="a column of the window table"):
                sp.dma_start(node_view(L.window_table)[:, k0:k0 + m0, :], self.table[:, q, 0:m0, g:g + w]
                             ).then_inc(self.stored[q], 16)

    def all_stored(self, sp):
        for q in range(2):
            sp.wait_ge(self.stored[q], 16 * self.stores * len(range(q, NCH, 2)))


def node_view(table):
    return table.rearrange("(k p) w -> p k w", p=P)


def first_tables(nc, L, S):
    ctx = ExitStack()
    with ctx:
        jobs = [j for c in range(NCH) for j in table_jobs(L, S, c)]
        projection = Projection(nc, ctx, "first_tables", S, jobs)
        made = Tables(nc, ctx, L, S, projection)
        block = ctx.enter_context(nc.Block())

        @block.tensor
        def _(pe):
            for c in range(NCH):
                projection.on_tensor(pe, projection.numbers("table", c))

        @block.scalar
        def _(act):
            for c in range(NCH + 1):
                if c < NCH:
                    projection.on_scalar(act, projection.numbers("table", c))
                if c > 0:
                    made.on_scalar(act, c - 1)

        @block.vector
        def _(dve):
            for c in range(NCH):
                made.on_vector(dve, c)

        @block.sync
        def _(sp):
            for c in range(NCH):
                made.on_sync(sp, c)
            made.all_stored(sp)


def spread(ap, w):
    return bc(ap, 2, [ap.shape[0], ap.shape[1], w])


def dense(nc, L, S, nxt, out):
    soft = L.heads > 0
    H, M, K = L.heads, L.msg, KN
    T, C = S["T_" + L.name], S["C_" + L.name]
    ctx = ExitStack()
    with ctx:
        def sb(name, shape, dt=F32):
            return ctx.enter_context(nc.sbuf_tensor(f"{L.name}_d_{name}", shape, dt))

        def sem(name):
            return ctx.enter_context(nc.semaphore(f"{L.name}_d_{name}"))

        node_sums = sb("node_sums", [P, K * L.row])
        sums = node_sums[:, :].rearrange("p (k w) -> p k w", k=K)
        into = sb("into", [P, K, L.row])
        tails = sb("tails", [P, LAST_C, B, L.row])
        tail_sums = sb("tail_sums", [M, NT])
        state = sb("state", [M, NTP])
        rows = sb("rows", [P, RB, L.row])
        X, nodes = S["X"], S["work"]
        stat = sb("stat", [P, 2, K])
        if soft:
            wide = sb("wide", [P, LAST_C, B, M])
            tail_max = sb("tail_max", [M, NT])
            top = sb("top", [M, NTP])
            gate = sb("gate", [M, NT])
            fade = sb("fade", [M, NT])
            node_top = sb("node_top", [P, K, H])
            carried_top = sb("carried_top", [P, K, H])
            unspanned = sb("unspanned", [P, K])
            weight = sb("weight", [P, 2, K, H])
            shifted, weighed = sem("shifted"), sem("weighed")
        ps = [ctx.enter_context(nc.psum_tensor(f"{L.name}_c_ps{n}", [P, SG * P], F32)) for n in range(2)]
        tails_in, wide_made, turned, copied = sem("tails_in"), sem("wide_made"), sem("turned"), sem("copied")
        chain_v, tops_shifted, faded, scanned = sem("chain_v"), sem("tops_shifted"), sem("faded"), sem("scanned")
        back, back_copied, ranked = sem("back"), sem("back_copied"), sem("ranked")
        carry_in = [sem(f"carry_in{c}") for c in range(NCH)]
        fetched = [S[f"{L.name}_fetched{c}"] for c in range(NCH)]
        scattered = S[L.name + "_scattered"]
        centred, squared, squares_summed, root_done = sem("centred"), sem("squared"), sem("squares_summed"), sem("root")
        x_ready = sem("x_ready")
        if L.name == "mlp":
            summed = sem("summed")
            ranks = Rank(nc, ctx, S)
        if L.name == "gatv2":
            mean = sb("mean", [P, D])
            scale = sb("scale", [P, D])
            bn_ps = ctx.enter_context(nc.psum_tensor("gatv2_bn_ps", [P, 512], F32))
            rows_ready, sum_made, bn_centred, bn_squared = (sem("rows_ready"), sem("sum_made"), sem("bn_centred"),
                                                            sem("bn_squared"))
            squares_made, var_made, scale_made = sem("squares_made"), sem("var_made"), sem("scale_made")
            gelu_in, gelu_out = sem("gelu_in"), sem("gelu_out")
        if L.name == "gat":
            neg = sb("neg", [P, K, D])
            elu_in, elu_out = sem("elu_in"), sem("elu_out")
        if nxt is not None and nxt.window:
            jobs = []
            for c in range(NCH + 1):
                if L.name == "mlp" and c < NCH:
                    k0, m0 = CHUNKS[c][0], min(CHUNKS[c][1], K - CHUNKS[c][0])
                    jobs += [(("w2", c), k, min(SG, k0 + m0 - k), nodes, S["w2"][:, :], D)
                             for k in range(k0, k0 + m0, SG)]
                if L.name != "mlp" and c < NCH:
                    jobs += table_jobs(nxt, S, c)
                if L.name == "mlp" and c > 0:
                    jobs += table_jobs(nxt, S, c - 1)
            projection = Projection(nc, ctx, L.name + "_d", S, jobs)
            made = Tables(nc, ctx, nxt, S, projection)
        else:
            made = projection = None
            x_stored = sem("x_stored")
        block = ctx.enter_context(nc.Block())

        counts = [min(P, NB - c * P) for c in range(LAST_C)]
        Tv = T.rearrange("(n p b) w -> n p (b w)", p=P, b=B)
        turns = []
        for c in range(LAST_C):
            for j0 in range(0, B, SG):
                turns.append((tail_sums, tails, c, j0, min(SG, B - j0)))
                if soft:
                    turns.append((tail_max, wide, c, j0, min(SG, B - j0)))
        backs = [(s, r, min(SG, RB - r)) for r in range(0, RB, SG) for s in (("state", "top") if soft else ("state",))]

        def span(c):
            k, m = CHUNKS[c]
            return slice(k, min(k + m, K))

        @block.sync
        def _(sp):
            for c in range(LAST_C):
                sp.dma_start(tails[0:counts[c], c, :, :].rearrange("n b w -> n (b w)"),
                             Tv[c * P:c * P + counts[c], P - 1, :]).then_inc(tails_in, 16)
            sp.wait_ge(scattered, 16 * RB)
            for c in range(NCH):
                sp.dma_start(into[:, span(c), :], node_view(C)[:, span(c), :]).then_inc(carry_in[c], 16)
            for c in range(NCH):
                if made:
                    made.on_sync(sp, c)
                elif nxt is not None:
                    k, m = CHUNKS[c]
                    sp.wait_ge(x_ready, c + 1)
                    sp.dma_start(node_view(nxt.gather_table)[:, k:k + m, :], X[:, k:k + m, :]).then_inc(x_stored, 16)
                else:
                    sp.wait_ge(x_ready, c + 1)
                    k, m = span(c).start, min(span(c).stop, K - 1) - span(c).start
                    if m > 0:
                        sp.dma_start(out[k * P:(k + m) * P, :].rearrange("(k p) f -> p k f", p=P),
                                     X[:, k:k + m, :]).then_inc(x_stored, 16)
                    if span(c).stop == K:
                        sp.dma_start(out[(K - 1) * P:N, :], X[0:NREST, K - 1, :]).then_inc(x_stored, 16)
            if made:
                made.all_stored(sp)
            else:
                sp.wait_ge(x_stored, 16 * NCH)

        @block.gpsimd
        def _(pool):
            if L.name == "mlp":
                pool.wait_ge(ranked, 1)

            def fetch(blocks):
                for k in blocks:
                    pool.indirect_dma_start(
                        out=node_sums[:, k * L.row:(k + 1) * L.row], out_offset=None, in_=T,
                        in_offset=bass.IndirectOffsetOnAxis(ap=S["last_row"][:, k:k + 1], axis=0)
                    ).then_inc(fetched[k // CHUNK], 16)

            early = EARLY_SOFT if soft else EARLY
            fetch(range(early))
            for r in range(RB):
                wait(pool, back_copied, sum(1 for s, r0, m in backs if r0 <= r))
                pool.indirect_dma_start(
                    out=C, out_offset=bass.IndirectOffsetOnAxis(ap=S["carry_row"][:, r:r + 1], axis=0),
                    in_=rows[:, r, :], in_offset=None, bounds_check=NP - 1, oob_is_err=False
                ).then_inc(scattered, 16)
            fetch(range(early, K))
            for c in range(NCH):
                pool.wait_ge(fetched[c], 16 * (span(c).stop - span(c).start))

        @block.tensor
        def _(pe):
            if L.name == "mlp":
                ranks.on_tensor(pe)
            pe.wait_ge(tails_in, 16 * LAST_C)
            if soft:
                pe.wait_ge(wide_made, 1)
            for n, (dst, src, c, j0, m) in enumerate(turns):
                wait(pe, copied, n - 1)
                k = counts[c]
                for j in range(m):
                    last = pe.transpose(ps[n % 2][0:M, j * P:j * P + k], src[0:k, c, j0 + j, 0:M],
                                        S["ident"][0:k, 0:k])
                last.then_inc(turned, 1)
            pe.wait_ge(scanned, 1)
            pe.wait_ge(copied, len(turns))
            for n, (s, r, m) in enumerate(backs):
                wait(pe, back_copied, n - 1)
                src = state if s == "state" else top
                for j in range(m):
                    last = pe.transpose(ps[n % 2][:, j * P:j * P + M], src[:, (r + j) * P:(r + j + 1) * P],
                                        S["ident"][0:M, 0:M])
                last.then_inc(back, 1)
            if L.name == "gatv2":
                for src, ready, done, at in ((nodes, rows_ready, sum_made, 0), (None, bn_squared, squares_made, D)):
                    for k in range(K):
                        if k % CHUNK == 0:
                            pe.wait_ge(ready, k // CHUNK + 1)
                        p = P if k < K - 1 else NREST
                        rhs = nodes[0:p, k, :] if src is not None else sums[0:p, k, 0:D]
                        last = pe.matmul(bn_ps[:, at:at + D], S["ones"][0:p, :], rhs, start=k == 0, stop=k == K - 1,
                                         skip_group_check=True)
                    last.then_inc(done, 1)
            if made:
                for c in range(NCH + 1):
                    if L.name == "mlp" and c < NCH:
                        pe.wait_ge(summed, c + 1)
                        projection.on_tensor(pe, projection.numbers("w2", c))
                    t = c - 1
                    if t >= 0:
                        pe.wait_ge(x_ready, t + 1)
                        projection.on_tensor(pe, projection.numbers("table", t))

        @block.scalar
        def _(act):
            for n, (dst, src, c, j0, m) in enumerate(turns):
                act.wait_ge(turned, n + 1)
                k = counts[c]
                t0 = c * P * B
                act.activation(
                    dst[:, t0:t0 + k * B].rearrange("f (n b) -> f b n", b=B)[:, j0:j0 + m, :],
                    ps[n % 2][0:M, 0:m * P].rearrange("f (b n) -> f b n", b=m)[:, :, 0:k], ACT.Copy
                ).then_inc(copied, 1)
            if soft:
                act.wait_ge(tops_shifted, 1)
                act.activation(tail_max[:, :], tail_max[:, :], ACT.Exp)
                act.activation(fade[:, 1:NT], fade[:, 1:NT], ACT.Exp).then_inc(faded, 1)
            for n, (s, r, m) in enumerate(backs):
                act.wait_ge(back, n + 1)
                part = slice(0, M) if s == "state" else slice(D, M)
                to = slice(0, M) if s == "state" else slice(M, L.row)
                act.activation(rows[:, r:r + m, to],
                               ps[n % 2][:, 0:m * P].rearrange("p (r f) -> p r f", r=m)[:, :, part], ACT.Copy
                               ).then_inc(back_copied, 1)

            def weights_of(c):
                act.wait_ge(shifted, c + 1)
                act.activation(weight[:, :, span(c), :], weight[:, :, span(c), :], ACT.Exp).then_inc(weighed, 1)

            if L.name == "gatv2":
                for c in range(NCH):
                    weights_of(c)
                for c in range(NCH):
                    act.wait_ge(bn_centred, c + 1)
                    act.activation(sums[:, span(c), 0:D], nodes[:, span(c), :], ACT.Square).then_inc(bn_squared, 1)
                act.wait_ge(var_made, 1)
                act.activation(scale[:, :], scale[:, :], ACT.Sqrt).then_inc(scale_made, 1)
                for c in range(NCH):
                    act.wait_ge(gelu_in, c + 1)
                    act.activation(nodes[:, span(c), :], nodes[:, span(c), :], ACT.Gelu).then_inc(gelu_out, 1)
            for c in range(NCH + 2):
                if 0 <= c - 1 < NCH:
                    act.wait_ge(squares_summed, c)
                    act.activation(stat[:, 1, span(c - 1)], stat[:, 1, span(c - 1)], ACT.Sqrt).then_inc(root_done, 1)
                if c < NCH and L.name == "mlp":
                    projection.on_scalar(act, projection.numbers("w2", c))
                if made and c - 2 >= 0:
                    made.on_scalar(act, c - 2)
                if c < NCH and L.name == "gat":
                    weights_of(c)
                    act.wait_ge(elu_in, c + 1)
                    act.activation(neg[:, span(c), :], neg[:, span(c), :], ACT.Exp).then_inc(elu_out, 1)
                if c < NCH:
                    act.wait_ge(centred, c + 1)
                    act.activation(X[:, span(c), :], nodes[:, span(c), :], ACT.Square).then_inc(squared, 1)
                if made and 0 <= c - 1 < NCH:
                    projection.on_scalar(act, projection.numbers("table", c - 1))

        @block.vector
        def _(dve):
            v = nc.vector
            chain = Chain(dve, chain_v)
            if L.name == "mlp":
                ranks.on_vector(dve, chain, ranked)

            def scan_soft():
                dve.wait_ge(tails_in, 16 * LAST_C)
                c64 = D // H
                for c in range(LAST_C):
                    k = counts[c]
                    top_h = tails[0:k, c, :, M:L.row]
                    v.tensor_copy(wide[0:k, c, :, 0:D].rearrange("n b (h c) -> n b h c", c=c64),
                                  bc(top_h, 3, [k, B, H, c64]))
                    last = v.tensor_copy(wide[0:k, c, :, D:M], top_h)
                last.then_inc(wide_made, 1)
                v.memset(top[:, 0:1], 0.0)
                v.memset(top[:, NT:NTP], 0.0)
                v.memset(state[:, 0:1], 0.0)
                v.memset(state[:, NT:NTP], 0.0)
                chain(v.tensor_scalar(gate[:, :], S["through"][0:M, :], 1.0, BIG, ALU.subtract, ALU.mult))
                dve.wait_ge(copied, len(turns))
                chain(v.tensor_tensor_scan(fade[:, :], gate[:, :], tail_max[:, :], 0.0, ALU.add, ALU.max))
                v.tensor_copy(top[:, 1:NT], fade[:, 0:NT - 1])
                chain(v.tensor_tensor(tail_max[:, :], tail_max[:, :], fade[:, :], ALU.subtract))
                chain(v.tensor_tensor(gate[:, 1:NT], fade[:, 0:NT - 1], fade[:, 1:NT], ALU.subtract))
                v.tensor_scalar(fade[:, 1:NT], gate[:, 1:NT], 0.0, None, ALU.min).then_inc(tops_shifted, 1)
                dve.wait_ge(faded, 1)
                chain(v.memset(gate[:, 0:1], 0.0))
                v.tensor_tensor(gate[:, 1:NT], fade[:, 1:NT], S["through"][0:M, 1:NT], ALU.mult)
                chain(v.tensor_tensor(tail_sums[:, :], tail_sums[:, :], tail_max[:, :], ALU.mult))
                v.tensor_tensor_scan(state[:, 1:NT], gate[:, 0:NT - 1], tail_sums[:, 0:NT - 1], 0.0,
                                     ALU.mult, ALU.add).then_inc(scanned, 1)

            def arrived(c):
                dve.wait_ge(fetched[c], 16 * (span(c).stop - span(c).start))
                dve.wait_ge(carry_in[c], 16)

            def softmax_sums(c):
                s = span(c)
                n, w = s.stop - s.start, D // H
                last_tile, carried, up = sums[:, s, :], into[:, s, :], node_top[:, s, :]
                chain(v.tensor_tensor(carried_top[:, s, :], carried[:, :, M:L.row], spread(S["spans"][:, s], H),
                                      ALU.mult))
                chain(v.tensor_tensor(carried_top[:, s, :], carried_top[:, s, :], spread(unspanned[:, s], H),
                                      ALU.add))
                chain(v.tensor_tensor(up, carried_top[:, s, :], last_tile[:, :, M:L.row], ALU.max))
                v.tensor_tensor(weight[:, 0, s, :], last_tile[:, :, M:L.row], up, ALU.subtract)
                v.tensor_tensor(weight[:, 1, s, :], carried_top[:, s, :], up, ALU.subtract).then_inc(shifted, 1)
                dve.wait_ge(weighed, c + 1)
                for i, t in enumerate((last_tile, carried)):
                    v.tensor_tensor(t[:, :, D:M], t[:, :, D:M], weight[:, i, s, :], ALU.mult)
                    last = v.tensor_tensor(t[:, :, 0:D].rearrange("p k (h c) -> p k h c", c=w),
                                           t[:, :, 0:D].rearrange("p k (h c) -> p k h c", c=w),
                                           bc(weight[:, i, s, :], 3, [P, n, H, w]), ALU.mult)
                chain(last)
                v.tensor_tensor(nodes[:, s, :], last_tile[:, :, 0:D], carried[:, :, 0:D], ALU.add)
                chain(v.tensor_tensor(up, last_tile[:, :, D:M], carried[:, :, D:M], ALU.add))
                if L.name == "gatv2":
                    chain(v.tensor_scalar(up, up, 1e-16, None, ALU.add))
                chain(v.reciprocal(up, up))
                return v.tensor_tensor(nodes[:, s, :].rearrange("p k (h c) -> p k h c", c=w),
                                       nodes[:, s, :].rearrange("p k (h c) -> p k h c", c=w),
                                       bc(up, 3, [P, n, H, w]), ALU.mult)

            def batch_norm():
                for c in range(NCH):
                    s = span(c)
                    arrived(c)
                    chain(softmax_sums(c))
                    n = s.stop - s.start
                    v.tensor_tensor(nodes[:, s, :], nodes[:, s, :], bc(S["bias"][:, :], 1, [P, n, D]), ALU.add
                                    ).then_inc(rows_ready, 1)
                    v.tensor_tensor(into[:, s, 0:D], X[:, s, :], bc(S["beta"][:, :], 1, [P, n, D]), ALU.add)
                dve.wait_ge(sum_made, 1)
                chain(v.tensor_scalar(mean[:, :], bn_ps[:, 0:D], 1.0 / N, None, ALU.mult))
                for c in range(NCH):
                    s = span(c)
                    v.tensor_tensor(nodes[:, s, :], nodes[:, s, :], bc(mean[:, :], 1, [P, s.stop - s.start, D]),
                                    ALU.subtract).then_inc(bn_centred, 1)
                dve.wait_ge(squares_made, 1)
                v.tensor_scalar(scale[:, :], bn_ps[:, D:2 * D], 1.0 / N, BN_EPS, ALU.mult, ALU.add
                                ).then_inc(var_made, 1)
                dve.wait_ge(scale_made, 1)
                chain(v.reciprocal(scale[:, :], scale[:, :]))
                chain(v.tensor_tensor(scale[:, :], scale[:, :], S["gamma"][:, :], ALU.mult))
                for c in range(NCH):
                    s = span(c)
                    chain(v.tensor_tensor(nodes[:, s, :], nodes[:, s, :],
                                          bc(scale[:, :], 1, [P, s.stop - s.start, D]), ALU.mult))
                    v.tensor_tensor(nodes[:, s, :], nodes[:, s, :], into[:, s, 0:D], ALU.add).then_inc(gelu_in, 1)

            def combine(c):
                s = span(c)
                if L.name == "gatv2":
                    dve.wait_ge(gelu_out, c + 1)
                    chain(v.tensor_tensor(nodes[:, s, :], nodes[:, s, :], X[:, s, :], ALU.add))
                    return
                arrived(c)
                if L.name == "mlp":
                    v.tensor_tensor(nodes[:, s, :], sums[:, s, :], into[:, s, :], ALU.add).then_inc(summed, 1)
                elif L.name == "gat":
                    chain(softmax_sums(c))
                    v.tensor_scalar(neg[:, s, :], nodes[:, s, :], 0.0, None, ALU.min).then_inc(elu_in, 1)
                    chain(v.scalar_tensor_tensor(out=nodes[:, s, :], in0=nodes[:, s, :], scalar=0.0,
                                                 in1=X[:, s, :], op0=ALU.max, op1=ALU.add))
                    dve.wait_ge(elu_out, c + 1)
                    chain(v.scalar_tensor_tensor(out=nodes[:, s, :], in0=neg[:, s, :], scalar=-1.0,
                                                 in1=nodes[:, s, :], op0=ALU.add, op1=ALU.add))
                else:
                    chain(v.tensor_tensor(nodes[:, s, :], sums[:, s, :], into[:, s, :], ALU.add))
                    chain(v.tensor_tensor(nodes[:, s, :], nodes[:, s, :], spread(S["per_edge"][:, s], D), ALU.mult))
                    chain(v.tensor_tensor(nodes[:, s, :], nodes[:, s, :], X[:, s, :], ALU.add))

            def add_projected(c):
                def evacuate(k, m, product):
                    return v.tensor_tensor(nodes[:, k:k + m, :], product, X[:, k:k + m, :], ALU.add)
                numbers = projection.numbers("w2", c)
                projection.on_vector(dve, numbers, evacuate)
                dve.wait_ge(projection.product_used, numbers[-1] + 1)

            def centre(c):
                s = span(c)
                chain(v.tensor_reduce(stat[:, 0, s], nodes[:, s, :], AX, ALU.add))
                v.scalar_tensor_tensor(out=nodes[:, s, :], in0=spread(stat[:, 0, s], D), scalar=-1.0 / D,
                                       in1=nodes[:, s, :], op0=ALU.mult, op1=ALU.add).then_inc(centred, 1)

            def variance(c):
                s = span(c)
                dve.wait_ge(squared, c + 1)
                chain(v.tensor_reduce(stat[:, 1, s], X[:, s, :], AX, ALU.add))
                v.tensor_scalar(stat[:, 1, s], stat[:, 1, s], 1.0 / D, LN_EPS, ALU.mult, ALU.add
                                ).then_inc(squares_summed, 1)

            def normalise(c):
                s = span(c)
                dve.wait_ge(root_done, c + 1)
                chain(v.reciprocal(stat[:, 1, s], stat[:, 1, s]))
                v.tensor_tensor(X[:, s, :], nodes[:, s, :], spread(stat[:, 1, s], D), ALU.mult).then_inc(x_ready, 1)

            if soft:
                v.tensor_scalar(unspanned[:, :], S["spans"][:, 0:K], 1.0, BIG, ALU.subtract, ALU.mult)
                scan_soft()
            else:
                v.memset(state[:, 0:1], 0.0)
                chain(v.memset(state[:, NT:NTP], 0.0))
                dve.wait_ge(copied, len(turns))
                v.tensor_tensor_scan(state[:, 1:NT], S["through"][0:M, 0:NT - 1], tail_sums[:, 0:NT - 1], 0.0,
                                     ALU.mult, ALU.add).then_inc(scanned, 1)
            if L.name == "mlp":
                v.tensor_scalar(S["per_edge"][:, :], S["degree"][:, 0:K], 1.0, None, ALU.max)
                chain(v.tensor_tensor(nodes[:, :, :], spread(S["degree"][:, 0:K], D), bc(S["b2"][:, :], 1, [P, K, D]),
                                      ALU.mult))
                v.reciprocal(S["per_edge"][:, :], S["per_edge"][:, :])
                chain(v.tensor_tensor(X[:, 0:K, :], X[:, 0:K, :], nodes[:, :, :], ALU.add))
            if L.name == "gatv2":
                batch_norm()
            for c in range(NCH + 2):
                if 0 <= c - 1 < NCH:
                    variance(c - 1)
                if c < NCH:
                    combine(c)
                if made and c - 2 >= 0:
                    made.on_vector(dve, c - 2)
                if c < NCH and L.name == "mlp":
                    add_projected(c)
                if c < NCH:
                    centre(c)
                if 0 <= c - 1 < NCH:
                    normalise(c - 1)

def clear_semaphores(nc, numbers):
    with nc.Block() as block:
        @block.gpsimd
        def _(pool):
            pool.sem_clear(numbers)


def build(nc, A, out, last=4):
    def dram(name, shape, dt=F32):
        return nc.dram_tensor(name, shape, dt, kind="Internal").ap()

    layers = [
        Layer("mlp", D, D, 32, 0, dram("mlp_src", [NP, D]), dram("mlp_dst", [NP, 3 * D], BF16)),
        Layer("gatv2", D, D, 16, HEADS, dram("gatv2_src", [NP, D]), dram("gatv2_dst", [NP, 3 * D], BF16)),
        Layer("gat", D + 1, 1, 0, 1, dram("gat_src", [NP, D + 1]), dram("gat_dst", [NP, 1])),
        Layer("mean", D, 0, 0, 0, dram("mean_src", [NP, D]), None),
    ]
    ctx = ExitStack()
    with ctx:
        def sb(name, shape, dt=F32):
            return ctx.enter_context(nc.sbuf_tensor(name, shape, dt))

        row = D + 2 * HEADS
        S = {
            "X": sb("X", [P, KP, D]), "work": sb("work", [P, KN, D]),
            "src_cols": sb("src_cols", [P, NTP], I32), "rel_cols": sb("rel_cols", [P, NTP]),
            "hi_cols": sb("hi_cols", [P, NTP], BF16), "lo_cols": sb("lo_cols", [P, NTP], BF16),
            "base_row": sb("base_row", [1, NTP], I32),
            "lane": sb("lane", [P, 1]), "iota": sb("iota", [P, P], BF16), "ident": sb("ident", [P, P]),
            "tri": sb("tri", [HI, HI]), "ones": sb("ones", [P, P]), "counts": sb("counts", [HI, P]),
            "through": sb("through", [D + HEADS, NT]), "carry_row": sb("carry_row", [P, RB], I32),
            "degree": sb("degree", [P, HI]), "spans": sb("spans", [P, HI]), "last_row": sb("last_row", [P, HI], I32),
            "per_edge": sb("per_edge", [P, KN]),
            "w1": sb("w1", [D, 2 * D]), "w2": sb("w2", [D, D]), "b2": sb("b2", [P, D]), "bias0": sb("bias0", [P, 2 * D]),
            "wlr": sb("wlr", [D, 2 * D]), "bias1": sb("bias1", [P, 2 * D]), "att_bc": sb("att_bc", [P, D]),
            "bias": sb("bias", [P, D]), "gamma": sb("gamma", [P, D]), "beta": sb("beta", [P, D]),
            "w3": sb("w3", [D, D + 2]), "a2": sb("a2", [D, 2]),
            "attr_w": {32: sb("attr_w32", [P, 4 * D]), 16: sb("attr_w16", [16 * B, B * D])},
            "attr": {32: A["edge_attr_32"], 16: A["edge_attr_16"]},
            "rel_rows": dram("rel_rows", [NTP * P], BF16), "edge_rows": dram("edge_rows", [NTP, HEADS, 2 * P]),
            "first_dram": dram("first_dram", [NTP + 1], I32), "last_dram": dram("last_dram", [NTP + 1], I32),
        }
        for L in layers:
            S["T_" + L.name] = dram("sums_" + L.name, [NT * P, L.row])
            S["C_" + L.name] = dram("carry_" + L.name, [NP, L.row])
        for L in layers:
            for name in [f"gathered{q}" for q in range(Q)] + ["scattered"] + [
                    f"fetched{c}" for c in range(NCH)]:
                S[f"{L.name}_{name}"] = ctx.enter_context(nc.semaphore(f"{L.name}_{name}"))
        for L, weights, cols, bias in zip(layers, ("w1", "wlr", "w3"), (2 * D, 2 * D, D + 2), ("bias0", "bias1", None)):
            L.weights, L.cols, L.bias = S[weights][:, :], cols, S[bias][:, :] if bias else None
        numbers = range(min(nc.free_semaphores), max(nc.free_semaphores) + 1)
        prepare(nc, S, A, [S["C_" + L.name] for L in layers])
        edge_scores(nc, S)
        for n, L in enumerate(layers[:last]):
            if n:
                clear_semaphores(nc, numbers)
            if n == 0:
                first_tables(nc, L, S)
            edge_pass(nc, L, S, hist=(n == 0))
            dense(nc, L, S, layers[n + 1] if n + 1 < last else None, out)


INPUTS = ["x", "src", "dst", "edge_attr_16", "edge_attr_32", "L0_gnn_W1", "L0_gnn_b1", "L0_gnn_W2", "L0_gnn_b2",
          "L1_gnn_W_l", "L1_gnn_b_l", "L1_gnn_W_r", "L1_gnn_b_r", "L1_gnn_W_e", "L1_gnn_att", "L1_gnn_bias",
          "L1_gnn_gamma", "L1_gnn_beta", "L2_gnn_W", "L2_gnn_a"]


def kernel(**inputs):
    import concourse.bacc as bacc
    from concourse.bass_utils import run_bass_kernel_spmd

    nc = bacc.Bacc("TRN2", target_bir_lowering=False, num_devices=1)
    arrays, A = {}, {}
    for name in INPUTS:
        a = np.ascontiguousarray(inputs[name])
        arrays["in_" + name] = a
        A[name] = nc.dram_tensor("in_" + name, a.shape, mybir.dt.from_np(a.dtype), kind="ExternalInput").ap()
    out = nc.dram_tensor("out_nodes", (N, D), F32, kind="ExternalOutput").ap()
    build(nc, A, out)
    r = run_bass_kernel_spmd(nc, [arrays], core_ids=[0])
    return r.results[0]["out_nodes"]
```

```python
import numpy as np
import concourse.bass as bass
from concourse import mybir
from contextlib import ExitStack

F32 = mybir.dt.float32
BF16 = mybir.dt.bfloat16
I32 = mybir.dt.int32
ALU = mybir.AluOpType
ACT = mybir.ActivationFunctionType
AX = mybir.AxisListType.X

P = 128
N = 6250
E = 206250
D = 64
HEADS = 4
B = 7
Q = 4
NB = -(-E // (P * B))
NT = NB * B
ETILES = -(-E // P)
RB = -(-NT // P)
NTP = RB * P
EFULL, EREST = E // P, E % P
KN = -(-N // P)
KP = KN + 1
NP = KP * P
NREST = N - (KN - 1) * P
HI = -(-(N + 1) // P)
BIG = 3.0e38
LN_EPS = 1e-5
BN_EPS = 1e-5
SLOPE = 0.2
LAST_C = -(-NB // P)
SP_TILES = 4
FIRST_CHUNKS = 1
EARLY, EARLY_SOFT = 8, 26
SG = 4


class Layer:

    def __init__(self, name, gathered, window, attr, heads, gather_table, window_table):
        self.name, self.gathered, self.window, self.attr, self.heads = name, gathered, window, attr, heads
        self.gather_table, self.window_table = gather_table, window_table
        self.msg = D + heads
        self.row = D + 2 * heads
        self.parts = 3 if window == D else 1
        self.win_dt = BF16 if self.parts == 3 else F32


class Batch:

    def __init__(self, loop, c):
        self.loop, self.c = loop, c
        self.q = c % Q
        self.n = loop * Q + c
        self.turn = loop + c // Q

    def __add__(self, d):
        return Batch(self.loop, self.c + d)

    def exists(self):
        return not isinstance(self.n, int) or 0 <= self.n < NB

    def used(self, back=0):
        return self.n + 1 - back

    def landed(self, dmas=1):
        return (self.turn + 1) * (16 * dmas)

    def tiles(self):
        return min(B, ETILES - self.n * B) if isinstance(self.n, int) else B

    def rows_landed(self):
        return self.landed_before(B) + 16 * self.tiles()

    def landed_before(self, dmas=1):
        return self.turn * (16 * dmas)


def wait(eng, sem, count):
    if not isinstance(count, int) or count > 0:
        eng.wait_ge(sem, count)


def over_batches(eng, first, step):
    start = 2 * Q
    loops = (NB - start) // Q - 1
    for n in range(first, start):
        step(Batch(0, n))
    with eng.Fori(0, loops) as it:
        for c in range(Q):
            step(Batch(it, start + c))
    for n in range(start + loops * Q, NB + 2):
        step(Batch(0, n))


def bc(ap, axis, shape):
    return ap.unsqueeze(axis).to_broadcast(shape)


def load_windows(nc, eng, L, S, win, win_in, b, tiles):
    _, bases = nc.values_load_multi_w_load_instructions(
        S["base_row"][0:1, bass.ds(b.n * B + tiles[0], len(tiles))], engines=[eng.engine], min_val=0, max_val=N,
        skip_runtime_bounds_check_because="they are destinations, which lie in 0..N")
    for j, base in zip(tiles, bases):
        eng.dma_start(win[:, b.q, j, :], L.window_table[bass.ds(base, P), :]).then_inc(win_in[b.q], 16)


def edge_pass(nc, L, S, hist):
    soft = L.heads > 0
    H = L.heads
    ax = L.attr
    groups = {0: [], 32: [(0, 4), (4, 3)], 16: [(0, 7)]}[ax]
    ctx = ExitStack()
    with ctx:
        def sb(name, shape, dt=F32):
            return ctx.enter_context(nc.sbuf_tensor(f"{L.name}_{name}", shape, dt))

        def pb(name, shape):
            return ctx.enter_context(nc.psum_tensor(f"{L.name}_{name}", shape, F32))

        def sem(name):
            return ctx.enter_context(nc.semaphore(f"{L.name}_{name}"))

        idx = sb("idx", [P, Q, B], I32)
        G = sb("G", [P, Q, B * L.gathered])
        rel = sb("rel", [P, Q, B * P], BF16)
        same = sb("same", [P, Q, B, P])
        out_rows = sb("out_rows", [P, Q, B * L.row])
        Gv = G[:].rearrange("p q (b w) -> p q b w", b=B)
        outv = out_rows[:].rearrange("p q (b w) -> p q b w", b=B)
        relv = rel[:].rearrange("p q (b e) -> p q b e", b=B)
        sums = [pb(f"sums{n}", [P, 512]) for n in range(2)]
        if L.window:
            hot = sb("hot", [P, Q, B, P], L.win_dt)
            win = sb("win", [P, Q, B, L.parts * L.window], L.win_dt)
            z = [pb(f"z{n}", [P, 512]) for n in range(2)]
            zs = sb("zs", [P, Q, B * L.window])
            act_out = sb("act_out", [P, Q, B * L.window])
        if ax:
            attr = sb("attr", [P, Q, B, ax])
            attrT = sb("attrT", [P, Q, 2, P])
            attrT_ps = pb("attrT_ps", [P, 512])
        if soft:
            logits = sb("logits", [P, Q, B * H]) if H > 1 else act_out
            edges = sb("edges", [B * H, Q, 2, P])
            runmax = sb("runmax", [B * H, P])
            segmax = sb("segmax", [B * H, Q, P])
            diff = sb("diff", [P, Q, B * H])
            msg = sb("msg", [P, Q, B, L.msg])
            lt_ps = pb("lt_ps", [P, 512])[0:B * H, 0:P]
            mb_all = pb("mb_ps", [P, 512])
            mb_ps = mb_all[:, 0:B * H]
            mb_cols = B * H + B * H % 2
        if hist:
            hot_hi = sb("hot_hi", [P, Q, B, HI], BF16)
            hot_lo = sb("hot_lo", [P, Q, B, P], BF16)
            count_ps = pb("count_ps", [P, 512])

        idx_ready = sem("idx_ready")
        gather_turn = sem("gather_turn")
        gathered = [S[f"{L.name}_gathered{q}"] for q in range(Q)]
        rel_in = [sem(f"rel_in{q}") for q in range(Q)]
        stored = [sem(f"stored{q}") for q in range(Q)]
        masks_made = sem("masks_made")
        written = sem("written")
        sums_made = sem("sums_made")
        sums_copied = sem("sums_copied")
        z_added = sem("z_added")
        act_done = sem("act_done")
        if L.window:
            win_in = [sem(f"win_in{q}") for q in range(Q)]
            hot_made = sem("hot_made")
            z_made = sem("z_made")
        if ax:
            attr_in = [sem(f"attr_in{q}") for q in range(Q)]
            attr_turned = sem("attr_turned")
            attr_copied = sem("attr_copied")
        if soft:
            edges_in = [sem(f"edges_in{q}") for q in range(Q)]
            att_done = sem("att_done")
            logits_ready = sem("logits_ready")
            logits_turned = sem("logits_turned")
            prefix_done = sem("prefix_done")
            max_ready = sem("max_ready")
            max_turned = sem("max_turned")
            diff_ready = sem("diff_ready")
            weights_ready = sem("weights_ready")
            msg_ready = sem("msg_ready")
        if hist:
            hist_ready = sem("hist_ready")
            hist_used = sem("hist_used")
        lg_ready = (logits_ready if H > 1 else act_done) if soft else None
        block = ctx.enter_context(nc.Block())

        relD = S["rel_rows"]
        Tv = S["T_" + L.name].rearrange("(n p b) w -> n p (b w)", p=P, b=B)

        @block.sync
        def _(sp):
            def step(i):
                b = i + 2
                if b.exists():
                    wait(sp, masks_made, b.used(Q))
                    sp.dma_start(rel[:, b.q, :],
                                 relD[bass.ds(b.n * (B * P), B * P)].unsqueeze(0).to_broadcast([P, B * P])
                                 ).then_inc(rel_in[b.q], 16)
                    if ax:
                        wait(sp, attr_turned, b.used(Q))
                        attr_load(b)
                    if L.window:
                        wait(sp, z_made, b.used(Q))
                        load_windows(nc, sp, L, S, win, win_in, b, range(0, SP_TILES))
                o = i + (-2)
                if o.exists():
                    wait(sp, sums_copied, o.used())
                    sp.dma_start(Tv[bass.ds(o.n, 1), :, :].rearrange("a p w -> p (a w)"),
                                 out_rows[:, o.q, :]).then_inc(stored[o.q], 16)
                if soft and b.exists():
                    wait(sp, max_ready, b.used(Q))
                    src = S["edge_rows"][bass.ds(b.n * B, B), 0:H, :].rearrange("b h x -> (b h) x")
                    sp.dma_start(edges[:, b.q, :, :].rearrange("r a e -> r (a e)"), src
                                 ).then_inc(edges_in[b.q], 16)
                if isinstance(i.n, int):
                    later_writes(i.n)

            def later_writes(n):
                if hist and 0 <= n < 2 * HEADS:
                    h, r = n // 2, RB // 2 * (n % 2)
                    m = RB // 2 if r == 0 else RB - RB // 2
                    sp.dma_start(S["edge_rows"][:, h, :].rearrange("(r q) x -> q r x", q=P)[:, r:r + m, :],
                                 S["masks"][:, r:r + m, :, :].rearrange("p r a e -> p r (a e)")
                                 ).then_inc(written, 16)
                fills = range(NB - 7, NB - 3) if hist else range(1, 9, 2)
                if n in fills:
                    k = KP * fills.index(n) // len(fills)
                    m = KP * (fills.index(n) + 1) // len(fills) - k
                    sp.dma_start(node_view(S["C_" + L.name])[:, k:k + m, :],
                                 S["zeros"][:, :, 0:L.row].to_broadcast([P, m, L.row])).then_inc(written, 16)

            def attr_load(b):
                A = S["attr"][ax]
                n0 = b.n * B
                if isinstance(n0, int) and n0 + B > EFULL:
                    whole = max(0, EFULL - n0)
                    if whole:
                        sp.dma_start(attr[:, b.q, 0:whole, :],
                                     A[n0 * P:(n0 + whole) * P, :].rearrange("(b p) f -> p b f", p=P)
                                     ).then_inc(attr_in[b.q], 16)
                    if n0 <= EFULL:
                        sp.dma_start(attr[0:EREST, b.q, whole, :], A[EFULL * P:E, :]).then_inc(attr_in[b.q], 16)
                else:
                    sp.dma_start(attr[:, b.q, :, :],
                                 A[bass.ds(b.n * (B * P), B * P), :].rearrange("(b p) f -> p b f", p=P)
                                 ).then_inc(attr_in[b.q], 16)

            over_batches(sp, -2, step)
            for n in range(NB - Q, NB):
                sp.wait_ge(stored[n % Q], Batch(0, n).landed())
            sp.wait_ge(written, 16 * (4 + 2 * HEADS * hist))

        @block.gpsimd
        def _(pool):
            freed = {"mlp": z_added, "gatv2": None, "gat": None, "mean": sums_made}[L.name]
            freed = freed or msg_ready

            def step(b):
                if not b.exists():
                    return
                wait(pool, idx_ready, b.used())
                wait(pool, freed, b.used(Q))
                pool.sem_inc(gather_turn, 1)
                for j in range(b.tiles()):
                    pool.indirect_dma_start(
                        out=G[:, b.q, j * L.gathered:(j + 1) * L.gathered], out_offset=None,
                        in_=L.gather_table, in_offset=bass.IndirectOffsetOnAxis(ap=idx[:, b.q, j:j + 1], axis=0)
                    ).then_inc(gathered[b.q], 16)

            over_batches(pool, 0, step)

        @block.vector
        def _(dve):
            def one_hots(b):
                wait(dve, rel_in[b.q], b.landed())
                wait(dve, z_made, b.used(Q))
                nc.vector.tensor_scalar(hot[:, b.q, :, :], relv[:, b.q, :, :], S["lane"][:, 0:1], None,
                                        ALU.is_equal).then_inc(hot_made, 1)

            def same_destination(b):
                wait(dve, rel_in[b.q], b.landed())
                wait(dve, sums_made, b.used(Q))
                nc.vector.tensor_tensor(same[:, b.q, :, :], relv[:, b.q, :, :],
                                        bc(S["rel_cols"][:, bass.ds(b.n * B, B)], 2, [P, B, P]),
                                        ALU.is_equal).then_inc(masks_made, 1)

            def indices(b):
                nc.vector.tensor_copy(idx[:, b.q, :], S["src_cols"][:, bass.ds(b.n * B, B)]).then_inc(idx_ready, 1)

            def add_gathered(b):
                wait(dve, gathered[b.q], b.rows_landed())
                wait(dve, z_made, b.used())
                if not soft:
                    wait(dve, act_done, b.used(Q))
                w = L.window
                nc.vector.tensor_tensor(zs[:, b.q, :].rearrange("p (b w) -> p b w", w=w),
                                        z[b.q % 2][:, 0:B * w].rearrange("p (b w) -> p b w", w=w),
                                        Gv[:, b.q, :, L.gathered - w:L.gathered], ALU.add).then_inc(z_added, 1)
                if soft:
                    wait(dve, z_added, b.used())
                    nc.vector.scalar_tensor_tensor(out=act_out[:, b.q, :], in0=zs[:, b.q, :], scalar=SLOPE,
                                                   in1=zs[:, b.q, :], op0=ALU.mult, op1=ALU.max
                                                   ).then_inc(act_done, 1)

            def prefix(b):
                wait(dve, logits_turned, b.used())
                wait(dve, edges_in[b.q], b.landed())
                nc.vector.tensor_tensor_scan(runmax[:, :], edges[:, b.q, 0, :], lt_ps, 0.0, ALU.add, ALU.max
                                             ).then_inc(prefix_done, 1)
                wait(dve, prefix_done, b.used())
                wait(dve, max_turned, b.used(Q))
                nc.vector.tensor_tensor_scan(segmax[:, b.q, ::-1], edges[:, b.q, 1, ::-1], runmax[:, ::-1],
                                             0.0, ALU.add, ALU.max).then_inc(max_ready, 1)

            def heads_dot(b):
                wait(dve, act_done, b.used())
                g4 = act_out[:, b.q, :].rearrange("p (b w) -> p b w", b=B)
                nc.vector.tensor_tensor(zs[:, b.q, :].rearrange("p (b w) -> p b w", b=B), g4,
                                        bc(S["att_bc"][:, :], 1, [P, B, D]), ALU.mult).then_inc(att_done, 1)
                wait(dve, att_done, b.used())
                nc.vector.tensor_reduce(logits[:, b.q, :],
                                        zs[:, b.q, :].rearrange("p (r c) -> p r c", c=D // H), AX, ALU.add
                                        ).then_inc(logits_ready, 1)

            def subtract_max(b):
                wait(dve, max_turned, b.used())
                wait(dve, weights_ready, b.used(Q))
                nc.vector.tensor_tensor(diff[:, b.q, :], logits[:, b.q, :], mb_ps, ALU.subtract
                                        ).then_inc(diff_ready, 1)

            def weigh(b):
                wait(dve, weights_ready, b.used())
                c = D // H
                nc.vector.tensor_tensor(
                    msg[:, b.q, :, 0:D].rearrange("p b (h c) -> p b h c", c=c),
                    Gv[:, b.q, :, 0:D].rearrange("p b (h c) -> p b h c", c=c),
                    bc(msg[:, b.q, :, D:D + H], 3, [P, B, H, c]), ALU.mult).then_inc(msg_ready, 1)

            def count(b):
                wait(dve, hist_used, b.used(Q))
                nc.vector.tensor_tensor(hot_hi[:, b.q, :, :], bc(S["iota"][:, 0:HI], 1, [P, B, HI]),
                                        bc(S["hi_cols"][:, bass.ds(b.n * B, B)], 2, [P, B, HI]), ALU.is_equal)
                nc.vector.tensor_tensor(hot_lo[:, b.q, :, :], bc(S["iota"][:, :], 1, [P, B, P]),
                                        bc(S["lo_cols"][:, bass.ds(b.n * B, B)], 2, [P, B, P]), ALU.is_equal
                                        ).then_inc(hist_ready, 1)

            def step(i):
                if L.window and (i + 1).exists():
                    one_hots(i + 1)
                if i.exists():
                    if L.window:
                        add_gathered(i)
                    else:
                        wait(dve, gathered[i.q], i.rows_landed())
                if (i + 3).exists():
                    indices(i + 3)
                if soft:
                    p = i + (-1)
                    if p.exists():
                        prefix(p)
                    if i.exists() and H > 1:
                        heads_dot(i)
                    if p.exists():
                        subtract_max(p)
                    if i.exists():
                        same_destination(i)
                    if p.exists():
                        weigh(p)
                elif i.exists():
                    same_destination(i)
                if hist and i.exists():
                    count(i)

            for n in range(2):
                indices(Batch(0, n))
            over_batches(dve, -1, step)
            if hist:
                dve.wait_ge(hist_used, NB)
                nc.vector.tensor_copy(S["counts"][:, :], count_ps[0:HI, 0:P])

        @block.scalar
        def _(act):
            def copy_sums(b):
                wait(act, sums_made, b.used())
                wait(act, stored[b.q], b.landed_before())
                act.activation(outv[:, b.q, :, 0:L.msg],
                               sums[b.q % 2][:, 0:B * L.msg].rearrange("p (b w) -> p b w", b=B), ACT.Copy
                               ).then_inc(sums_copied, 1)

            def copy_attr(b):
                wait(act, attr_turned, b.used())
                wait(act, z_made, b.used(Q))
                for g, (t0, nt) in enumerate(groups):
                    last = act.activation(attrT[0:nt * ax, b.q, g, :], attrT_ps[0:nt * ax, g * P:(g + 1) * P],
                                          ACT.Copy)
                last.then_inc(attr_copied, 1)

            def nonlinear(b):
                wait(act, z_added, b.used())
                wait(act, sums_made, b.used(Q))
                act.activation(act_out[:, b.q, :], zs[:, b.q, :], ACT.Relu).then_inc(act_done, 1)

            def exponentiate(b):
                wait(act, diff_ready, b.used())
                wait(act, sums_made, b.used(Q))
                wait(act, stored[b.q], b.landed_before())
                act.activation(outv[:, b.q, :, L.msg:L.row],
                               mb_ps.rearrange("p (b h) -> p b h", h=H), ACT.Copy)
                act.activation(msg[:, b.q, :, D:D + H],
                               diff[:, b.q, :].rearrange("p (b h) -> p b h", h=H), ACT.Exp
                               ).then_inc(weights_ready, 1)

            def step(i):
                if (i + (-2)).exists():
                    copy_sums(i + (-2))
                if ax and (i + 1).exists():
                    copy_attr(i + 1)
                if L.window and not soft and i.exists():
                    nonlinear(i)
                w = i + 2
                if L.window and w.exists():
                    wait(act, z_made, w.used(Q))
                    load_windows(nc, act, L, S, win, win_in, w, range(SP_TILES, B))
                if soft and (i + (-1)).exists():
                    exponentiate(i + (-1))

            over_batches(act, -2, step)

        @block.tensor
        def _(pe):
            ident = S["ident"]

            def turn_attr(b):
                n0 = b.n * B
                partial = isinstance(n0, int) and n0 + B > EFULL
                dmas = (1 if EFULL > n0 else 0) + (1 if n0 <= EFULL else 0) if partial else 1
                wait(pe, attr_in[b.q], b.landed_before() + 16 * dmas if partial else b.landed())
                wait(pe, attr_copied, b.used(1))
                for g, (t0, nt) in enumerate(groups):
                    last = pe.transpose(attrT_ps[0:nt * ax, g * P:(g + 1) * P],
                                        attr[:, b.q, t0:t0 + nt, :].rearrange("p b f -> p (b f)"), ident[:, :])
                last.then_inc(attr_turned, 1)

            def make_z(b):
                wait(pe, hot_made, b.used())
                wait(pe, win_in[b.q], b.landed(B))
                wait(pe, z_added, b.used(2))
                w = L.window
                if ax:
                    wait(pe, attr_copied, b.used())
                for t0, nt in groups or [(0, B)]:
                    if ax:
                        g = groups.index((t0, nt))
                        pe.matmul(z[b.q % 2][:, t0 * w:(t0 + nt) * w], attrT[0:nt * ax, b.q, g, :],
                                  S["attr_w"][ax][0:nt * ax, 0:nt * w], start=True, stop=True)
                    for j in range(t0, t0 + nt):
                        for part in range(L.parts):
                            last = pe.matmul(z[b.q % 2][:, j * w:(j + 1) * w], hot[:, b.q, j, :],
                                             win[:, b.q, j, part * w:(part + 1) * w],
                                             start=not ax and part == 0, stop=True, skip_group_check=True)
                last.then_inc(z_made, 1)

            def turn_max(b):
                wait(pe, max_ready, b.used())
                wait(pe, diff_ready, b.used(1))
                wait(pe, weights_ready, b.used(1))
                pe.matmul(mb_all[:, 0:mb_cols], segmax[:, b.q, :], ident[0:B * H, 0:mb_cols], start=True, stop=True
                          ).then_inc(max_turned, 1)

            def turn_logits(b):
                wait(pe, lg_ready, b.used())
                wait(pe, max_ready, b.used(1))
                pe.transpose(lt_ps, logits[:, b.q, :], ident[:, :]).then_inc(logits_turned, 1)

            def make_sums(b):
                wait(pe, masks_made, b.used())
                if soft:
                    wait(pe, msg_ready, b.used())
                elif L.window:
                    wait(pe, act_done, b.used())
                else:
                    wait(pe, gathered[b.q], b.rows_landed())
                wait(pe, sums_copied, b.used(2))
                for j in range(B):
                    if soft:
                        rhs = msg[:, b.q, j, :]
                    elif L.window:
                        rhs = act_out[:, b.q, j * D:(j + 1) * D]
                    else:
                        rhs = Gv[:, b.q, j, :]
                    last = pe.matmul(sums[b.q % 2][:, j * L.msg:(j + 1) * L.msg], same[:, b.q, j, :], rhs,
                                     start=True, stop=True)
                last.then_inc(sums_made, 1)

            def add_counts(b):
                wait(pe, hist_ready, b.used())
                for j in range(B):
                    first = isinstance(b.n, int) and b.n == 0 and j == 0
                    final = isinstance(b.n, int) and b.n == NB - 1 and j == B - 1
                    last = pe.matmul(count_ps[0:HI, 0:P], hot_hi[:, b.q, j, :], hot_lo[:, b.q, j, :],
                                     start=first, stop=final, skip_group_check=True)
                last.then_inc(hist_used, 1)

            def step(i):
                p = i + (-1)
                if ax and (i + 1).exists():
                    turn_attr(i + 1)
                if soft and p.exists():
                    turn_max(p)
                if L.window and (i + 1).exists():
                    make_z(i + 1)
                if soft and i.exists():
                    turn_logits(i)
                if p.exists():
                    make_sums(p)
                if hist and p.exists():
                    add_counts(p)

            over_batches(pe, -1, step)


class Chain:

    def __init__(self, eng, sem):
        self.eng, self.sem, self.count = eng, sem, 0

    def __call__(self, instruction):
        instruction.then_inc(self.sem, 1)
        self.count += 1
        self.eng.wait_ge(self.sem, self.count)


def prepare(nc, L, S, A):
    ctx = ExitStack()
    with ctx:
        def sb(name, shape, dt=F32):
            return ctx.enter_context(nc.sbuf_tensor("prep_" + name, shape, dt))

        def sem(name):
            return ctx.enter_context(nc.semaphore("prep_" + name))

        rows = {k: sb(k + "_rows", [P, RB, P], I32) for k in ("src", "dst")}
        f = {k: sb(k + "_f", [P, RB, P]) for k in ("src", "dst", "rel", "hi", "lo")}
        hi_int = sb("hi_int", [P, RB, P], I32)
        rel_bf = sb("rel_bf", [P, RB, P], BF16)
        masks = S["masks"]
        next_first = sb("next_first", [P, RB], I32)
        last_before = sb("last_before", [P, RB], I32)
        ends = sb("ends", [P, RB])
        starts = sb("starts", [P, RB])
        one_int = sb("one_int", [1, 2], I32)
        last_a = sb("last_a", [D + HEADS, NT], I32)
        last_b = sb("last_b", [D + HEADS, NT], I32)
        iota_i = sb("iota_i", [P, P], I32)
        lane_i = sb("lane_i", [P, 1], I32)
        turned = [ctx.enter_context(nc.psum_tensor(f"prep_turned{n}", [P, SG * P], F32)) for n in range(2)]
        cleared = sem("cleared")
        chain_v = sem("chain_v")
        chain_g = sem("chain_g")
        edges_in = sem("edges_in")
        params_in = sem("params_in")
        ident_made = sem("ident_made")
        weights_cleared = sem("weights_cleared")
        rows_made = sem("rows_made")
        rows_out = sem("rows_out")
        back_in = sem("back_in")
        turned_made = sem("turned_made")
        turned_used = sem("turned_used")
        ones_made, masks_cleared = sem("ones_made"), sem("masks_cleared")
        rel_ready, rel_made = sem("rel_ready"), sem("rel_made")
        src_made, src_copied = sem("src_made"), sem("src_copied")
        x_in = [sem(f"x_in{c}") for c in range(NCH)]
        w1_in = sem("w1_in")
        scores_ps = ctx.enter_context(nc.psum_tensor("prep_scores", [P, 512], F32))
        w3T = sb("w3T", [D, D])
        w3_turned, w3_copied, scores_made = sem("w3_turned"), sem("w3_copied"), sem("scores_made")
        jobs_t = [j for c in range(NCH) for j in table_jobs(L, S, c)]
        projection = Projection(nc, ctx, "prep_p", S, jobs_t)
        made = Tables(nc, ctx, L, S, projection)
        block = ctx.enter_context(nc.Block())
        full_r, full_q = EFULL // P, EFULL % P
        jobs = [(k, r) for k in ("src", "rel", "hi", "lo") for r in range(0, RB, SG)]
        SRC_JOBS = len(range(0, RB, SG))
        cols = {"src": S["src_cols"], "rel": S["rel_cols"], "hi": S["hi_cols"], "lo": S["lo_cols"]}

        params = [
            (S["w2"][:, :], A["L0_gnn_W2"]),
            (S["b2"][:, :], A["L0_gnn_b2"].unsqueeze(0).to_broadcast([P, D])),
            (S["wlr"][:, 0:D], A["L1_gnn_W_l"]),
            (S["wlr"][:, D:2 * D], A["L1_gnn_W_r"]),
            (S["bias1"][:, 0:D], A["L1_gnn_b_l"].unsqueeze(0).to_broadcast([P, D])),
            (S["bias1"][:, D:2 * D], A["L1_gnn_b_r"].unsqueeze(0).to_broadcast([P, D])),
            (S["att_bc"][:, :], A["L1_gnn_att"].rearrange("h c -> (h c)").unsqueeze(0).to_broadcast([P, D])),
            (S["bias"][:, :], A["L1_gnn_bias"].unsqueeze(0).to_broadcast([P, D])),
            (S["gamma"][:, :], A["L1_gnn_gamma"].unsqueeze(0).to_broadcast([P, D])),
            (S["beta"][:, :], A["L1_gnn_beta"].unsqueeze(0).to_broadcast([P, D])),
            (S["w3"][:, 0:D], A["L2_gnn_W"]),
        ]
        attr_weights = ((32, 4, A["L0_gnn_W1"][2 * D:2 * D + 32, :]), (16, B, A["L1_gnn_W_e"]))
        PARAMS = len(params) + 1 + sum(tiles for _, tiles, _ in attr_weights)

        @block.sync
        def _(sp):
            sp.wait_ge(cleared, 1)
            for k in ("dst", "src"):
                e = A[k]
                sp.dma_start(rows[k][:, 0:full_r, :], e[0:full_r * P * P].rearrange("(r q e) -> q r e", q=P, e=P)
                             ).then_inc(edges_in, 16)
                sp.dma_start(rows[k][0:full_q, full_r, :],
                             e[full_r * P * P:EFULL * P].rearrange("(q e) -> q e", e=P)).then_inc(edges_in, 16)
                sp.dma_start(rows[k][full_q:full_q + 1, full_r, 0:EREST], e[EFULL * P:E].unsqueeze(0)
                             ).then_inc(edges_in, 16)
            X = S["X"]
            sp.wait_ge(weights_cleared, 1)
            for dst, src in ((S["w1"][:, 0:D], A["L0_gnn_W1"][0:D, :]),
                             (S["w1"][:, D:2 * D], A["L0_gnn_W1"][D:2 * D, :]),
                             (S["bias0"][:, D:2 * D], A["L0_gnn_b1"].unsqueeze(0).to_broadcast([P, D]))):
                sp.dma_start(dst, src).then_inc(w1_in, 16)
            for c in range(NCH - 1):
                k, m = CHUNKS[c]
                sp.dma_start(X[:, k:k + m, :], A["x"][k * P:(k + m) * P, :].rearrange("(k p) f -> p k f", p=P)
                             ).then_inc(x_in[c], 16)
            sp.dma_start(X[0:NREST, KN - 1, :], A["x"][(KN - 1) * P:N, :]).then_inc(x_in[NCH - 1], 16)
            for dst, src in params:
                sp.dma_start(dst, src).then_inc(params_in, 16)
            with nc.allow_non_contiguous_dma(reason="the two halves of a, once"):
                sp.dma_start(S["a2"][:, :], A["L2_gnn_a"].rearrange("(s f) -> f s", s=2)).then_inc(params_in, 16)
            for width, tiles, w in attr_weights:
                for j in range(tiles):
                    sp.dma_start(S["attr_w"][width][j * width:(j + 1) * width, j * D:(j + 1) * D], w
                                 ).then_inc(params_in, 16)
            sp.wait_ge(rel_made, 1)
            view = S["rel_rows"].rearrange("(r q e) -> q r e", q=P, e=P)
            sp.dma_start(view, rel_bf[:, :, :]).then_inc(rows_out, 16)
            with nc.allow_non_contiguous_dma(reason="one number per tile, once"):
                sp.dma_start(S["first_dram"][0:NTP].rearrange("(r q) -> q r", q=P), rows["dst"][:, :, 0]
                             ).then_inc(rows_out, 16)
                sp.dma_start(S["last_dram"][1:NTP + 1].rearrange("(r q) -> q r", q=P), rows["dst"][:, :, P - 1]
                             ).then_inc(rows_out, 16)
            sp.wait_ge(ones_made, 1)
            sp.dma_start(S["first_dram"][NTP:NTP + 1].unsqueeze(0), one_int[0:1, 0:1]).then_inc(rows_out, 16)
            sp.dma_start(S["last_dram"][0:1].unsqueeze(0), one_int[0:1, 1:2]).then_inc(rows_out, 16)
            sp.wait_ge(rows_out, 16 * 5)
            sp.dma_start(S["base_row"][0:1, :], S["first_dram"][0:NTP].unsqueeze(0)).then_inc(back_in, 16)
            with nc.allow_non_contiguous_dma(reason="one number per tile, once"):
                sp.dma_start(next_first[:, :], S["first_dram"][1:NTP + 1].rearrange("(r q) -> q r", q=P)
                             ).then_inc(back_in, 16)
                sp.dma_start(last_before[:, :], S["last_dram"][0:NTP].rearrange("(r q) -> q r", q=P)
                             ).then_inc(back_in, 16)
            for dst, o in ((last_a, 0), (last_b, 1)):
                sp.dma_start(dst[:, :], S["last_dram"][o:o + NT].unsqueeze(0).to_broadcast([D + HEADS, NT])
                             ).then_inc(back_in, 16)
            sp.wait_ge(params_in, 16 * PARAMS)
            sp.wait_ge(back_in, 80)

        @block.gpsimd
        def _(pool):
            pool.memset(rows["dst"][:, RB - 1, :], N)
            pool.memset(rows["src"][:, RB - 1, :], 0).then_inc(cleared, 1)
            pool.memset(S["X"][:, KN - 1:KP, :], 0.0)
            pool.memset(S["bias0"][:, 0:D], 0.0)
            pool.memset(S["attr_w"][32][:, :], 0.0)
            pool.memset(S["attr_w"][16][:, :], 0.0).then_inc(weights_cleared, 1)
            chain = Chain(pool, chain_g)
            chain(pool.memset(S["ident"][:, :], 0.0))
            chain(pool.affine_select(out=S["ident"][:, :], in_=S["ident"][:, :], compare_op=ALU.not_equal, fill=1.0,
                                     base=0, pattern=[[-1, P]], channel_multiplier=1))
            chain(pool.memset(S["tri"][:, :], 1.0))
            chain(pool.affine_select(out=S["tri"][:, :], in_=S["tri"][:, :], compare_op=ALU.is_gt, fill=0.0,
                                     base=0, pattern=[[1, HI]], channel_multiplier=-1))
            pool.memset(S["ones"][:, :], 1.0)
            pool.iota(iota_i[:, :], pattern=[[1, P]], base=0, channel_multiplier=0)
            pool.iota(lane_i[:, :], pattern=[[1, 1]], base=0, channel_multiplier=1).then_inc(ident_made, 1)
            pool.memset(S["zeros"][:, :], 0.0)
            pool.memset(one_int[0:1, 0:1], N)
            pool.memset(one_int[0:1, 1:2], -1).then_inc(ones_made, 1)
            pool.memset(masks[:, :, :, :], 0.0).then_inc(masks_cleared, 1)

        @block.vector
        def _(dve):
            v = nc.vector
            chain = Chain(dve, chain_v)
            dve.wait_ge(edges_in, 16 * 6)
            chain(v.tensor_copy(f["dst"][:, :, :], rows["dst"][:, :, :]))
            v.tensor_tensor(f["rel"][:, :, :], f["dst"][:, :, :], f["dst"][:, :, 0:1].to_broadcast([P, RB, P]),
                            ALU.subtract).then_inc(rel_ready, 1)
            chain(v.tensor_scalar(hi_int[:, :, :], f["dst"][:, :, :], 1.0 / P, 127.0 / 256.0, ALU.mult,
                                  ALU.subtract))
            chain(v.tensor_copy(f["hi"][:, :, :], hi_int[:, :, :]))
            v.scalar_tensor_tensor(out=f["lo"][:, :, :], in0=f["hi"][:, :, :], scalar=-float(P),
                                   in1=f["dst"][:, :, :], op0=ALU.mult, op1=ALU.add).then_inc(rows_made, 1)
            dve.wait_ge(ident_made, 1)
            v.tensor_copy(S["iota"][:, :], iota_i[:, :])
            v.tensor_copy(S["lane"][:, :], lane_i[:, :])
            dve.wait_ge(w1_in, 48)
            for c in range(FIRST_CHUNKS):
                made.on_vector(dve, c)
            for n, (k, r) in enumerate(jobs[:SRC_JOBS]):
                m = min(SG, RB - r)
                dve.wait_ge(turned_made, n + 1)
                v.tensor_copy(cols[k][:, r * P:(r + m) * P], turned[n % 2][:, 0:m * P]).then_inc(src_copied, 1)
            dve.wait_ge(masks_cleared, 1)
            for c in range(FIRST_CHUNKS, NCH):
                made.on_vector(dve, c)
            v.tensor_tensor(masks[:, :, 0, 1:P], f["rel"][:, :, 1:P], f["rel"][:, :, 0:P - 1], ALU.is_equal)
            chain(v.tensor_tensor(masks[:, :, 1, 0:P - 1], f["rel"][:, :, 1:P], f["rel"][:, :, 0:P - 1],
                                  ALU.is_equal))
            both = masks[:, :, :, :].rearrange("p r a e -> p (r a e)")
            v.tensor_scalar(both, both, 1.0, BIG, ALU.subtract, ALU.mult)
            dve.wait_ge(w3_turned, 1)
            v.tensor_copy(w3T[:, :], scores_ps[0:D, 0:D]).then_inc(w3_copied, 1)
            dve.wait_ge(scores_made, 1)
            v.tensor_copy(S["w3"][:, D:D + 2], scores_ps[0:D, P:P + 2])
            dve.wait_ge(back_in, 80)
            v.tensor_tensor(starts[:, :], last_before[:, :], rows["dst"][:, :, 0], ALU.not_equal)
            chain(v.tensor_tensor(ends[:, :], next_first[:, :], rows["dst"][:, :, 0], ALU.is_equal))
            chain(v.tensor_tensor(ends[:, :], ends[:, :], starts[:, :], ALU.max))
            v.scalar_tensor_tensor(out=S["carry_row"][:, :], in0=ends[:, :], scalar=float(1 << 20),
                                   in1=rows["dst"][:, :, 0], op0=ALU.mult, op1=ALU.add)
            v.tensor_tensor(S["through"][:, :], last_a[:, :], last_b[:, :], ALU.is_equal)

        @block.scalar
        def _(act):
            def tables(chunks):
                for c in chunks:
                    if c > 1:
                        made.store(act, c - 2)
                    projection.on_scalar(act, projection.numbers("table", c))
                    if c > chunks[0]:
                        made.on_scalar(act, c - 1)
                made.on_scalar(act, chunks[-1])

            act.wait_ge(edges_in, 16 * 6)
            act.activation(f["src"][:, :, :], rows["src"][:, :, :], ACT.Copy).then_inc(src_made, 1)
            act.wait_ge(rel_ready, 1)
            act.activation(rel_bf[:, :, :], f["rel"][:, :, :], ACT.Copy).then_inc(rel_made, 1)
            tables(range(FIRST_CHUNKS))
            for n, (k, r) in enumerate(jobs[SRC_JOBS:]):
                m = min(SG, RB - r)
                act.wait_ge(turned_made, SRC_JOBS + n + 1)
                act.activation(cols[k][:, r * P:(r + m) * P], turned[n % 2][:, 0:m * P], ACT.Copy
                               ).then_inc(turned_used, 1)
            tables(range(FIRST_CHUNKS, NCH))
            made.store(act, NCH - 2)
            made.store(act, NCH - 1)
            made.all_stored(act)

        @block.tensor
        def _(pe):
            def tables(chunks):
                for c in chunks:
                    pe.wait_ge(x_in[c], 16)
                    projection.on_tensor(pe, projection.numbers("table", c))

            pe.wait_ge(ident_made, 1)
            pe.wait_ge(w1_in, 48)
            tables(range(FIRST_CHUNKS))
            pe.wait_ge(rows_made, 1)
            pe.wait_ge(src_made, 1)
            for n, (k, r) in enumerate(jobs):
                m = min(SG, RB - r)
                wait(pe, src_copied, min(n - 1, SRC_JOBS))
                wait(pe, turned_used, n - 1 - SRC_JOBS)
                for j in range(m):
                    last = pe.transpose(turned[n % 2][:, j * P:(j + 1) * P], f[k][:, r + j, :], S["ident"][:, :])
                last.then_inc(turned_made, 1)
            tables(range(FIRST_CHUNKS, NCH))
            pe.wait_ge(params_in, 16 * PARAMS)
            pe.transpose(scores_ps[0:D, 0:D], S["w3"][:, 0:D], S["ident"][0:D, 0:D]).then_inc(w3_turned, 1)
            pe.wait_ge(w3_copied, 1)
            pe.matmul(scores_ps[0:D, P:P + 2], w3T[:, :], S["a2"][:, :], start=True, stop=True
                      ).then_inc(scores_made, 1)


class Rank:

    def __init__(self, nc, ctx, S):
        def sb(name, shape, dt=F32):
            return ctx.enter_context(nc.sbuf_tensor("rank_" + name, shape, dt))

        def sem(name):
            return ctx.enter_context(nc.semaphore("rank_" + name))

        self.nc, self.S = nc, S
        self.ones, self.upto, self.before = sb("ones", [HI, P]), sb("upto", [HI, P]), sb("before", [HI, 1])
        self.last, self.first, self.whole = sb("last", [P, HI]), sb("first", [P, HI]), sb("whole", [P, HI], I32)
        self.tile_l, self.tile_f, self.batch = sb("tile_l", [P, HI]), sb("tile_f", [P, HI]), sb("batch", [P, HI])
        self.ps = ctx.enter_context(nc.psum_tensor("rank_ps", [P, 512], F32))
        self.scanned, self.summed, self.added, self.turned = sem("scanned"), sem("summed"), sem("added"), sem("turned")

    def on_vector(self, dve, chain, ranked):
        v, S = self.nc.vector, self.S
        chain(v.memset(self.ones[:, :], 1.0))
        v.tensor_tensor_scan(self.upto[:, :], self.ones[:, :], S["counts"][:, :], 0.0, ALU.mult, ALU.add
                             ).then_inc(self.scanned, 1)
        dve.wait_ge(self.summed, 1)
        chain(v.tensor_copy(self.before[:, :], self.ps[0:HI, 0:1]))
        v.tensor_scalar(self.upto[:, :], self.upto[:, :], self.before[:, 0:1], None, ALU.add).then_inc(self.added, 1)
        dve.wait_ge(self.turned, 1)
        v.tensor_copy(S["degree"][:, :], self.ps[:, P:P + HI])
        chain(v.tensor_scalar(self.last[:, :], self.ps[:, 2 * P:2 * P + HI], 1.0, None, ALU.subtract))
        chain(v.tensor_tensor(self.first[:, :], self.last[:, :], S["degree"][:, :], ALU.subtract))
        chain(v.tensor_scalar(self.first[:, :], self.first[:, :], 1.0, None, ALU.add))
        for e, t in ((self.first, self.tile_f), (self.last, self.tile_l)):
            chain(v.tensor_scalar(self.whole[:, :], e[:, :], 1.0 / P, 127.0 / 256.0, ALU.mult, ALU.subtract))
            chain(v.tensor_copy(t[:, :], self.whole[:, :]))
        v.tensor_tensor(S["spans"][:, :], self.tile_l[:, :], self.tile_f[:, :], ALU.is_gt)
        chain(v.tensor_scalar(self.whole[:, :], self.tile_l[:, :], 1.0 / B, 3.0 / B, ALU.mult, ALU.subtract))
        chain(v.tensor_copy(self.batch[:, :], self.whole[:, :]))
        chain(v.scalar_tensor_tensor(out=self.last[:, :], in0=self.tile_l[:, :], scalar=-float(P), in1=self.last[:, :],
                                     op0=ALU.mult, op1=ALU.add))
        chain(v.scalar_tensor_tensor(out=self.last[:, :], in0=self.last[:, :], scalar=float(B), in1=self.tile_l[:, :],
                                     op0=ALU.mult, op1=ALU.add))
        v.scalar_tensor_tensor(out=S["last_row"][:, :], in0=self.batch[:, :], scalar=float(P * B - B),
                               in1=self.last[:, :], op0=ALU.mult, op1=ALU.add).then_inc(ranked, 1)

    def on_tensor(self, pe):
        ps, S, upto = self.ps, self.S, self.upto
        pe.wait_ge(self.scanned, 1)
        pe.matmul(ps[0:HI, 0:1], S["tri"][:, :], upto[:, P - 1:P], start=True, stop=True).then_inc(self.summed, 1)
        pe.wait_ge(self.added, 1)
        pe.transpose(ps[:, P:P + HI], S["counts"][:, :], S["ident"][0:HI, 0:HI])
        pe.transpose(ps[:, 2 * P:2 * P + HI], upto[:, :], S["ident"][0:HI, 0:HI]).then_inc(self.turned, 1)


class Projection:

    def __init__(self, nc, ctx, name, S, jobs):
        self.nc, self.S, self.jobs = nc, S, jobs
        self.turned = [ctx.enter_context(nc.psum_tensor(f"{name}_turned{n}", [D, SG * P], F32)) for n in range(2)]
        self.out = [ctx.enter_context(nc.psum_tensor(f"{name}_out{n}", [P, 512], F32)) for n in range(2)]
        self.lhsT = ctx.enter_context(nc.sbuf_tensor(name + "_lhsT", [D, 2, SG * P], F32))
        self.turned_made = ctx.enter_context(nc.semaphore(name + "_turned_made"))
        self.turned_copied = ctx.enter_context(nc.semaphore(name + "_turned_copied"))
        self.product_made = ctx.enter_context(nc.semaphore(name + "_product_made"))
        self.product_used = ctx.enter_context(nc.semaphore(name + "_product_used"))

    def on_tensor(self, pe, numbers):
        for n in numbers:
            _, k, m, source, _, _ = self.jobs[n]
            wait(pe, self.turned_copied, n - 1)
            for j in range(m):
                last = pe.transpose(self.turned[n % 2][:, j * P:(j + 1) * P], source[:, k + j, :],
                                    self.S["ident"][:, :])
            last.then_inc(self.turned_made, 1)
        for n in numbers:
            _, k, m, _, weights, cols = self.jobs[n]
            pe.wait_ge(self.turned_copied, n + 1)
            wait(pe, self.product_used, n - 1)
            for j in range(m):
                last = pe.matmul(self.out[n % 2][:, j * cols:(j + 1) * cols], self.lhsT[:, n % 2, j * P:(j + 1) * P],
                                 weights, start=True, stop=True)
            last.then_inc(self.product_made, 1)

    def on_scalar(self, act, numbers):
        for n in numbers:
            m = self.jobs[n][2]
            act.wait_ge(self.turned_made, n + 1)
            wait(act, self.product_made, n - 1)
            act.activation(self.lhsT[:, n % 2, 0:m * P], self.turned[n % 2][:, 0:m * P], ACT.Copy
                           ).then_inc(self.turned_copied, 1)

    def on_vector(self, dve, numbers, evacuate):
        for n in numbers:
            _, k, m, _, _, cols = self.jobs[n]
            dve.wait_ge(self.product_made, n + 1)
            evacuate(k, m, self.out[n % 2][:, 0:m * cols].rearrange("p (k w) -> p k w", k=m)
                     ).then_inc(self.product_used, 1)

    def numbers(self, kind, chunk):
        return [n for n, j in enumerate(self.jobs) if j[0] == (kind, chunk)]


CHUNK = 2 * SG
CHUNKS = [(k, min(CHUNK, KP - k)) for k in range(0, KP, CHUNK)]
NCH = len(CHUNKS)
GROUPS = [(0, 3), (3, 5), (5, 6), (6, NCH)]
assert CHUNKS[-1][0] == KN - 1


def table_jobs(L, S, c):
    k0, m0 = CHUNKS[c]
    return [(("table", c), k, min(SG, k0 + m0 - k), S["X"], L.weights, L.cols) for k in range(k0, k0 + m0, SG)]


class Tables:

    def __init__(self, nc, ctx, L, S, projection):
        self.nc, self.L, self.S, self.projection = nc, L, S, projection
        n = L.name
        self.table = ctx.enter_context(nc.sbuf_tensor(n + "_table", [P, 2, CHUNK, L.cols], F32))
        self.filled = ctx.enter_context(nc.semaphore(n + "_filled"))
        self.stored = [ctx.enter_context(nc.semaphore(f"{n}_table_out{q}")) for q in range(2)]
        self.stores = 2
        if L.parts == 3:
            self.parts = ctx.enter_context(nc.sbuf_tensor(n + "_parts", [P, 2, CHUNK, 3 * L.window], BF16))
            self.rounded = ctx.enter_context(nc.semaphore(n + "_rounded"))
            self.left = ctx.enter_context(nc.semaphore(n + "_left"))

    def on_vector(self, dve, c):
        v, L, q = self.nc.vector, self.L, c % 2
        k0, m0 = CHUNKS[c]

        def evacuate(k, m, product):
            out = self.table[:, q, k - k0:k - k0 + m, :]
            if L.bias is None:
                return v.tensor_copy(out, product)
            return v.tensor_tensor(out, product, bc(L.bias, 1, [P, m, L.cols]), ALU.add)

        wait(dve, self.stored[q], 16 * self.stores * (c // 2))
        self.projection.on_vector(dve, self.projection.numbers("table", c), evacuate)
        dve.wait_ge(self.projection.product_used, self.projection.numbers("table", c)[-1] + 1)
        dve.sem_inc(self.filled, 1)
        if L.parts == 3:
            g, w = L.gathered, L.window
            left = self.table[:, q, 0:m0, g:g + w]
            for part in range(2):
                out = left if part == 0 else self.parts[:, q, 0:m0, 2 * w:3 * w]
                dve.wait_ge(self.rounded, 2 * c + part + 1)
                v.tensor_tensor(out, left, self.parts[:, q, 0:m0, part * w:(part + 1) * w], ALU.subtract
                                ).then_inc(self.left, 1)

    def on_scalar(self, act, c):
        L, q = self.L, c % 2
        if L.parts != 3:
            return
        m0, g, w = CHUNKS[c][1], L.gathered, L.window
        act.wait_ge(self.filled, c + 1)
        wait(act, self.stored[q], 16 * self.stores * (c // 2))
        for part in range(2):
            if part:
                act.wait_ge(self.left, 2 * c + 1)
            act.activation(self.parts[:, q, 0:m0, part * w:(part + 1) * w], self.table[:, q, 0:m0, g:g + w],
                           ACT.Copy).then_inc(self.rounded, 1)

    def store(self, eng, c):
        L, q = self.L, c % 2
        k0, m0 = CHUNKS[c]
        g, w = L.gathered, L.window
        eng.wait_ge(self.filled, c + 1)
        eng.dma_start(node_view(L.gather_table)[:, k0:k0 + m0, :], self.table[:, q, 0:m0, 0:g]
                     ).then_inc(self.stored[q], 16)
        if L.parts == 3:
            eng.wait_ge(self.left, 2 * (c + 1))
            eng.dma_start(node_view(L.window_table)[:, k0:k0 + m0, :], self.parts[:, q, 0:m0, :]
                         ).then_inc(self.stored[q], 16)
        else:
            with self.nc.allow_non_contiguous_dma(reason="a column of the window table"):
                eng.dma_start(node_view(L.window_table)[:, k0:k0 + m0, :], self.table[:, q, 0:m0, g:g + w]
                             ).then_inc(self.stored[q], 16)

    def all_stored(self, sp):
        for q in range(2):
            sp.wait_ge(self.stored[q], 16 * self.stores * len(range(q, NCH, 2)))


def node_view(table):
    return table.rearrange("(k p) w -> p k w", p=P)


def spread(ap, w):
    return bc(ap, 2, [ap.shape[0], ap.shape[1], w])


def dense(nc, L, S, nxt, out):
    soft = L.heads > 0
    H, M, K = L.heads, L.msg, KN
    T, C = S["T_" + L.name], S["C_" + L.name]
    ctx = ExitStack()
    with ctx:
        def sb(name, shape, dt=F32):
            return ctx.enter_context(nc.sbuf_tensor(f"{L.name}_d_{name}", shape, dt))

        def sem(name):
            return ctx.enter_context(nc.semaphore(f"{L.name}_d_{name}"))

        node_sums = sb("node_sums", [P, K * L.row])
        sums = node_sums[:, :].rearrange("p (k w) -> p k w", k=K)
        into = sb("into", [P, K, L.row])
        tails = sb("tails", [P, LAST_C, B, L.row])
        tail_sums = sb("tail_sums", [M, NT])
        state = sb("state", [M, NTP])
        rows = sb("rows", [P, RB, L.row])
        X, nodes = S["X"], S["work"]
        stat = sb("stat", [P, 2, K])
        if soft:
            wide = sb("wide", [P, LAST_C, B, M])
            tail_max = sb("tail_max", [M, NT])
            top = sb("top", [M, NTP])
            gate = sb("gate", [M, NT])
            fade = sb("fade", [M, NT])
            node_top = sb("node_top", [P, K, H])
            carried_top = sb("carried_top", [P, K, H])
            unspanned = sb("unspanned", [P, K])
            weight = sb("weight", [P, 2, K, H])
            shifted, weighed = sem("shifted"), sem("weighed")
        ps = [ctx.enter_context(nc.psum_tensor(f"{L.name}_c_ps{n}", [P, SG * P], F32)) for n in range(2)]
        tails_in, wide_made, turned, copied = sem("tails_in"), sem("wide_made"), sem("turned"), sem("copied")
        chain_v, tops_shifted, faded, scanned = sem("chain_v"), sem("tops_shifted"), sem("faded"), sem("scanned")
        back, back_copied, ranked = sem("back"), sem("back_copied"), sem("ranked")
        carry_in = [sem(f"carry_in{c}") for c in range(NCH)]
        fetched = [S[f"{L.name}_fetched{c}"] for c in range(NCH)]
        scattered = S[L.name + "_scattered"]
        centred, squared, squares_summed, root_done = sem("centred"), sem("squared"), sem("squares_summed"), sem("root")
        x_ready = sem("x_ready")
        if L.name == "mlp":
            summed = sem("summed")
            ranks = Rank(nc, ctx, S)
        if L.name == "gatv2":
            shifted_x = sb("shifted_x", [P, K, D])
            mean = sb("mean", [P, D])
            scale = sb("scale", [P, D])
            bn_ps = [ctx.enter_context(nc.psum_tensor(f"gatv2_bn_ps{n}", [P, CHUNK * D], F32)) for n in range(2)]
            rows_ready, sum_made, bn_centred, bn_squared = (sem("rows_ready"), sem("sum_made"), sem("bn_centred"),
                                                            sem("bn_squared"))
            squares_made, var_made, scale_made = sem("squares_made"), sem("var_made"), sem("scale_made")
            gelu_in, gelu_out = sem("gelu_in"), sem("gelu_out")
        if L.name == "gat":
            neg = sb("neg", [P, K, D])
            elu_in, clipped, elu_out = sem("elu_in"), sem("clipped"), sem("elu_out")
        if nxt is not None and nxt.window:
            jobs = []
            for c in range(NCH + 1):
                if L.name == "mlp" and c < NCH:
                    k0, m0 = CHUNKS[c][0], min(CHUNKS[c][1], K - CHUNKS[c][0])
                    jobs += [(("w2", c), k, min(SG, k0 + m0 - k), nodes, S["w2"][:, :], D)
                             for k in range(k0, k0 + m0, SG)]
                if L.name != "mlp" and c < NCH:
                    jobs += table_jobs(nxt, S, c)
                if L.name == "mlp" and c > 0:
                    jobs += table_jobs(nxt, S, c - 1)
            projection = Projection(nc, ctx, L.name + "_d", S, jobs)
            made = Tables(nc, ctx, nxt, S, projection)
        else:
            made = projection = None
            x_stored = sem("x_stored")
        block = ctx.enter_context(nc.Block())

        counts = [min(P, NB - c * P) for c in range(LAST_C)]
        Tv = T.rearrange("(n p b) w -> n p (b w)", p=P, b=B)
        turns = []
        for c in range(LAST_C):
            for j0 in range(0, B, SG):
                turns.append((tail_sums, tails, c, j0, min(SG, B - j0)))
                if soft:
                    turns.append((tail_max, wide, c, j0, min(SG, B - j0)))
        backs = [(s, r, min(SG, RB - r)) for r in range(0, RB, SG) for s in (("state", "top") if soft else ("state",))]

        def span(c):
            k, m = CHUNKS[c]
            return slice(k, min(k + m, K))

        def group_span(g):
            return slice(span(GROUPS[g][0]).start, span(GROUPS[g][1] - 1).stop)

        @block.sync
        def _(sp):
            for c in range(LAST_C):
                sp.dma_start(tails[0:counts[c], c, :, :].rearrange("n b w -> n (b w)"),
                             Tv[c * P:c * P + counts[c], P - 1, :]).then_inc(tails_in, 16)
            sp.wait_ge(scattered, 16 * RB)
            for c in range(NCH):
                sp.dma_start(into[:, span(c), :], node_view(C)[:, span(c), :]).then_inc(carry_in[c], 16)
            for c in range(NCH):
                if made:
                    made.store(sp, c)
                elif nxt is not None:
                    k, m = CHUNKS[c]
                    sp.wait_ge(x_ready, c + 1)
                    sp.dma_start(node_view(nxt.gather_table)[:, k:k + m, :], X[:, k:k + m, :]).then_inc(x_stored, 16)
                else:
                    sp.wait_ge(x_ready, c + 1)
                    k, m = span(c).start, min(span(c).stop, K - 1) - span(c).start
                    if m > 0:
                        sp.dma_start(out[k * P:(k + m) * P, :].rearrange("(k p) f -> p k f", p=P),
                                     X[:, k:k + m, :]).then_inc(x_stored, 16)
                    if span(c).stop == K:
                        sp.dma_start(out[(K - 1) * P:N, :], X[0:NREST, K - 1, :]).then_inc(x_stored, 16)
            if made:
                made.all_stored(sp)
            else:
                sp.wait_ge(x_stored, 16 * NCH)

        @block.gpsimd
        def _(pool):
            if L.name == "mlp":
                pool.wait_ge(ranked, 1)

            def fetch(blocks):
                for k in blocks:
                    pool.indirect_dma_start(
                        out=node_sums[:, k * L.row:(k + 1) * L.row], out_offset=None, in_=T,
                        in_offset=bass.IndirectOffsetOnAxis(ap=S["last_row"][:, k:k + 1], axis=0)
                    ).then_inc(fetched[k // CHUNK], 16)

            early = EARLY_SOFT if soft else EARLY
            fetch(range(early))
            for r in range(RB):
                wait(pool, back_copied, sum(1 for s, r0, m in backs if r0 <= r))
                pool.indirect_dma_start(
                    out=C, out_offset=bass.IndirectOffsetOnAxis(ap=S["carry_row"][:, r:r + 1], axis=0),
                    in_=rows[:, r, :], in_offset=None, bounds_check=NP - 1, oob_is_err=False
                ).then_inc(scattered, 16)
            fetch(range(early, K))
            for c in range(NCH):
                pool.wait_ge(fetched[c], 16 * (span(c).stop - span(c).start))

        @block.tensor
        def _(pe):
            if L.name == "mlp":
                ranks.on_tensor(pe)
            pe.wait_ge(tails_in, 16 * LAST_C)
            if soft:
                pe.wait_ge(wide_made, 1)
            for n, (dst, src, c, j0, m) in enumerate(turns):
                wait(pe, copied, n - 1)
                k = counts[c]
                for j in range(m):
                    last = pe.transpose(ps[n % 2][0:M, j * P:j * P + k], src[0:k, c, j0 + j, 0:M],
                                        S["ident"][0:k, 0:k])
                last.then_inc(turned, 1)
            pe.wait_ge(scanned, 1)
            pe.wait_ge(copied, len(turns))
            for n, (s, r, m) in enumerate(backs):
                wait(pe, back_copied, n - 1)
                src = state if s == "state" else top
                for j in range(m):
                    last = pe.transpose(ps[n % 2][:, j * P:j * P + M], src[:, (r + j) * P:(r + j + 1) * P],
                                        S["ident"][0:M, 0:M])
                last.then_inc(back, 1)
            if L.name == "gatv2":
                for src, ps_all, ready, done in ((nodes[:, :, :], bn_ps[0], rows_ready, sum_made),
                                                 (sums[:, :, 0:D], bn_ps[1], bn_squared, squares_made)):
                    for c in range(NCH):
                        pe.wait_ge(ready, c + 1)
                        m = span(c).stop - span(c).start
                        p = P if c < NCH - 1 else NREST
                        last = pe.matmul(ps_all[:, 0:m * D].rearrange("p (k f) -> p k f", k=m), S["ones"][0:p, :],
                                         src[0:p, span(c), :], start=c == 0, stop=c == NCH - 1,
                                         skip_group_check=True)
                    last.then_inc(done, 1)
            if made:
                for c in range(NCH + 1):
                    if L.name == "mlp" and c < NCH:
                        pe.wait_ge(summed, c + 1)
                        projection.on_tensor(pe, projection.numbers("w2", c))
                    t = c - 1
                    if t >= 0:
                        pe.wait_ge(x_ready, t + 1)
                        projection.on_tensor(pe, projection.numbers("table", t))

        @block.scalar
        def _(act):
            for n, (dst, src, c, j0, m) in enumerate(turns):
                act.wait_ge(turned, n + 1)
                k = counts[c]
                t0 = c * P * B
                act.activation(
                    dst[:, t0:t0 + k * B].rearrange("f (n b) -> f b n", b=B)[:, j0:j0 + m, :],
                    ps[n % 2][0:M, 0:m * P].rearrange("f (b n) -> f b n", b=m)[:, :, 0:k], ACT.Copy
                ).then_inc(copied, 1)
            if soft:
                act.wait_ge(tops_shifted, 1)
                act.activation(tail_max[:, :], tail_max[:, :], ACT.Exp)
                act.activation(fade[:, 1:NT], fade[:, 1:NT], ACT.Exp).then_inc(faded, 1)
            for n, (s, r, m) in enumerate(backs):
                act.wait_ge(back, n + 1)
                part = slice(0, M) if s == "state" else slice(D, M)
                to = slice(0, M) if s == "state" else slice(M, L.row)
                act.activation(rows[:, r:r + m, to],
                               ps[n % 2][:, 0:m * P].rearrange("p (r f) -> p r f", r=m)[:, :, part], ACT.Copy
                               ).then_inc(back_copied, 1)

            def weights_of(g):
                act.wait_ge(shifted, g + 1)
                act.activation(weight[:, :, group_span(g), :], weight[:, :, group_span(g), :], ACT.Exp
                               ).then_inc(weighed, 1)

            if L.name == "gatv2":
                for g in range(len(GROUPS)):
                    weights_of(g)
                for c in range(NCH):
                    act.wait_ge(bn_centred, c + 1)
                    act.activation(sums[:, span(c), 0:D], nodes[:, span(c), :], ACT.Square).then_inc(bn_squared, 1)
                act.wait_ge(var_made, 1)
                act.activation(scale[:, :], scale[:, :], ACT.Sqrt).then_inc(scale_made, 1)
                for c in range(NCH):
                    act.wait_ge(gelu_in, c + 1)
                    act.activation(nodes[:, span(c), :], nodes[:, span(c), :], ACT.Gelu).then_inc(gelu_out, 1)
            for c in range(NCH + 2):
                if c < NCH and L.name == "gat":
                    for g, (first, _) in enumerate(GROUPS):
                        if c == first:
                            weights_of(g)
                    act.wait_ge(elu_in, c + 1)
                    act.activation(neg[:, span(c), :], nodes[:, span(c), :], ACT.Relu, scale=-1.0
                                   ).then_inc(clipped, 1)
                    act.wait_ge(clipped, c + 1)
                    act.activation(neg[:, span(c), :], neg[:, span(c), :], ACT.Exp, scale=-1.0).then_inc(elu_out, 1)
                if 0 <= c - 1 < NCH:
                    act.wait_ge(squares_summed, c)
                    act.activation(stat[:, 1, span(c - 1)], stat[:, 1, span(c - 1)], ACT.Sqrt).then_inc(root_done, 1)
                if c < NCH and L.name == "mlp":
                    projection.on_scalar(act, projection.numbers("w2", c))
                if made and c - 2 >= 0:
                    made.on_scalar(act, c - 2)
                if made and 0 <= c - 1 < NCH:
                    projection.on_scalar(act, projection.numbers("table", c - 1))
                if c < NCH:
                    act.wait_ge(centred, c + 1)
                    act.activation(X[:, span(c), :], nodes[:, span(c), :], ACT.Square).then_inc(squared, 1)

        @block.vector
        def _(dve):
            v = nc.vector
            chain = Chain(dve, chain_v)
            if L.name == "mlp":
                ranks.on_vector(dve, chain, ranked)

            def scan_soft():
                dve.wait_ge(tails_in, 16 * LAST_C)
                c64 = D // H
                for c in range(LAST_C):
                    k = counts[c]
                    top_h = tails[0:k, c, :, M:L.row]
                    v.tensor_copy(wide[0:k, c, :, 0:D].rearrange("n b (h c) -> n b h c", c=c64),
                                  bc(top_h, 3, [k, B, H, c64]))
                    last = v.tensor_copy(wide[0:k, c, :, D:M], top_h)
                last.then_inc(wide_made, 1)
                v.memset(top[:, 0:1], 0.0)
                v.memset(top[:, NT:NTP], 0.0)
                v.memset(state[:, 0:1], 0.0)
                v.memset(state[:, NT:NTP], 0.0)
                chain(v.tensor_scalar(gate[:, :], S["through"][0:M, :], 1.0, BIG, ALU.subtract, ALU.mult))
                dve.wait_ge(copied, len(turns))
                chain(v.tensor_tensor_scan(fade[:, :], gate[:, :], tail_max[:, :], 0.0, ALU.add, ALU.max))
                v.tensor_copy(top[:, 1:NT], fade[:, 0:NT - 1])
                chain(v.tensor_tensor(tail_max[:, :], tail_max[:, :], fade[:, :], ALU.subtract))
                chain(v.tensor_tensor(gate[:, 1:NT], fade[:, 0:NT - 1], fade[:, 1:NT], ALU.subtract))
                v.tensor_scalar(fade[:, 1:NT], gate[:, 1:NT], 0.0, None, ALU.min).then_inc(tops_shifted, 1)
                dve.wait_ge(faded, 1)
                chain(v.memset(gate[:, 0:1], 0.0))
                v.tensor_tensor(gate[:, 1:NT], fade[:, 1:NT], S["through"][0:M, 1:NT], ALU.mult)
                chain(v.tensor_tensor(tail_sums[:, :], tail_sums[:, :], tail_max[:, :], ALU.mult))
                v.tensor_tensor_scan(state[:, 1:NT], gate[:, 0:NT - 1], tail_sums[:, 0:NT - 1], 0.0,
                                     ALU.mult, ALU.add).then_inc(scanned, 1)

            def arrived(c):
                dve.wait_ge(fetched[c], 16 * (span(c).stop - span(c).start))
                dve.wait_ge(carry_in[c], 16)

            def softmax_sums(g):
                for c in range(*GROUPS[g]):
                    arrived(c)
                s = group_span(g)
                n, w = s.stop - s.start, D // H
                last_tile, carried, up = sums[:, s, :], into[:, s, :], node_top[:, s, :]
                chain(v.tensor_tensor(carried_top[:, s, :], carried[:, :, M:L.row], spread(S["spans"][:, s], H),
                                      ALU.mult))
                chain(v.tensor_tensor(carried_top[:, s, :], carried_top[:, s, :], spread(unspanned[:, s], H),
                                      ALU.add))
                chain(v.tensor_tensor(up, carried_top[:, s, :], last_tile[:, :, M:L.row], ALU.max))
                v.tensor_tensor(weight[:, 0, s, :], last_tile[:, :, M:L.row], up, ALU.subtract)
                v.tensor_tensor(weight[:, 1, s, :], carried_top[:, s, :], up, ALU.subtract).then_inc(shifted, 1)
                dve.wait_ge(weighed, g + 1)
                v.tensor_tensor(last_tile[:, :, D:M], last_tile[:, :, D:M], weight[:, 0, s, :], ALU.mult)
                chain(v.tensor_tensor(carried[:, :, D:M], carried[:, :, D:M], weight[:, 1, s, :], ALU.mult))
                chain(v.tensor_tensor(up, last_tile[:, :, D:M], carried[:, :, D:M], ALU.add))
                if L.name == "gatv2":
                    chain(v.tensor_scalar(up, up, 1e-16, None, ALU.add))
                chain(v.reciprocal(up, up))
                chain(v.tensor_tensor(weight[:, :, s, :], weight[:, :, s, :], bc(up, 1, [P, 2, n, H]), ALU.mult))
                for i, t in enumerate((last_tile, carried)):
                    last = v.tensor_tensor(t[:, :, 0:D].rearrange("p k (h c) -> p k h c", c=w),
                                           t[:, :, 0:D].rearrange("p k (h c) -> p k h c", c=w),
                                           bc(weight[:, i, s, :], 3, [P, n, H, w]), ALU.mult)
                chain(last)
                return v.tensor_tensor(nodes[:, s, :], last_tile[:, :, 0:D], carried[:, :, 0:D], ALU.add)

            def batch_norm():
                for g, (first, end) in enumerate(GROUPS):
                    s = group_span(g)
                    chain(softmax_sums(g))
                    n = s.stop - s.start
                    v.tensor_tensor(nodes[:, s, :], nodes[:, s, :], bc(S["bias"][:, :], 1, [P, n, D]), ALU.add
                                    ).then_inc(rows_ready, end - first)
                dve.wait_ge(sum_made, 1)
                chain(v.tensor_reduce(mean[:, :], bn_ps[0][:, :].rearrange("p (k f) -> p f k", f=D), AX, ALU.add))
                chain(v.tensor_scalar(mean[:, :], mean[:, :], 1.0 / N, None, ALU.mult))
                for c in range(NCH):
                    s = span(c)
                    v.tensor_tensor(nodes[:, s, :], nodes[:, s, :], bc(mean[:, :], 1, [P, s.stop - s.start, D]),
                                    ALU.subtract).then_inc(bn_centred, 1)
                dve.wait_ge(squares_made, 1)
                chain(v.tensor_reduce(scale[:, :], bn_ps[1][:, :].rearrange("p (k f) -> p f k", f=D), AX, ALU.add))
                v.tensor_scalar(scale[:, :], scale[:, :], 1.0 / N, BN_EPS, ALU.mult, ALU.add
                                ).then_inc(var_made, 1)
                dve.wait_ge(scale_made, 1)
                chain(v.reciprocal(scale[:, :], scale[:, :]))
                chain(v.tensor_tensor(scale[:, :], scale[:, :], S["gamma"][:, :], ALU.mult))
                for c in range(NCH):
                    s = span(c)
                    chain(v.tensor_tensor(nodes[:, s, :], nodes[:, s, :],
                                          bc(scale[:, :], 1, [P, s.stop - s.start, D]), ALU.mult))
                    v.tensor_tensor(nodes[:, s, :], nodes[:, s, :], shifted_x[:, s, :], ALU.add).then_inc(gelu_in, 1)

            def combine(c):
                s = span(c)
                if L.name == "gatv2":
                    dve.wait_ge(gelu_out, c + 1)
                    chain(v.tensor_tensor(nodes[:, s, :], nodes[:, s, :], X[:, s, :], ALU.add))
                    return
                if not soft:
                    arrived(c)
                if L.name == "mlp":
                    v.tensor_tensor(nodes[:, s, :], sums[:, s, :], into[:, s, :], ALU.add).then_inc(summed, 1)
                elif L.name == "gat":
                    for g, (first, end) in enumerate(GROUPS):
                        if c == first:
                            softmax_sums(g).then_inc(elu_in, end - first)
                            dve.wait_ge(elu_in, end)
                    chain(v.scalar_tensor_tensor(out=sums[:, s, 0:D], in0=nodes[:, s, :], scalar=0.0,
                                                 in1=X[:, s, :], op0=ALU.max, op1=ALU.add))
                    dve.wait_ge(elu_out, c + 1)
                    chain(v.scalar_tensor_tensor(out=nodes[:, s, :], in0=neg[:, s, :], scalar=-1.0,
                                                 in1=sums[:, s, 0:D], op0=ALU.add, op1=ALU.add))
                else:
                    chain(v.tensor_tensor(nodes[:, s, :], sums[:, s, :], into[:, s, :], ALU.add))
                    chain(v.tensor_tensor(nodes[:, s, :], nodes[:, s, :], spread(S["per_edge"][:, s], D), ALU.mult))
                    chain(v.tensor_tensor(nodes[:, s, :], nodes[:, s, :], X[:, s, :], ALU.add))

            def add_projected(c):
                def evacuate(k, m, product):
                    return v.tensor_tensor(nodes[:, k:k + m, :], product, X[:, k:k + m, :], ALU.add)
                numbers = projection.numbers("w2", c)
                projection.on_vector(dve, numbers, evacuate)
                dve.wait_ge(projection.product_used, numbers[-1] + 1)

            def centre(c):
                s = span(c)
                chain(v.tensor_reduce(stat[:, 0, s], nodes[:, s, :], AX, ALU.add))
                v.scalar_tensor_tensor(out=nodes[:, s, :], in0=spread(stat[:, 0, s], D), scalar=-1.0 / D,
                                       in1=nodes[:, s, :], op0=ALU.mult, op1=ALU.add).then_inc(centred, 1)

            def variance(c):
                s = span(c)
                dve.wait_ge(squared, c + 1)
                chain(v.tensor_reduce(stat[:, 1, s], X[:, s, :], AX, ALU.add))
                v.tensor_scalar(stat[:, 1, s], stat[:, 1, s], 1.0 / D, LN_EPS, ALU.mult, ALU.add
                                ).then_inc(squares_summed, 1)

            def normalise(c):
                s = span(c)
                dve.wait_ge(root_done, c + 1)
                chain(v.reciprocal(stat[:, 1, s], stat[:, 1, s]))
                v.tensor_tensor(X[:, s, :], nodes[:, s, :], spread(stat[:, 1, s], D), ALU.mult).then_inc(x_ready, 1)

            if soft:
                v.tensor_scalar(unspanned[:, :], S["spans"][:, 0:K], 1.0, BIG, ALU.subtract, ALU.mult)
                scan_soft()
            else:
                v.memset(state[:, 0:1], 0.0)
                chain(v.memset(state[:, NT:NTP], 0.0))
                dve.wait_ge(copied, len(turns))
                v.tensor_tensor_scan(state[:, 1:NT], S["through"][0:M, 0:NT - 1], tail_sums[:, 0:NT - 1], 0.0,
                                     ALU.mult, ALU.add).then_inc(scanned, 1)
            if L.name == "mlp":
                v.tensor_scalar(S["per_edge"][:, :], S["degree"][:, 0:K], 1.0, None, ALU.max)
                chain(v.tensor_tensor(nodes[:, :, :], spread(S["degree"][:, 0:K], D), bc(S["b2"][:, :], 1, [P, K, D]),
                                      ALU.mult))
                v.reciprocal(S["per_edge"][:, :], S["per_edge"][:, :])
                chain(v.tensor_tensor(X[:, 0:K, :], X[:, 0:K, :], nodes[:, :, :], ALU.add))
            if L.name == "gatv2":
                chain(v.tensor_tensor(shifted_x[:, :, :], X[:, 0:K, :], bc(S["beta"][:, :], 1, [P, K, D]), ALU.add))
                batch_norm()
            for c in range(NCH + 2):
                if c < NCH:
                    combine(c)
                if 0 <= c - 1 < NCH:
                    variance(c - 1)
                    normalise(c - 1)
                if made and c - 2 >= 0:
                    made.on_vector(dve, c - 2)
                if c < NCH and L.name == "mlp":
                    add_projected(c)
                if c < NCH:
                    centre(c)

def clear_semaphores(nc, numbers):
    with nc.Block() as block:
        @block.gpsimd
        def _(pool):
            pool.sem_clear(numbers)


def build(nc, A, out, last=4):
    def dram(name, shape, dt=F32):
        return nc.dram_tensor(name, shape, dt, kind="Internal").ap()

    layers = [
        Layer("mlp", D, D, 32, 0, dram("mlp_src", [NP, D]), dram("mlp_dst", [NP, 3 * D], BF16)),
        Layer("gatv2", D, D, 16, HEADS, dram("gatv2_src", [NP, D]), dram("gatv2_dst", [NP, 3 * D], BF16)),
        Layer("gat", D + 1, 1, 0, 1, dram("gat_src", [NP, D + 1]), dram("gat_dst", [NP, 1])),
        Layer("mean", D, 0, 0, 0, dram("mean_src", [NP, D]), None),
    ]
    ctx = ExitStack()
    with ctx:
        def sb(name, shape, dt=F32):
            return ctx.enter_context(nc.sbuf_tensor(name, shape, dt))

        row = D + 2 * HEADS
        S = {
            "X": sb("X", [P, KP, D]), "work": sb("work", [P, KN, D]),
            "src_cols": sb("src_cols", [P, NTP], I32), "rel_cols": sb("rel_cols", [P, NTP]),
            "hi_cols": sb("hi_cols", [P, NTP], BF16), "lo_cols": sb("lo_cols", [P, NTP], BF16),
            "base_row": sb("base_row", [1, NTP], I32),
            "lane": sb("lane", [P, 1]), "iota": sb("iota", [P, P], BF16), "ident": sb("ident", [P, P]),
            "tri": sb("tri", [HI, HI]), "ones": sb("ones", [P, P]), "counts": sb("counts", [HI, P]),
            "through": sb("through", [D + HEADS, NT]), "carry_row": sb("carry_row", [P, RB], I32),
            "degree": sb("degree", [P, HI]), "spans": sb("spans", [P, HI]), "last_row": sb("last_row", [P, HI], I32),
            "per_edge": sb("per_edge", [P, KN]),
            "masks": sb("masks", [P, RB, 2, P]), "zeros": sb("zeros", [P, 1, D + 2 * HEADS]),
            "w1": sb("w1", [D, 2 * D]), "w2": sb("w2", [D, D]), "b2": sb("b2", [P, D]), "bias0": sb("bias0", [P, 2 * D]),
            "wlr": sb("wlr", [D, 2 * D]), "bias1": sb("bias1", [P, 2 * D]), "att_bc": sb("att_bc", [P, D]),
            "bias": sb("bias", [P, D]), "gamma": sb("gamma", [P, D]), "beta": sb("beta", [P, D]),
            "w3": sb("w3", [D, D + 2]), "a2": sb("a2", [D, 2]),
            "attr_w": {32: sb("attr_w32", [P, 4 * D]), 16: sb("attr_w16", [16 * B, B * D])},
            "attr": {32: A["edge_attr_32"], 16: A["edge_attr_16"]},
            "rel_rows": dram("rel_rows", [NTP * P], BF16), "edge_rows": dram("edge_rows", [NTP, HEADS, 2 * P]),
            "first_dram": dram("first_dram", [NTP + 1], I32), "last_dram": dram("last_dram", [NTP + 1], I32),
        }
        for L in layers:
            S["T_" + L.name] = dram("sums_" + L.name, [NT * P, L.row])
            S["C_" + L.name] = dram("carry_" + L.name, [NP, L.row])
        for L in layers:
            for name in [f"gathered{q}" for q in range(Q)] + ["scattered"] + [
                    f"fetched{c}" for c in range(NCH)]:
                S[f"{L.name}_{name}"] = ctx.enter_context(nc.semaphore(f"{L.name}_{name}"))
        for L, weights, cols, bias in zip(layers, ("w1", "wlr", "w3"), (2 * D, 2 * D, D + 2), ("bias0", "bias1", None)):
            L.weights, L.cols, L.bias = S[weights][:, :], cols, S[bias][:, :] if bias else None
        numbers = range(min(nc.free_semaphores), max(nc.free_semaphores) + 1)
        prepare(nc, layers[0], S, A)
        for n, L in enumerate(layers[:last]):
            if n:
                clear_semaphores(nc, numbers)
            edge_pass(nc, L, S, hist=(n == 0))
            dense(nc, L, S, layers[n + 1] if n + 1 < last else None, out)


INPUTS = ["x", "src", "dst", "edge_attr_16", "edge_attr_32", "L0_gnn_W1", "L0_gnn_b1", "L0_gnn_W2", "L0_gnn_b2",
          "L1_gnn_W_l", "L1_gnn_b_l", "L1_gnn_W_r", "L1_gnn_b_r", "L1_gnn_W_e", "L1_gnn_att", "L1_gnn_bias",
          "L1_gnn_gamma", "L1_gnn_beta", "L2_gnn_W", "L2_gnn_a"]


def kernel(**inputs):
    import concourse.bacc as bacc
    from concourse.bass_utils import run_bass_kernel_spmd

    nc = bacc.Bacc("TRN2", target_bir_lowering=False, num_devices=1)
    arrays, A = {}, {}
    for name in INPUTS:
        a = np.ascontiguousarray(inputs[name])
        arrays["in_" + name] = a
        A[name] = nc.dram_tensor("in_" + name, a.shape, mybir.dt.from_np(a.dtype), kind="ExternalInput").ap()
    out = nc.dram_tensor("out_nodes", (N, D), F32, kind="ExternalOutput").ap()
    build(nc, A, out)
    r = run_bass_kernel_spmd(nc, [arrays], core_ids=[0])
    return r.results[0]["out_nodes"]
```
